# Optimizing a Trainium2 kernel written in Bass

```python
import numpy as np
import jax
import jax.numpy as jnp

def _softmax(x, axis=-1):
    return jax.nn.softmax(x, axis=axis)

def _gelu(x):
    return jax.nn.gelu(x, approximate=True)

def _silu(x):
    return jax.nn.silu(x)

def _sigmoid(x):
    return jax.nn.sigmoid(x)

def _layernorm(x, axis=-1, eps=1e-05):
    m = jnp.mean(x, axis=axis, keepdims=True)
    v = jnp.var(x, axis=axis, keepdims=True)
    return (x - m) / jnp.sqrt(v + eps)

def _scatter_add(tgt, idx, src, axis=0):
    return tgt.at[idx].add(src)

def _segment_sum(src, seg, n):
    return jax.ops.segment_sum(src, seg, n)
kernel_name = 'mk_audio_tower_d2_tok_audfeat1024_r4_c1dc9d'

def setup_inputs(seed: int=0):
    np.random.seed(seed)
    _w = jnp.asarray

    def _rec_inputs():
        import jax
        import jax.numpy as jnp
        _rk = jax.random.key(seed)
        x = -0.000125008 + 0.999885 * jax.random.normal(jax.random.fold_in(_rk, 1), (8, 512, 375), jnp.float32)
        return x
    x = _rec_inputs()

    def _L0_tok_setup():
        import jax, jax.numpy as jnp
        import numpy as np
        B, L, N, K, D = (32, 512, 128, 64, 256)

        def dct_fft(x):
            n = x.shape[-1]
            v = jnp.concatenate([x[..., ::2], x[..., 1::2][..., ::-1]], axis=-1)
            return jnp.fft.fft(v).real[..., :n]
        key = jax.random.key(seed)
        k1, k2, k3, k4 = jax.random.split(key, 4)
        x = jax.random.normal(k1, (B, L, N), jnp.float32)
        W = jax.random.normal(k2, (K, D), jnp.float32) * (1.0 / np.sqrt(K))
        b = jax.random.normal(k3, (D,), jnp.float32) * 0.01
        alpha = jax.random.normal(k4, (1,), jnp.float32) * 0.1
        return {'x': x, 'W': W, 'b': b, 'alpha': alpha}
    _L0_tok_all = _L0_tok_setup()
    _L0_tok_in = {k: v for k, v in _L0_tok_all.items() if k in ('W', 'b', 'alpha')}
    del _L0_tok_all

    def _L0_attn_setup():
        import jax, jax.numpy as jnp
        import numpy as np
        B, T, D = (1, 1024, 256)
        H, KD, VD = (16, 64, 64)
        MIN_THETA, MAX_THETA = (1.0, 10000.0)

        def _sin_cos(t, d, dtype):
            half = d // 2
            p = jnp.arange(half, dtype=dtype) / (half - 1)
            thetas = MIN_THETA * (MAX_THETA / MIN_THETA) ** p
            pos = jnp.arange(t, dtype=dtype)[:, None] / thetas[None, :]
            return (jnp.sin(pos), jnp.cos(pos))

        def _rope(x, sin, cos):
            d = x.shape[-1] // 2
            x_hi, x_lo = (x[..., :d], x[..., d:])
            y_lo = x_lo * cos + x_hi * sin
            y_hi = x_hi * cos - x_lo * sin
            return jnp.concatenate([y_lo, y_hi], axis=-1)
        key = jax.random.key(seed)
        k0, k1, k2 = jax.random.split(key, 3)
        x = jax.random.normal(k0, (B, T, D), dtype=jnp.float32)
        W_in = jax.random.normal(k1, ((2 * KD + VD) * H, D), dtype=jnp.float32) * 0.02
        b_in = jnp.zeros(((2 * KD + VD) * H,), dtype=jnp.float32)
        W_out = jax.random.normal(k2, (D, H * VD), dtype=jnp.float32) * 0.02
        b_out = jnp.zeros((D,), dtype=jnp.float32)
        return {'x': x, 'W_in': W_in, 'b_in': b_in, 'W_out': W_out, 'b_out': b_out}
    _L0_attn_all = _L0_attn_setup()
    _L0_attn_in = {k: v for k, v in _L0_attn_all.items() if k in ('W_in', 'b_in', 'W_out', 'b_out')}
    del _L0_attn_all

    def _L0_ffn_setup():
        import jax, jax.numpy as jnp
        import numpy as np
        DIM = 256
        INTER = 128
        E = 16
        TOPK = 4
        N_GROUPS = 4
        TOPK_GROUPS = 2
        ROUTE_SCALE = 1.0
        INIT_STD = 0.02
        B, S = (2, 256)
        key = jax.random.key(seed)
        ks = jax.random.split(key, 8)
        return {'x': jax.random.normal(ks[0], (B, S, DIM), jnp.float32), 'gate_w': jax.random.normal(ks[1], (E, DIM), jnp.float32) * INIT_STD, 'gate_bias': jnp.zeros((E,), jnp.float32), 'w1': jax.random.normal(ks[2], (E, INTER, DIM), jnp.float32) * INIT_STD, 'w2': jax.random.normal(ks[3], (E, DIM, INTER), jnp.float32) * INIT_STD, 'w3': jax.random.normal(ks[4], (E, INTER, DIM), jnp.float32) * INIT_STD, 'ws1': jax.random.normal(ks[5], (INTER, DIM), jnp.float32) * INIT_STD, 'ws2': jax.random.normal(ks[6], (DIM, INTER), jnp.float32) * INIT_STD, 'ws3': jax.random.normal(ks[7], (INTER, DIM), jnp.float32) * INIT_STD}
    _L0_ffn_all = _L0_ffn_setup()
    _L0_ffn_in = {k: v for k, v in _L0_ffn_all.items() if k in ('gate_w', 'gate_bias', 'w1', 'w2', 'w3', 'ws1', 'ws2', 'ws3')}
    del _L0_ffn_all

    def _L1_attn_setup():
        import jax, jax.numpy as jnp
        import numpy as np
        B, S, HID, NH = (4, 1024, 256, 16)
        D = HID // NH
        EPS = 1e-05

        def _delta_scan(q, k, v, beta):
            vsum = v.sum(-1)
            qs = jnp.moveaxis(q, 1, 0)
            ks_ = jnp.moveaxis(k, 1, 0)
            vs = jnp.moveaxis(vsum, 1, 0)
            bs = jnp.moveaxis(beta, 1, 0)

            def step(h, inp):
                q_t, k_t, vsum_t, beta_t = inp
                h = h * beta_t[..., None, None]
                h = h + (k_t * vsum_t[..., None])[:, :, None, :]
                o_t = jnp.einsum('bhj,bhjk->bhk', q_t, h)
                return (h, o_t)
            h0 = jnp.zeros((q.shape[0], q.shape[2], D, D), dtype=q.dtype)
            _, o = jax.lax.scan(step, h0, (qs, ks_, vs, bs))
            return jnp.moveaxis(o, 0, 1)
        key = jax.random.key(seed)
        ks = jax.random.split(key, 8)
        x = jax.random.normal(ks[0], (B, S, HID), dtype=jnp.float32)
        sc = 0.03
        Wq = jax.random.normal(ks[1], (HID, HID), dtype=jnp.float32) * sc
        Wk = jax.random.normal(ks[2], (HID, HID), dtype=jnp.float32) * sc
        Wv = jax.random.normal(ks[3], (HID, HID), dtype=jnp.float32) * sc
        Wbeta = jax.random.normal(ks[4], (HID, NH), dtype=jnp.float32) * sc
        b_beta = jnp.full((NH,), 0.9, dtype=jnp.float32)
        Wo = jax.random.normal(ks[5], (HID, HID), dtype=jnp.float32) * sc
        b_o = jnp.zeros((HID,), dtype=jnp.float32)
        ln_g = jnp.ones((HID,), dtype=jnp.float32)
        ln_b = jnp.zeros((HID,), dtype=jnp.float32)
        return {'x': x, 'Wq': Wq, 'Wk': Wk, 'Wv': Wv, 'Wbeta': Wbeta, 'b_beta': b_beta, 'Wo': Wo, 'b_o': b_o, 'ln_g': ln_g, 'ln_b': ln_b}
    _L1_attn_all = _L1_attn_setup()
    _L1_attn_in = {k: v for k, v in _L1_attn_all.items() if k in ('Wq', 'Wk', 'Wv', 'Wbeta', 'b_beta', 'Wo', 'b_o', 'ln_g', 'ln_b')}
    del _L1_attn_all

    def _L1_ffn_setup():
        import jax, jax.numpy as jnp
        import numpy as np
        B, S, D, F, E, NS, K = (2, 256, 256, 1024, 8, 8, 2)
        FS = F // NS
        key = jax.random.key(seed)
        ks = jax.random.split(key, 8)
        scale = 0.02
        return {'hidden_states': jax.random.normal(ks[0], (B, S, D), jnp.float32), 'gate_W': jax.random.normal(ks[1], (E, D), jnp.float32) * scale, 'w1_e': jax.random.normal(ks[2], (E, D, F), jnp.float32) * scale, 'w3_e': jax.random.normal(ks[3], (E, D, F), jnp.float32) * scale, 'w2_e': jax.random.normal(ks[4], (E, F, D), jnp.float32) * scale, 'w1_s': jax.random.normal(ks[5], (NS, D, FS), jnp.float32) * scale, 'w3_s': jax.random.normal(ks[6], (NS, D, FS), jnp.float32) * scale, 'w2_s': jax.random.normal(ks[7], (NS, FS, D), jnp.float32) * scale}
    _L1_ffn_all = _L1_ffn_setup()
    _L1_ffn_in = {k: v for k, v in _L1_ffn_all.items() if k in ('gate_W', 'w1_e', 'w3_e', 'w2_e', 'w1_s', 'w3_s', 'w2_s')}
    del _L1_ffn_all
    return {'x': x, 'L0_tok_W': _L0_tok_in['W'], 'L0_tok_b': _L0_tok_in['b'], 'L0_tok_alpha': _L0_tok_in['alpha'], 'L0_attn_W_in': _L0_attn_in['W_in'], 'L0_attn_b_in': _L0_attn_in['b_in'], 'L0_attn_W_out': _L0_attn_in['W_out'], 'L0_attn_b_out': _L0_attn_in['b_out'], 'L0_ffn_gate_w': _L0_ffn_in['gate_w'], 'L0_ffn_gate_bias': _L0_ffn_in['gate_bias'], 'L0_ffn_w1': _L0_ffn_in['w1'], 'L0_ffn_w2': _L0_ffn_in['w2'], 'L0_ffn_w3': _L0_ffn_in['w3'], 'L0_ffn_ws1': _L0_ffn_in['ws1'], 'L0_ffn_ws2': _L0_ffn_in['ws2'], 'L0_ffn_ws3': _L0_ffn_in['ws3'], 'L1_attn_Wq': _L1_attn_in['Wq'], 'L1_attn_Wk': _L1_attn_in['Wk'], 'L1_attn_Wv': _L1_attn_in['Wv'], 'L1_attn_Wbeta': _L1_attn_in['Wbeta'], 'L1_attn_b_beta': _L1_attn_in['b_beta'], 'L1_attn_Wo': _L1_attn_in['Wo'], 'L1_attn_b_o': _L1_attn_in['b_o'], 'L1_attn_ln_g': _L1_attn_in['ln_g'], 'L1_attn_ln_b': _L1_attn_in['ln_b'], 'L1_ffn_gate_W': _L1_ffn_in['gate_W'], 'L1_ffn_w1_e': _L1_ffn_in['w1_e'], 'L1_ffn_w3_e': _L1_ffn_in['w3_e'], 'L1_ffn_w2_e': _L1_ffn_in['w2_e'], 'L1_ffn_w1_s': _L1_ffn_in['w1_s'], 'L1_ffn_w3_s': _L1_ffn_in['w3_s'], 'L1_ffn_w2_s': _L1_ffn_in['w2_s']}

def reference(x, L0_tok_W, L0_tok_b, L0_tok_alpha, L0_attn_W_in, L0_attn_b_in, L0_attn_W_out, L0_attn_b_out, L0_ffn_gate_w, L0_ffn_gate_bias, L0_ffn_w1, L0_ffn_w2, L0_ffn_w3, L0_ffn_ws1, L0_ffn_ws2, L0_ffn_ws3, L1_attn_Wq, L1_attn_Wk, L1_attn_Wv, L1_attn_Wbeta, L1_attn_b_beta, L1_attn_Wo, L1_attn_b_o, L1_attn_ln_g, L1_attn_ln_b, L1_ffn_gate_W, L1_ffn_w1_e, L1_ffn_w3_e, L1_ffn_w2_e, L1_ffn_w1_s, L1_ffn_w3_s, L1_ffn_w2_s):
    import jax
    import jax.numpy as jnp

    def _L0_tok_ref(x, W, b, alpha):
        import jax, jax.numpy as jnp
        import numpy as np
        B, L, N, K, D = (32, 512, 128, 64, 256)

        def dct_fft(x):
            n = x.shape[-1]
            v = jnp.concatenate([x[..., ::2], x[..., 1::2][..., ::-1]], axis=-1)
            return jnp.fft.fft(v).real[..., :n]
        Bs, Ls, Ns = x.shape
        k = W.shape[0]
        xt = jnp.transpose(x, (0, 2, 1)).reshape(-1, Ls)
        freq_k = dct_fft(xt)[:, :k].reshape(Bs, Ns, k)
        out = jnp.einsum('bnk,kd->bnd', freq_k, W) + b
        return alpha * out

    def _L0_attn_ref(x, W_in, b_in, W_out, b_out):
        import jax, jax.numpy as jnp
        import numpy as np
        B, T, D = (1, 1024, 256)
        H, KD, VD = (16, 64, 64)
        MIN_THETA, MAX_THETA = (1.0, 10000.0)

        def _sin_cos(t, d, dtype):
            half = d // 2
            p = jnp.arange(half, dtype=dtype) / (half - 1)
            thetas = MIN_THETA * (MAX_THETA / MIN_THETA) ** p
            pos = jnp.arange(t, dtype=dtype)[:, None] / thetas[None, :]
            return (jnp.sin(pos), jnp.cos(pos))

        def _rope(x, sin, cos):
            d = x.shape[-1] // 2
            x_hi, x_lo = (x[..., :d], x[..., d:])
            y_lo = x_lo * cos + x_hi * sin
            y_hi = x_hi * cos - x_lo * sin
            return jnp.concatenate([y_lo, y_hi], axis=-1)
        b, t, _ = x.shape
        proj = x @ W_in.T + b_in
        i1, i2 = (KD * H, 2 * KD * H)
        q = proj[..., :i1].reshape(b, t, H, KD).transpose(0, 2, 1, 3)
        k = proj[..., i1:i2].reshape(b, t, H, KD).transpose(0, 2, 1, 3)
        v = proj[..., i2:].reshape(b, t, H, VD).transpose(0, 2, 1, 3)
        sin, cos = _sin_cos(t, KD, x.dtype)
        q = _rope(q, sin, cos)
        k = _rope(k, sin, cos)
        scale = 1.0 / np.sqrt(KD)
        att = jnp.einsum('bhqd,bhkd->bhqk', q, k) * jnp.asarray(scale, x.dtype)
        mask = jnp.tril(jnp.ones((t, t), dtype=bool))
        att = jnp.where(mask[None, None], att, jnp.asarray(-jnp.inf, x.dtype))
        att = jax.nn.softmax(att, axis=-1)
        y = jnp.einsum('bhqk,bhkd->bhqd', att, v)
        y = y.transpose(0, 2, 1, 3).reshape(b, t, H * VD)
        return y @ W_out.T + b_out

    def _L0_ffn_ref(x, gate_w, gate_bias, w1, w2, w3, ws1, ws2, ws3):
        import jax, jax.numpy as jnp
        import numpy as np
        DIM = 256
        INTER = 128
        E = 16
        TOPK = 4
        N_GROUPS = 4
        TOPK_GROUPS = 2
        ROUTE_SCALE = 1.0
        INIT_STD = 0.02
        B, S = (2, 256)
        Bx, Sx, D = x.shape
        T = Bx * Sx
        xf = x.reshape(T, D)
        scores = jax.nn.sigmoid(xf @ gate_w.T)
        original_scores = scores
        s = scores + gate_bias
        sg = s.reshape(T, N_GROUPS, E // N_GROUPS)
        group_scores = sg.max(axis=-1)
        _, gidx = jax.lax.top_k(group_scores, TOPK_GROUPS)
        keep = jnp.zeros((T, N_GROUPS), bool).at[jnp.arange(T)[:, None], gidx].set(True)
        s_masked = jnp.where(keep[:, :, None], sg, -jnp.inf).reshape(T, E)
        _, idx = jax.lax.top_k(s_masked, TOPK)
        weights = jnp.take_along_axis(original_scores, idx, axis=1) * ROUTE_SCALE
        comb = jnp.zeros((T, E), x.dtype).at[jnp.arange(T)[:, None], idx].add(weights)
        h1 = jnp.einsum('td,eid->tei', xf, w1)
        h3 = jnp.einsum('td,eid->tei', xf, w3)
        h = jax.nn.silu(h1) * h3
        y = jnp.einsum('tei,edi,te->td', h, w2, comb)
        z = jax.nn.silu(xf @ ws1.T) * (xf @ ws3.T) @ ws2.T
        return (y + z).reshape(Bx, Sx, D)

    def _L1_attn_ref(x, Wq, Wk, Wv, Wbeta, b_beta, Wo, b_o, ln_g, ln_b):
        import jax, jax.numpy as jnp
        import numpy as np
        B, S, HID, NH = (4, 1024, 256, 16)
        D = HID // NH
        EPS = 1e-05

        def _delta_scan(q, k, v, beta):
            vsum = v.sum(-1)
            qs = jnp.moveaxis(q, 1, 0)
            ks_ = jnp.moveaxis(k, 1, 0)
            vs = jnp.moveaxis(vsum, 1, 0)
            bs = jnp.moveaxis(beta, 1, 0)

            def step(h, inp):
                q_t, k_t, vsum_t, beta_t = inp
                h = h * beta_t[..., None, None]
                h = h + (k_t * vsum_t[..., None])[:, :, None, :]
                o_t = jnp.einsum('bhj,bhjk->bhk', q_t, h)
                return (h, o_t)
            h0 = jnp.zeros((q.shape[0], q.shape[2], D, D), dtype=q.dtype)
            _, o = jax.lax.scan(step, h0, (qs, ks_, vs, bs))
            return jnp.moveaxis(o, 0, 1)
        b, s, hid = x.shape
        residual = x
        q = (x @ Wq).reshape(b, s, NH, D)
        k = (x @ Wk).reshape(b, s, NH, D)
        v = (x @ Wv).reshape(b, s, NH, D)
        beta = jax.nn.sigmoid(x @ Wbeta + b_beta)
        o = _delta_scan(q, k, v, beta).reshape(b, s, hid)
        out = o @ Wo + b_o
        y = residual + out
        mu = y.mean(-1, keepdims=True)
        var = ((y - mu) ** 2).mean(-1, keepdims=True)
        return ln_g * (y - mu) * jax.lax.rsqrt(var + EPS) + ln_b

    def _L1_ffn_ref(hidden_states, gate_W, w1_e, w3_e, w2_e, w1_s, w3_s, w2_s):
        import jax, jax.numpy as jnp
        import numpy as np
        B, S, D, F, E, NS, K = (2, 256, 256, 1024, 8, 8, 2)
        FS = F // NS
        b, s, d = hidden_states.shape
        e = gate_W.shape[0]
        flat = hidden_states.reshape(-1, d)
        T = flat.shape[0]
        logits = (flat @ gate_W.T).astype(jnp.float32)
        probs = jax.nn.softmax(logits, axis=-1)
        top_v, top_i = jax.lax.top_k(probs, K)
        gates = jnp.zeros((T, e), probs.dtype).at[jnp.arange(T)[:, None], top_i].set(top_v)
        g = jax.nn.silu(jnp.einsum('td,edf->etf', flat, w1_e))
        u = jnp.einsum('td,edf->etf', flat, w3_e)
        out_e = jnp.einsum('etf,efd->etd', g * u, w2_e)
        routed = jnp.einsum('te,etd->td', gates, out_e).reshape(b, s, d)
        gs = jax.nn.silu(jnp.einsum('bsd,ndf->nbsf', hidden_states, w1_s))
        us = jnp.einsum('bsd,ndf->nbsf', hidden_states, w3_s)
        shared = jnp.einsum('nbsf,nfd->bsd', gs * us, w2_s) / w1_s.shape[0]
        alpha = 0.5
        return alpha * shared + (1.0 - alpha) * routed
    h = _L0_tok_ref(x, L0_tok_W, L0_tok_b, L0_tok_alpha)
    h = h + _L0_attn_ref(_layernorm(h, axis=-1), L0_attn_W_in, L0_attn_b_in, L0_attn_W_out, L0_attn_b_out)
    h = h + _L0_ffn_ref(_layernorm(h, axis=-1), L0_ffn_gate_w, L0_ffn_gate_bias, L0_ffn_w1, L0_ffn_w2, L0_ffn_w3, L0_ffn_ws1, L0_ffn_ws2, L0_ffn_ws3)
    h = h + _L1_attn_ref(_layernorm(h, axis=-1), L1_attn_Wq, L1_attn_Wk, L1_attn_Wv, L1_attn_Wbeta, L1_attn_b_beta, L1_attn_Wo, L1_attn_b_o, L1_attn_ln_g, L1_attn_ln_b)
    h = h + _L1_ffn_ref(_layernorm(h, axis=-1), L1_ffn_gate_W, L1_ffn_w1_e, L1_ffn_w3_e, L1_ffn_w2_e, L1_ffn_w1_s, L1_ffn_w3_s, L1_ffn_w2_s)
    return h

_drawn_inputs = setup_inputs


def setup_inputs(seed=0):
    import zlib

    import numpy as np

    out = dict(_drawn_inputs(seed))
    spreads = {'L0_attn_b_in': (0.0, 0.1),
     'L0_attn_b_out': (0.0, 0.1),
     'L0_ffn_gate_bias': (0.0, 0.614),
     'L1_attn_b_beta': (0.8999999761581421, 0.2),
     'L1_attn_b_o': (0.0, 0.1),
     'L1_attn_ln_g': (1.0, 0.2),
     'L1_attn_ln_b': (0.0, 0.1)}
    factors = {'L0_tok_b': 8.0,
     'L0_ffn_gate_w': 3.886,
     'L0_ffn_w1': 3.017,
     'L0_ffn_w2': 2.967,
     'L0_ffn_w3': 2.978,
     'L0_ffn_ws1': 4.117,
     'L0_ffn_ws2': 4.09,
     'L0_ffn_ws3': 4.058,
     'L1_ffn_gate_W': 8.0,
     'L1_ffn_w1_e': 8.0,
     'L1_ffn_w3_e': 8.0,
     'L1_ffn_w2_e': 8.0,
     'L1_ffn_w1_s': 8.0,
     'L1_ffn_w3_s': 8.0,
     'L1_ffn_w2_s': 8.0}
    for name, (base, spread) in spreads.items():
        noise = np.random.default_rng([zlib.crc32(name.encode()), seed]).standard_normal(out[name].shape)
        drawn = base * np.exp(spread * noise) if base else spread * noise
        out[name] = jnp.asarray(drawn.astype(out[name].dtype))
    for name, factor in factors.items():
        out[name] = (out[name] * factor).astype(out[name].dtype)
    return out
```

```python
import numpy as np

import concourse.bass as bass
from concourse import mybir
from contextlib import ExitStack

F32 = mybir.dt.float32
ALU = mybir.AluOpType
ACT = mybir.ActivationFunctionType
AX = mybir.AxisListType

B, L, N = 8, 512, 375
D, DK = 256, 64
P = 125
TB = N // P
TT = B * TB
LC = L // 128
DC = D // 128
NH, HD = 16, 64
HP = NH // 2
UW = 3 * 2 * HD
E0, F0 = 16, 128
E1, F1 = 8, 1024
FC1 = F1 // 128
H1, D1 = 16, 16
GT = 4
GN = GT * P
NG = TT // GT
EPS = 1e-5
SCALE = HD ** -0.5
MASKED = -1e30
BIG = 3e38


PRIMED = dict(x_free=2, tok_free=2, xt_ready=2, pj_read=2, rope_ready=2, masked=2, exped=2, ptT_ready=1,
              o_normed=1, oT_ready=2, hid0_ready=2, hid1_ready=2, y0_added=2, y1_added=2, stage_copied=2,
              u_made=2, vs_ready=1, beta_ready=1, scanned=2, scan_out=1, l1_added=3)


def wait_apart(eng, sem, value, unused):
    eng.wait_ge(sem, value)
    eng.sem_inc(unused, 1)


class Count:

    def __init__(self, eng, sem):
        self.eng, self.sem, self.base, self.n, self.outer = eng, sem, 0, 0, []

    def enter(self, it, per):
        self.outer.append((self.base, self.n))
        self.base, self.n = self.base + self.n + it * per, 0

    def leave(self, times, per):
        assert self.n == per, (self.n, per)
        base, n = self.outer.pop()
        self.base, self.n = base, n + times * per

    def __call__(self, ins, apart=None):
        ins.then_inc(self.sem, 1)
        self.n += 1
        if apart:
            wait_apart(self.eng, self.sem, self.base + self.n, apart)
        else:
            self.eng.wait_ge(self.sem, self.base + self.n)


def build(nc, x, dct, tok_w, tok_b, tok_alpha, w_in, b_in, w_out, b_out, sincos, mask, ident_in,
          gate0_w, gate0_b, ffn0_w, tri0, l1_w, l1_wk, l1_b_beta, l1_wo, l1_rows, gate1_w, ffn1_w, out):
    ctx = ExitStack()
    with ctx:
        def sb(name, shape):
            return ctx.enter_context(nc.sbuf_tensor(name, shape, F32))

        def sem(name):
            return ctx.enter_context(nc.semaphore(name))

        bank = [ctx.enter_context(nc.psum_tensor(f"bank{i}", [128, 512], F32)) for i in range(8)]

        Hs = sb("hidden", [P, TT, D])
        XN = sb("normed", [P, TT, D])
        XT = sb("normed_T", [128, DC, B * N])
        ident = sb("ident", [128, 128])
        stage = sb("norm_stage", [P, 2, D])
        stats = sb("stats", [P, 2, 6])
        pair = sb("mean_var_pair", [P, 2, 2])
        mv = sb("mean_var", [P, TT, 2])
        sd = sb("std", [P, TT])
        rstd = sb("rstd", [P, TT])
        eps = sb("eps", [P, 1])
        alpha = sb("alpha", [P, 1])
        alpha_b = sb("alpha_b", [P, D])
        bout_rows = sb("bout_rows", [P, D])
        l1rows = sb("l1_rows", [P, 3, D])
        comb0 = sb("comb0", [P, TT, E0 + 1])
        gates1 = sb("gates1", [P, TT, E1 + 1])
        g0w = sb("gate0_w", [128, DC, E0])
        g1w = sb("gate1_w", [128, DC, E1])
        g0b = sb("gate0_b", [P, E0])
        tri = sb("tri", [P, E0, E0])
        small = sb("small", [P, 6, TT * E0])

        AR = 22600
        arena = sb("arena", [128, AR])

        class Arena:
            def __init__(self):
                self.at = 0

            def take(self, parts, *dims):
                n = int(np.prod(dims))
                v = arena[0:parts, self.at:self.at + n]
                self.at += n
                assert self.at <= AR, self.at
                if len(dims) > 1:
                    names = "abcde"[:len(dims)]
                    v = v.rearrange(f"p ({' '.join(names)}) -> p {' '.join(names)}",
                                    **{k: d for k, d in zip(names[1:], dims[1:])})
                return v

        a = Arena()
        xbuf = a.take(128, 2, LC, N)
        cT = a.take(DK, L)
        tokw = a.take(DK, D)
        cw = a.take(128, LC, D)
        a = Arena()
        win = a.take(128, DC, HP * UW)
        wout = a.take(128, HP, D)
        cs = a.take(P, 2, TB, 32)
        mk = a.take(P, 3 * P)
        xtb = a.take(128, DC, N)
        qkb = a.take(P, 2, 4, 2, 32)
        mcos = a.take(P, 2, 4, 2, 32)
        msin = a.take(P, 2, 4, 2, 32)
        rk = a.take(P, 2, TB, 4, 64)
        vv = a.take(P, HP, TB, 2, HD + 1)
        qT = a.take(128, 2, 2, N)
        kT = a.take(128, 2, N)
        sm = a.take(P, 2, N)
        nmax = a.take(P, 2)
        pr = a.take(P, 2, 2, 6 * P)
        ptT = a.take(P, 2, N)
        rsum = a.take(P, 6)
        xn_flat = XN[:, :, :].rearrange("p t d -> p (t d)")
        bin_rows = xn_flat[:, 0:HP * UW]
        on = xn_flat[:, HP * UW:HP * UW + TB * D * 4].rearrange("p (t a h d) -> p t a h d", t=TB, a=HP, h=2)
        a = Arena()
        w13 = a.take(128, 2, 2, DC, F0)
        w2 = a.take(128, 2, D)
        hid = a.take(128, 2, GN)
        sg = a.take(128, 2, GN)
        cmpA = a.take(P, TT, E0, E0)
        cmpB = a.take(P, TT, E0, E0)
        a = Arena()
        l1w = a.take(128, DC, 4, D)
        lraw = a.take(128, DC, 2 * D + H1)
        lwo = a.take(128, DC, D)
        hsum = a.take(128, DC, 2, H1)
        bbeta = a.take(128, DC)
        vsb = a.take(128, 2, N)
        bet = a.take(128, 2, N)
        uu = a.take(128, 2, N)
        ss = a.take(128, 2, N)
        oo = a.take(128, 2, DC, N)
        ztmp = a.take(P, 2, D)
        a = Arena()
        fw = a.take(128, 2, 3 * DC * F1)
        fhid = a.take(128, 2, FC1, GN)
        fsg = a.take(128, 2, GN)
        oT1 = sb("heads_T", [128, HP, N])

        S = {}

        def s(name):
            if name not in S:
                S[name] = sem(name)
            return S[name]

        phase_done = s("phase_done")

        block = ctx.enter_context(nc.Block())

        def barrier(eng, k):
            eng.drain().then_inc(phase_done, 1)
            eng.wait_ge(phase_done, 5 * k)

        @block.sync
        def _(sp):
            for name, n in PRIMED.items():
                sp.sem_inc(s(name), n)
            sp.dma_start(cT, dct).then_inc(s("load_tok"), 16)
            sp.dma_start(tokw, tok_w).then_inc(s("load_tok"), 16)
            sp.dma_start(ident[:, :], ident_in).then_inc(s("load_tok"), 16)
            sp.dma_start(alpha[:, :], tok_alpha.partition_broadcast(P)).then_inc(s("load_tok"), 16)
            sp.dma_start(alpha_b[:, :], tok_b.partition_broadcast(P)).then_inc(s("load_tok"), 16)
            sp.dma_start(bout_rows[:, :], b_out.partition_broadcast(P)).then_inc(s("load_rows"), 16)
            sp.dma_start(l1rows[:, :, :], l1_rows.partition_broadcast(P)).then_inc(s("load_rows"), 16)
            sp.dma_start(g0b[:, :], gate0_b.partition_broadcast(P)).then_inc(s("load_rows"), 16)
            sp.dma_start(tri[:, :, :], tri0.partition_broadcast(P)).then_inc(s("load_rows"), 16)
            sp.dma_start(g0w[:, :, :], gate0_w).then_inc(s("load_rows"), 16)
            sp.dma_start(g1w[:, :, :], gate1_w).then_inc(s("load_rows"), 16)
            with sp.Fori(0, B // 2) as bb:
                for j in range(2):
                    sp.wait_ge(s("x_free"), 2 * bb + j + 1)
                    sp.dma_start(xbuf[:, j], x[bass.ds(2 * bb + j, 1)].rearrange("o (c p) n -> p (o c) n", p=128))\
                        .then_inc(s(f"x_ready{j}"), 16)
            barrier(sp, 1)
            sp.dma_start(win, w_in).then_inc(s("load_attn"), 16)
            sp.dma_start(bin_rows, b_in.partition_broadcast(P)).then_inc(s("load_attn"), 16)
            sp.dma_start(wout, w_out).then_inc(s("load_attn"), 16)
            sp.dma_start(cs, sincos).then_inc(s("load_attn"), 16)
            sp.dma_start(mk, mask).then_inc(s("load_attn"), 16)
            barrier(sp, 2)
            barrier(sp, 3)
            for i in range(2):
                sp.dma_start(w13[:, i], ffn0_w[i, :, 0:4 * F0]).then_inc(s(f"w0_ready{i}"), 16)
                sp.dma_start(w2[:, i], ffn0_w[i, :, 4 * F0:4 * F0 + D]).then_inc(s(f"w0_ready{i}"), 16)
            with sp.Fori(1, E0 // 2) as ee:
                for i in range(2):
                    sp.wait_ge(s("y0_ready"), (2 * ee + i - 1) * 2 * NG)
                    sp.dma_start(w13[:, i], ffn0_w[bass.ds(2 * ee + i, 1), :, 0:4 * F0].rearrange("o p n -> p (o n)"))\
                        .then_inc(s(f"w0_ready{i}"), 16)
                    sp.dma_start(w2[:, i], ffn0_w[bass.ds(2 * ee + i, 1), :, 4 * F0:4 * F0 + D].rearrange("o p n -> p (o n)"))\
                        .then_inc(s(f"w0_ready{i}"), 16)
            sp.wait_ge(s("y0_ready"), (E0 - 1) * 2 * NG)
            sp.dma_start(w13[:, 0], ffn0_w[E0, :, 0:4 * F0]).then_inc(s("w0_ready0"), 16)
            sp.dma_start(w2[:, 0], ffn0_w[E0, :, 4 * F0:4 * F0 + D]).then_inc(s("w0_ready0"), 16)
            barrier(sp, 4)
            sp.dma_start(lraw, l1_w).then_inc(s("load_l1"), 16)
            sp.dma_start(lwo, l1_wo).then_inc(s("load_l1"), 16)
            sp.dma_start(l1w[:, :, 0, :], l1_wk).then_inc(s("load_l1"), 16)
            sp.dma_start(bbeta, l1_b_beta).then_inc(s("load_l1"), 16)
            barrier(sp, 5)
            barrier(sp, 6)
            barrier(sp, 7)
            for i in range(2):
                sp.dma_start(fw[:, i], ffn1_w[i]).then_inc(s(f"w1_ready{i}"), 16)
            with sp.Fori(1, E1 // 2) as ee:
                for i in range(2):
                    sp.wait_ge(s("y1_ready"), (2 * ee + i - 1) * 2 * NG)
                    sp.dma_start(fw[:, i], ffn1_w[bass.ds(2 * ee + i, 1)].rearrange("o p n -> p (o n)"))\
                        .then_inc(s(f"w1_ready{i}"), 16)
            sp.wait_ge(s("y1_ready"), (E1 - 1) * 2 * NG)
            sp.dma_start(fw[:, 0], ffn1_w[E1]).then_inc(s("w1_ready0"), 16)
            barrier(sp, 8)
            sp.dma_start(out.rearrange("(t p) d -> p t d", p=P), Hs[:, :, :]).then_inc(s("stored"), 16)
            sp.wait_ge(s("stored"), 16)

        @block.tensor
        def _(pe):
            def transpose_normed(k):
                with pe.Fori(0, TT // 2) as tt:
                    for i in range(2):
                        g = k * TT + 2 * tt + i
                        pe.wait_ge(s("stage_ready"), g + 1)
                        pe.wait_ge(s("xt_ready"), g + 1)
                        for c in range(DC):
                            m = pe.transpose(bank[4 + i][:, c * P:(c + 1) * P], stage[:, i, c * 128:(c + 1) * 128],
                                             ident[0:P, 0:P])
                        m.then_inc(s("turned"), 1)

            def gate_scores(w, e, sem_name):
                for t in range(TT):
                    for c in range(DC):
                        m = pe.matmul(bank[0][0:P, t * e:(t + 1) * e], XT[:, c, t * P:(t + 1) * P], w[:, c, :],
                                      start=(c == 0), stop=(c == DC - 1))
                m.then_inc(s(sem_name), 1)

            pe.wait_ge(s("load_tok"), 80)
            for c in range(LC):
                m = pe.matmul(bank[c // 2][:, (c % 2) * D:(c % 2 + 1) * D], cT[:, c * 128:(c + 1) * 128], tokw,
                              start=True, stop=True)
            m.then_inc(s("cw_made"), 1)
            pe.wait_ge(s("cw_ready"), 1)
            with pe.Fori(0, B // 2) as bb:
                for j in range(2):
                    pe.wait_ge(s(f"x_ready{j}"), 16 * bb + 16)
                    for t in range(TB):
                        i = j * TB + t
                        pe.wait_ge(s("tok_free"), 6 * bb + i + 1)
                        for c in range(LC):
                            m = pe.matmul(bank[i % 2][0:P, 0:D], xbuf[:, j, c, t * P:(t + 1) * P], cw[:, c, :],
                                          start=(c == 0), stop=(c == LC - 1))
                        m.then_inc(s("tok_made"), 1)
                    pe.drain().then_inc(s("x_free"), 1)
            barrier(pe, 1)
            transpose_normed(0)
            barrier(pe, 2)

            pe.wait_ge(s("load_attn"), 80)

            def project(b, hp, par, t):
                n = (b * HP + hp) * TB + t
                pe.wait_ge(s("pj_read"), n + 1)
                for c in range(DC):
                    m = pe.matmul(bank[(par + t) % 2][0:P, 0:UW], xtb[:, c, t * P:(t + 1) * P],
                                  win[:, c, bass.ds(hp * UW, UW)], start=(c == 0), stop=(c == DC - 1))
                m.then_inc(s("pj_made"), 1)

            def turn_qk(b, hp, par):
                u = b * HP + hp
                pe.wait_ge(s("rope_ready"), (u + 1) * TB + 2)
                for k in range(2):
                    for t in range(TB):
                        m = pe.transpose(bank[2 + k][:, t * P:(t + 1) * P],
                                         rk[:, par, t, 2 * k:2 * k + 2, :].rearrange("p a b -> p (a b)"), ident[0:P, 0:P])
                m.then_inc(s("qk_turned"), 1)

            def scores(b, hp, par, g):
                n = (b * HP + hp) * 6 + g
                h, qt = g // TB, g % TB
                pe.wait_ge(s("qkT_ready"), b * HP + hp + 1)
                pe.wait_ge(s("masked"), n + 1)
                pe.matmul(bank[4 + g % 2][0:P, 0:(qt + 1) * P], qT[:, par, h, qt * P:(qt + 1) * P],
                          kT[:, par, 0:(qt + 1) * P], start=True, stop=True).then_inc(s("scored"), 1)

            def turn_probs(b, hp, par, g):
                n = (b * HP + hp) * 6 + g
                h, qt = g // TB, g % TB
                pe.wait_ge(s("exped"), n + 3)
                pe.wait_ge(s("ptT_ready"), n + 1)
                for j in range(qt + 1):
                    o = (0, P, 3 * P)[qt] + j * P
                    m = pe.transpose(bank[6][0:P, j * P:(j + 1) * P], pr[:, par, h, o:o + P], ident[0:P, 0:P])
                m.then_inc(s("p_turned"), 1)

            def weigh(b, hp, par, g):
                u = b * HP + hp
                h, qt = g // TB, g % TB
                if g == 0:
                    pe.wait_ge(s("o_normed"), u + 1)
                pe.wait_ge(s("ptT_ready"), u * 6 + g + 2)
                for j in range(qt + 1):
                    m = pe.matmul(bank[7][0:P, g * (HD + 1):(g + 1) * (HD + 1)], ptT[:, g % 2, j * P:(j + 1) * P],
                                  vv[:, bass.ds(hp, 1), j, h, :].rearrange("p o d -> p (o d)"),
                                  start=(j == 0), stop=(j == qt))
                if g == 5:
                    m.then_inc(s("weighed"), 1)

            with pe.Fori(0, B) as b:
                pe.wait_ge(s("xtb_ready"), b + 1)
                for t in range(TB):
                    project(b, 0, 0, t)
                turn_qk(b, 0, 0)

                def step(hp, par, before, after):
                    for g in range(6):
                        scores(b, hp, par, g)
                        if after and g % 2 == 0:
                            project(b, hp + 1, 1 - par, g // 2)
                        if before:
                            turn_probs(b, hp - 1, 1 - par, g)
                            if g >= 1:
                                weigh(b, hp - 1, 1 - par, g - 1)
                    if before:
                        weigh(b, hp - 1, 1 - par, 5)
                    if after:
                        turn_qk(b, hp + 1, 1 - par)

                step(0, 0, False, True)
                with pe.Fori(0, HP // 2 - 1) as hh:
                    for i in range(2):
                        step(2 * hh + (1 + i), (1 + i) % 2, True, True)
                step(HP - 1, 1, True, False)
                for g in range(6):
                    turn_probs(b, HP - 1, 1, g)
                    if g >= 1:
                        weigh(b, HP - 1, 1, g - 1)
                weigh(b, HP - 1, 1, 5)
                pe.wait_ge(s("o_normed"), b * HP + HP + 1)
                for hp in range(HP):
                    pe.wait_ge(s("oT_ready"), b * HP + hp + 1)
                    for t in range(TB):
                        m = pe.transpose(bank[2 + hp % 2][:, t * P:(t + 1) * P],
                                         on[:, t, hp].rearrange("p a b -> p (a b)"), ident[0:P, 0:P])
                    m.then_inc(s("o_turned"), 1)
                pe.wait_ge(s("oT_ready"), b * HP + HP + 2)
                pe.wait_ge(s("masked"), (b + 1) * HP * 6 + 2)
                for t in range(TB):
                    for hp in range(HP):
                        m = pe.matmul(bank[(4, 5, 7)[t]][0:P, 0:D], oT1[:, hp, t * P:(t + 1) * P], wout[:, hp, :],
                                      start=(hp == 0), stop=(hp == HP - 1))
                    m.then_inc(s("att_made"), 1)
                pe.wait_ge(s("att_added"), TB * b + TB)
            barrier(pe, 3)

            def feed_forward(k, experts, fc, e, i, w1_at, w3_at, w2_at, hidden):
                with pe.Fori(0, NG // 2) as gg:
                    for j in range(2):
                        for f in range(fc):
                            n = ((e * NG) + 2 * gg + j) * fc + f
                            r = f % 2 if fc > 1 else j
                            pe.wait_ge(s(f"hid{k}_ready"), n + 1)
                            for w, bk, name in ((w1_at, 0, "up"), (w3_at, 2, "side")):
                                for c in range(DC):
                                    m = pe.matmul(bank[bk + r][:, 0:GN], w(i, c, f),
                                                  XT[:, c, bass.ds((2 * gg + j) * GN, GN)],
                                                  start=(c == 0), stop=(c == DC - 1))
                                m.then_inc(s(f"{name}{k}_made"), 1)
                    for j in range(2):
                        m_ = e * NG + 2 * gg + j
                        pe.wait_ge(s(f"hid{k}_ready"), (m_ + 1) * fc + 2)
                        for h in range(GT // 2):
                            pe.wait_ge(s(f"y{k}_added"), 2 * m_ + h + 1)
                            for t in range(2):
                                for f in range(fc):
                                    m = pe.matmul(bank[4 + h][0:P, t * D:(t + 1) * D],
                                                  hidden(j, f)[:, (2 * h + t) * P:(2 * h + t + 1) * P], w2_at(i, f),
                                                  start=(f == 0), stop=(f == fc - 1))
                            m.then_inc(s(f"y{k}_ready"), 1)

            transpose_normed(1)
            pe.wait_ge(s("xt_ready"), 2 * TT + 2)
            pe.wait_ge(s("load_rows"), 96)
            gate_scores(g0w, E0, "gate0_made")

            def w0_1(i, c, f):
                return w13[:, i, 0, c, :]

            def w0_3(i, c, f):
                return w13[:, i, 1, c, :]

            def w0_2(i, f):
                return w2[:, i, :]

            def hid0(j, f):
                return hid[:, j, :]

            pe.wait_ge(s("gate0_sig"), 1)
            with pe.Fori(0, E0 // 2) as ee:
                for i in range(2):
                    wait_apart(pe, s(f"w0_ready{i}"), 32 * ee + 32, s("unused"))
                    feed_forward(0, E0, 1, 2 * ee + i, i, w0_1, w0_3, w0_2, hid0)
            pe.wait_ge(s("w0_ready0"), 32 * (E0 // 2) + 32)
            feed_forward(0, E0, 1, E0, 0, w0_1, w0_3, w0_2, hid0)
            barrier(pe, 4)

            transpose_normed(2)
            barrier(pe, 5)
            pe.wait_ge(s("l1w_ready"), 1)
            with pe.Fori(0, B) as b:
                for c in range(DC):
                    for q in range(4):
                        pe.wait_ge(s(("u_made", "vs_ready", "beta_ready", "scan_out")[q]), DC * b + c + (2 if q == 0 else 1))
                        for kc in range(DC):
                            m = pe.matmul(bank[q][:, 0:N], l1w[:, kc, q, c * 128:(c + 1) * 128],
                                          XT[:, kc, bass.ds(b * N, N)], start=(kc == 0), stop=(kc == DC - 1))
                        m.then_inc(s(f"l1_made{q}"), 1)
                pe.wait_ge(s("scan_out"), DC * b + DC + 1)
                for t in range(TB):
                    pe.wait_ge(s("l1_added"), TB * b + t + 1)
                    for c in range(DC):
                        m = pe.matmul(bank[4 + t][0:P, 0:D], oo[:, 0, c, t * P:(t + 1) * P], lwo[:, c, :],
                                      start=(c == 0), stop=(c == DC - 1))
                    m.then_inc(s("l1_out"), 1)
            barrier(pe, 6)
            transpose_normed(3)
            pe.wait_ge(s("xt_ready"), 4 * TT + 2)
            gate_scores(g1w, E1, "gate1_made")
            barrier(pe, 7)

            fwv = fw.rearrange("p i (w n) -> p i w n", w=3)
            f13 = fwv[:, :, 0:2, :].rearrange("p i w (c n) -> p i w c n", c=DC)
            f2 = fwv[:, :, 2, :].rearrange("p i (f n) -> p i f n", f=FC1)

            def w1_1(i, c, f):
                return f13[:, i, 0, c, f * 128:(f + 1) * 128]

            def w1_3(i, c, f):
                return f13[:, i, 1, c, f * 128:(f + 1) * 128]

            def w1_2(i, f):
                return f2[:, i, f, :]

            def hid1(j, f):
                return fhid[:, j, f, :]

            with pe.Fori(0, E1 // 2) as ee:
                for i in range(2):
                    wait_apart(pe, s(f"w1_ready{i}"), 16 * ee + 16, s("unused"))
                    feed_forward(1, E1, FC1, 2 * ee + i, i, w1_1, w1_3, w1_2, hid1)
            pe.wait_ge(s("w1_ready0"), 16 * (E1 // 2) + 16)
            feed_forward(1, E1, FC1, E1, 0, w1_1, w1_3, w1_2, hid1)
            barrier(pe, 8)

        @block.scalar
        def _(act):
            def copy_turned(k):
                act.wait_ge(s("var_ready"), (k + 1) * (TT // 2))
                act.activation(sd[:, :], mv[:, :, 1], ACT.Sqrt, bias=eps[:, 0:1]).then_inc(s("sd_ready"), 1)
                with act.Fori(0, TT // 2) as tt:
                    for i in range(2):
                        act.wait_ge(s("turned"), k * TT + 2 * tt + i + 1)
                        act.activation(XT[:, :, bass.ds((2 * tt + i) * P, P)],
                                       bank[4 + i][:, 0:DC * P].rearrange("p (c n) -> p c n", c=DC),
                                       ACT.Copy).then_inc(s("xt_ready"), 1)

            act.wait_ge(s("eps_ready"), 1)
            barrier(act, 1)
            copy_turned(0)
            barrier(act, 2)

            def exps(b, hp, par, g):
                n = (b * HP + hp) * 6 + g
                h, qt = g // TB, g % TB
                w, o = (qt + 1) * P, (0, P, 3 * P)[qt]
                act.wait_ge(s("masked"), n + 3)
                act.activation(pr[:, par, h, o:o + w], sm[:, g % 2, 0:w], ACT.Exp, bias=nmax[:, g % 2:g % 2 + 1],
                               scale=-1.0).then_inc(s("exped"), 1)

            def copy_probs(b, hp, g):
                n = (b * HP + hp) * 6 + g
                w = (g % TB + 1) * P
                act.wait_ge(s("p_turned"), n + 1)
                act.activation(ptT[:, g % 2, 0:w], bank[6][0:P, 0:w], ACT.Copy).then_inc(s("ptT_ready"), 1)

            with act.Fori(0, B) as b:
                def step(hp, par, before):
                    for g in range(6):
                        exps(b, hp, par, g)
                        if before:
                            copy_probs(b, hp - 1, g)

                step(0, 0, False)
                with act.Fori(0, HP // 2 - 1) as hh:
                    for i in range(2):
                        step(2 * hh + (1 + i), (1 + i) % 2, True)
                step(HP - 1, 1, True)
                for g in range(6):
                    copy_probs(b, HP - 1, g)
                for hp in range(HP):
                    act.wait_ge(s("o_turned"), b * HP + hp + 1)
                    act.activation(oT1[:, hp, :], bank[2 + hp % 2][:, 0:N], ACT.Copy).then_inc(s("oT_ready"), 1)
            barrier(act, 3)

            def silus(k, fc, e, sgv):
                with act.Fori(0, NG // 2) as gg:
                    for j in range(2):
                        for f in range(fc):
                            n = (e * NG + 2 * gg + j) * fc + f
                            r = f % 2 if fc > 1 else j
                            act.wait_ge(s(f"up{k}_made"), n + 1)
                            act.wait_ge(s(f"hid{k}_ready"), n + 1)
                            act.activation(sgv[:, r, :], bank[r][:, 0:GN], ACT.Silu).then_inc(s(f"silu{k}"), 1)

            copy_turned(1)
            act.wait_ge(s("gate0_made"), 1)
            act.activation(small[:, 0, :], bank[0][0:P, 0:TT * E0], ACT.Sigmoid).then_inc(s("gate0_sig"), 1)
            with act.Fori(0, E0 // 2) as ee:
                for i in range(2):
                    silus(0, 1, 2 * ee + i, sg)
            silus(0, 1, E0, sg)
            barrier(act, 4)
            copy_turned(2)
            barrier(act, 5)
            with act.Fori(0, B) as b:
                for c in range(DC):
                    act.wait_ge(s("l1_made1"), DC * b + c + 1)
                    act.wait_ge(s("u_made"), DC * b + c + 1)
                    act.activation(vsb[:, c, :], bank[1][:, 0:N], ACT.Copy).then_inc(s("vs_ready"), 1)
                    act.wait_ge(s("l1_made2"), DC * b + c + 1)
                    act.wait_ge(s("scanned"), DC * b + c + 1)
                    act.activation(bet[:, c, :], bank[2][:, 0:N], ACT.Sigmoid, bias=bbeta[:, c:c + 1])\
                        .then_inc(s("beta_ready"), 1)
            barrier(act, 6)
            act.wait_ge(s("var2_ready"), TT // 2)
            act.activation(sd[:, :], mv[:, :, 1], ACT.Sqrt, bias=eps[:, 0:1]).then_inc(s("sd2_ready"), 1)
            copy_turned(3)
            act.wait_ge(s("gate1_made"), 1)
            act.wait_ge(s("gate1_max"), 1)
            act.activation(small[:, 1, 0:TT * E1], small[:, 0, 0:TT * E1], ACT.Exp).then_inc(s("gate1_exp"), 1)
            barrier(act, 7)
            with act.Fori(0, E1 // 2) as ee:
                for i in range(2):
                    silus(1, FC1, 2 * ee + i, fsg)
            silus(1, FC1, E1, fsg)
            barrier(act, 8)

        @block.gpsimd
        def _(pool):
            chain = Count(pool, s("pool_step"))
            pool.memset(eps[:, :], EPS).then_inc(s("eps_ready"), 1)
            barrier(pool, 1)
            barrier(pool, 2)
            pool.wait_ge(s("load_rows"), 96)
            pool.memset(qT[:, :, :, :], 0.0).then_inc(s("q_zero"), 1)
            pool.memset(vv[:, :, :, :, HD:HD + 1], 1.0).then_inc(s("q_zero"), 1)

            def rope(b, hp, par):
                for t in range(TB):
                    n = (b * HP + hp) * TB + t
                    r = (par + t) % 2
                    pool.wait_ge(s("roped"), n + 1)
                    pool.tensor_tensor(rk[:, par, t, :, 0:32], mcos[:, r, :, 1, :], msin[:, r, :, 0, :], ALU.add)
                    pool.tensor_tensor(rk[:, par, t, :, 32:64], mcos[:, r, :, 0, :], msin[:, r, :, 1, :],
                                       ALU.subtract).then_inc(s("rope_ready"), 1)

            with pool.Fori(0, B) as b:
                pool.wait_ge(s("pj_read"), b * HP * TB + 2)
                pool.tensor_copy(xtb, XT[:, :, bass.ds(b * N, N)]).then_inc(s("xtb_ready"), 1)
                for t in range(TB):
                    ins = pool.tensor_tensor(Hs[:, bass.ds(b * TB + t, 1), :].rearrange("p o d -> p (o d)"),
                                             Hs[:, bass.ds(b * TB + t, 1), :].rearrange("p o d -> p (o d)"),
                                             bout_rows[:, :], ALU.add)
                ins.then_inc(s("bout_added"), 1)
                rope(b, 0, 0)
                rope(b, 1, 1)
                with pool.Fori(0, HP // 2 - 1) as hh:
                    for i in range(2):
                        rope(b, 2 * hh + (2 + i), i)
            barrier(pool, 3)
            barrier(pool, 4)
            with pool.Fori(0, TT // 2) as tt:
                for i in range(2):
                    pool.wait_ge(s("stage_ready"), 2 * TT + 2 * tt + i + 1)
                    pool.tensor_copy(XN[:, bass.ds(2 * tt + i, 1), :].rearrange("p o d -> p (o d)"), stage[:, i, :])\
                        .then_inc(s("stage_copied"), 1)
            barrier(pool, 5)
            barrier(pool, 6)
            barrier(pool, 7)
            barrier(pool, 8)

        @block.vector
        def _(v):
            chain = Count(v, s("dve_step"))

            def tile(buf, g):
                return buf[:, bass.ds(g, 1), :].rearrange("p o d -> p (o d)")

            def variances(src, sem_name):
                with v.Fori(0, TT // 2) as tt:
                    chain.enter(tt, 3)
                    for i in range(2):
                        st = v.bn_stats(stats[:, i, :], tile(src, 2 * tt + i))
                        if i == 0:
                            st.then_inc(s("dve_step"), 1)
                            chain.n += 1
                    chain(st, apart=s("unused"))
                    for i in range(2):
                        ag = v.bn_aggr(pair[:, i, :], stats[:, i, :])
                    chain(ag)
                    v.tensor_copy(mv[:, bass.ds(2 * tt, 2), :], pair[:, :, :]).then_inc(s(sem_name), 1)
                chain.leave(TT // 2, 3)

            def normalise(k, src, extra_wait=None):
                variances(src, "var_ready")
                v.wait_ge(s("sd_ready"), k + 1)
                chain(v.reciprocal(rstd[:, :], sd[:, :]))
                with v.Fori(0, TT // 2) as tt:
                    for i in range(2):
                        g = 2 * tt + i
                        v.wait_ge(s("xt_ready"), k * TT + g + 1)
                        if extra_wait:
                            v.wait_ge(s(extra_wait), g + 1)
                        v.tensor_scalar(stage[:, i, :], tile(src, g), mv[:, bass.ds(g, 1), 0], rstd[:, bass.ds(g, 1)],
                                        ALU.subtract, ALU.mult).then_inc(s("stage_ready"), 1)

            v.wait_ge(s("load_tok"), 80)
            v.wait_ge(s("cw_made"), 1)
            for h in range(2):
                cp = v.tensor_copy(cw[:, 2 * h:2 * h + 2, :].rearrange("p a b -> p (a b)"), bank[h][:, :])
            cp.then_inc(s("cw_ready"), 1)
            chain(v.tensor_scalar(alpha_b[:, :], alpha_b[:, :], alpha[:, 0:1], None, ALU.mult))
            with v.Fori(0, B // 2) as bb:
                for i in range(2 * TB):
                    g = 2 * TB * bb + i
                    v.wait_ge(s("tok_made"), g + 1)
                    v.scalar_tensor_tensor(tile(Hs, g), bank[i % 2][0:P, 0:D], alpha[:, 0:1], alpha_b[:, :],
                                           ALU.mult, ALU.add).then_inc(s("tok_free"), 1)
            v.wait_ge(s("tok_free"), TT + 2)
            barrier(v, 1)
            normalise(0, Hs)
            barrier(v, 2)

            v.wait_ge(s("load_attn"), 80)
            v.wait_ge(s("q_zero"), 2)

            def take_projection(b, hp, par, t):
                n = (b * HP + hp) * TB + t
                r = (par + t) % 2
                v.wait_ge(s("pj_made"), n + 1)
                v.tensor_tensor(vv[:, bass.ds(hp, 1), t, :, 0:HD].rearrange("p o h d -> p (o h) d"),
                                bank[r][0:P, 4 * HD:6 * HD].rearrange("p (h d) -> p h d", h=2),
                                bin_rows[:, bass.ds(hp * UW + 4 * HD, 2 * HD)].rearrange("p (h d) -> p h d", h=2),
                                ALU.add)
                v.tensor_tensor(qkb[:, r].rearrange("p a b c -> p (a b c)"), bank[r][0:P, 0:4 * HD],
                                bin_rows[:, bass.ds(hp * UW, 4 * HD)], ALU.add).then_inc(s("pj_read"), 1)
                v.wait_ge(s("pj_read"), n + 3)
                v.wait_ge(s("rope_ready"), n + 1)
                x8 = qkb[:, r].rearrange("p a b c -> p (a b) c")
                for k, m in ((0, mcos), (1, msin)):
                    ins = v.tensor_tensor(m[:, r].rearrange("p a b c -> p (a b) c"), x8,
                                          cs[:, k, t, :].unsqueeze(1).to_broadcast([P, 8, 32]), ALU.mult)
                ins.then_inc(s("roped"), 1)

            def take_qkT(b, hp, par):
                v.wait_ge(s("qk_turned"), b * HP + hp + 1)
                v.tensor_copy(qT[0:64, par, 0, :], bank[2][0:64, 0:N])
                v.tensor_copy(qT[64:128, par, 1, :], bank[2][64:128, 0:N])
                v.tensor_copy(kT[:, par, :], bank[3][:, 0:N]).then_inc(s("qkT_ready"), 1)

            def mask_scores(b, hp, g):
                n = (b * HP + hp) * 6 + g
                w = (g % TB + 1) * P
                v.wait_ge(s("exped"), n + 1)
                wait_apart(v, s("scored"), n + 1, s("unused"))
                v.tensor_tensor_reduce(sm[:, g % 2, 0:w], bank[4 + g % 2][0:P, 0:w], mk[:, 3 * P - w:3 * P], -SCALE, BIG,
                                       ALU.add, ALU.min, nmax[:, g % 2:g % 2 + 1]).then_inc(s("masked"), 1)

            def divide(b, hp):
                v.wait_ge(s("weighed"), b * HP + hp + 1)
                ob = bank[7][0:P, 0:6 * (HD + 1)].rearrange("p (g d) -> p g d", d=HD + 1)
                chain(v.reciprocal(rsum, ob[:, :, HD]))
                for h in range(2):
                    ins = v.tensor_tensor(on[:, :, bass.ds(hp, 1), h, :].rearrange("p t o d -> p t (o d)"),
                                          ob[:, h * TB:(h + 1) * TB, 0:HD],
                                          rsum[:, h * TB:(h + 1) * TB].unsqueeze(2).to_broadcast([P, TB, HD]), ALU.mult)
                ins.then_inc(s("o_normed"), 1)

            with v.Fori(0, B) as b:
                chain.enter(b, HP)
                for t in range(TB):
                    take_projection(b, 0, 0, t)
                take_qkT(b, 0, 0)

                def step(hp, par, before, after):
                    for g in range(6):
                        mask_scores(b, hp, g)
                        if after and g % 2 == 0:
                            take_projection(b, hp + 1, 1 - par, g // 2)
                    if after:
                        take_qkT(b, hp + 1, 1 - par)
                    if before:
                        divide(b, hp - 1)

                step(0, 0, False, True)
                with v.Fori(0, HP // 2 - 1) as hh:
                    chain.enter(hh, 2)
                    for i in range(2):
                        step(2 * hh + (1 + i), (1 + i) % 2, True, True)
                chain.leave(HP // 2 - 1, 2)
                step(HP - 1, 1, True, False)
                divide(b, HP - 1)
                v.wait_ge(s("bout_added"), b + 1)
                for t in range(TB):
                    v.wait_ge(s("att_made"), TB * b + t + 1)
                    v.tensor_tensor(tile(Hs, b * TB + t), bank[(4, 5, 7)[t]][0:P, 0:D], tile(Hs, b * TB + t), ALU.add)\
                        .then_inc(s("att_added"), 1)
            chain.leave(B, HP)
            barrier(v, 3)

            normalise(1, Hs)
            v.wait_ge(s("load_rows"), 96)

            def top(src, e, out_ap, keep_n, big_a, big_b, T):
                si = src.unsqueeze(3).to_broadcast([P, T, e, e])
                sj = src.unsqueeze(2).to_broadcast([P, T, e, e])
                tr = tri[:, 0:e, 0:e].unsqueeze(1).to_broadcast([P, T, e, e])
                chain(v.tensor_tensor(big_a, sj, si, ALU.is_equal))
                chain(v.tensor_tensor(big_a, big_a, tr, ALU.mult))
                chain(v.tensor_tensor(big_b, sj, si, ALU.is_gt))
                chain(v.tensor_tensor(big_a, big_a, big_b, ALU.add))
                chain(v.tensor_reduce(out_ap, big_a, AX.X, ALU.add))
                chain(v.tensor_scalar(out_ap, out_ap, float(keep_n), None, ALU.is_lt))

            def sm3(k, e):
                return small[:, k, 0:TT * e].rearrange("p (t e) -> p t e", e=e)

            v.wait_ge(s("gate0_sig"), 1)
            sig, sbias, gmax, keep, rank = (sm3(k, E0) for k in range(5))
            chain(v.tensor_tensor(sbias, sig, g0b[:, :].unsqueeze(1).to_broadcast([P, TT, E0]), ALU.add))
            s4 = sbias.rearrange("p t (g e) -> p (t g) e", g=4)
            gm = small[:, 2, 0:TT * 4]
            chain(v.tensor_reduce(gm, s4, AX.X, ALU.max))
            kp = small[:, 3, 0:TT * 4]
            ca = cmpA.rearrange("p a b c -> p (a b c)")[:, 0:TT * 16].rearrange("p (t i j) -> p t i j", i=4, j=4)
            cb = cmpB.rearrange("p a b c -> p (a b c)")[:, 0:TT * 16].rearrange("p (t i j) -> p t i j", i=4, j=4)
            top(gm.rearrange("p (t g) -> p t g", g=4), 4, kp.rearrange("p (t g) -> p t g", g=4), 2, ca, cb, TT)
            keep3 = kp.unsqueeze(2).to_broadcast([P, TT * 4, 4])
            off = small[:, 4, 0:TT * 4]
            chain(v.tensor_scalar(off, kp, BIG, BIG, ALU.mult, ALU.subtract))
            chain(v.tensor_tensor(s4, s4, keep3, ALU.mult))
            chain(v.tensor_tensor(s4, s4, off.unsqueeze(2).to_broadcast([P, TT * 4, 4]), ALU.add))
            rk5 = sm3(5, E0)
            top(sbias, E0, rk5, 4, cmpA, cmpB, TT)
            chain(v.tensor_tensor(comb0[:, :, 0:E0], rk5, sig, ALU.mult))
            chain(v.memset(comb0[:, :, E0:E0 + 1], 1.0))

            def experts(k, fc, e, sgv, hidden, gate):
                with v.Fori(0, NG // 2) as gg:
                    for j in range(2):
                        for f in range(fc):
                            n = (e * NG + 2 * gg + j) * fc + f
                            r = f % 2 if fc > 1 else j
                            v.wait_ge(s(f"silu{k}"), n + 1)
                            v.wait_ge(s(f"side{k}_made"), n + 1)
                            v.tensor_tensor(hidden(j, f), bank[2 + r][:, 0:GN], sgv[:, r, :], ALU.mult)\
                                .then_inc(s(f"hid{k}_ready"), 1)
                    for j in range(2):
                        m_ = e * NG + 2 * gg + j
                        for h in range(GT // 2):
                            v.wait_ge(s(f"y{k}_ready"), 2 * m_ + h + 1)
                            v.wait_ge(s(f"y{k}_added"), 2 * m_ + h + 1)
                            for t in range(2):
                                g = (2 * gg + j) * GT + 2 * h + t
                                ins = v.scalar_tensor_tensor(tile(Hs, g), bank[4 + h][0:P, t * D:(t + 1) * D],
                                                             gate(g), tile(Hs, g), ALU.mult, ALU.add)
                            ins.then_inc(s(f"y{k}_added"), 1)

            def hid0(j, f):
                return hid[:, j, :]

            with v.Fori(0, E0 // 2) as ee:
                for i in range(2):
                    experts(0, 1, 2 * ee + i, sg, hid0,
                            lambda g, e=2 * ee + i: comb0[:, bass.ds(g, 1), bass.ds(e, 1)].rearrange("p a b -> p (a b)"))
            experts(0, 1, E0, sg, hid0, lambda g: comb0[:, bass.ds(g, 1), E0])
            barrier(v, 4)

            normalise(2, Hs, "stage_copied")
            v.wait_ge(s("load_l1"), 64)
            lr = lraw
            for q in range(2):
                hs = v.tensor_reduce(hsum[:, :, q, :], lr[:, :, q * D:(q + 1) * D].rearrange("p c (h d) -> p c h d", d=D1),
                                     AX.X, ALU.add)
            chain(hs)
            for q, src in ((3, hsum[:, :, 0, :]), (1, hsum[:, :, 1, :]), (2, lr[:, :, 2 * D:2 * D + H1])):
                for c in range(DC):
                    cp = v.tensor_copy(l1w[:, c, q, :].rearrange("p (h d) -> p h d", d=D1),
                                       src[:, c, :].unsqueeze(2).to_broadcast([128, H1, D1]))
            cp.then_inc(s("l1w_ready"), 1)
            barrier(v, 5)
            with v.Fori(0, B) as b:
                for c in range(DC):
                    v.wait_ge(s("vs_ready"), DC * b + c + 2)
                    v.wait_ge(s("l1_made0"), DC * b + c + 1)
                    v.tensor_tensor(uu[:, c, :], bank[0][:, 0:N], vsb[:, c, :], ALU.mult).then_inc(s("u_made"), 1)
                    v.wait_ge(s("u_made"), DC * b + c + 3)
                    v.wait_ge(s("beta_ready"), DC * b + c + 2)
                    v.tensor_tensor_scan(ss[:, c, :], bet[:, c, :], uu[:, c, :], 0.0, ALU.mult, ALU.add)\
                        .then_inc(s("scanned"), 1)
                    v.wait_ge(s("scanned"), DC * b + c + 3)
                    v.wait_ge(s("l1_made3"), DC * b + c + 1)
                    v.tensor_tensor(oo[:, 0, c, :], bank[3][:, 0:N], ss[:, c, :], ALU.mult).then_inc(s("scan_out"), 1)
                for t in range(TB):
                    v.wait_ge(s("l1_out"), TB * b + t + 1)
                    v.tensor_tensor(ztmp[:, t % 2, :], bank[4 + t][0:P, 0:D], l1rows[:, 0, :], ALU.add)\
                        .then_inc(s("z_part"), 1)
                    v.wait_ge(s("z_part"), TB * b + t + 1)
                    v.tensor_tensor(tile(XN, b * TB + t), tile(XN, b * TB + t), ztmp[:, t % 2, :], ALU.add)\
                        .then_inc(s("l1_added"), 1)
            v.wait_ge(s("l1_added"), TT + 3)
            barrier(v, 6)
            variances(XN, "var2_ready")
            v.wait_ge(s("sd2_ready"), 1)
            chain(v.reciprocal(rstd[:, :], sd[:, :]))
            with v.Fori(0, TT // 2) as tt:
                chain.enter(tt, 8)
                for i in range(2):
                    g = 2 * tt + i
                    chain(v.tensor_scalar(tile(XN, g), tile(XN, g), mv[:, bass.ds(g, 1), 0], rstd[:, bass.ds(g, 1)],
                                          ALU.subtract, ALU.mult))
                    chain(v.tensor_tensor(tile(XN, g), tile(XN, g), l1rows[:, 1, :], ALU.mult))
                    chain(v.tensor_tensor(tile(XN, g), tile(XN, g), l1rows[:, 2, :], ALU.add))
                    chain(v.tensor_tensor(tile(Hs, g), tile(Hs, g), tile(XN, g), ALU.add))
            chain.leave(TT // 2, 8)
            normalise(3, Hs)
            v.wait_ge(s("gate1_made"), 1)
            lg = bank[0][0:P, 0:TT * E1].rearrange("p (t e) -> p t e", e=E1)
            mx = small[:, 2, 0:TT]
            a0, a1 = sm3(0, E1), sm3(1, E1)
            chain(v.tensor_reduce(mx, lg, AX.X, ALU.max))
            v.tensor_tensor(a0, lg, mx.unsqueeze(2).to_broadcast([P, TT, E1]), ALU.subtract).then_inc(s("gate1_max"), 1)
            v.wait_ge(s("gate1_exp"), 1)
            sume = small[:, 3, 0:TT]
            chain(v.tensor_reduce(sume, a1, AX.X, ALU.add))
            chain(v.reciprocal(sume, sume))
            chain(v.tensor_tensor(a1, a1, sume.unsqueeze(2).to_broadcast([P, TT, E1]), ALU.mult))
            c8a = arena[0:P, 0:TT * 64].rearrange("p (t i j) -> p t i j", i=8, j=8)
            c8b = arena[0:P, TT * 64:2 * TT * 64].rearrange("p (t i j) -> p t i j", i=8, j=8)
            a4 = sm3(4, E1)
            top(a1, E1, a4, 2, c8a, c8b, TT)
            chain(v.tensor_tensor(a4, a4, a1, ALU.mult))
            chain(v.tensor_scalar(gates1[:, :, 0:E1], a4, 0.5, None, ALU.mult))
            chain(v.memset(gates1[:, :, E1:E1 + 1], 0.5 / E1))
            barrier(v, 7)

            def hid1(j, f):
                return fhid[:, j, f, :]

            with v.Fori(0, E1 // 2) as ee:
                for i in range(2):
                    experts(1, FC1, 2 * ee + i, fsg, hid1,
                            lambda g, e=2 * ee + i: gates1[:, bass.ds(g, 1), bass.ds(e, 1)].rearrange("p a b -> p (a b)"))
            experts(1, FC1, E1, fsg, hid1, lambda g: gates1[:, bass.ds(g, 1), E1])
            barrier(v, 8)


def kernel(x, L0_tok_W, L0_tok_b, L0_tok_alpha, L0_attn_W_in, L0_attn_b_in, L0_attn_W_out, L0_attn_b_out,
           L0_ffn_gate_w, L0_ffn_gate_bias, L0_ffn_w1, L0_ffn_w2, L0_ffn_w3, L0_ffn_ws1, L0_ffn_ws2, L0_ffn_ws3,
           L1_attn_Wq, L1_attn_Wk, L1_attn_Wv, L1_attn_Wbeta, L1_attn_b_beta, L1_attn_Wo, L1_attn_b_o,
           L1_attn_ln_g, L1_attn_ln_b, L1_ffn_gate_W, L1_ffn_w1_e, L1_ffn_w3_e, L1_ffn_w2_e,
           L1_ffn_w1_s, L1_ffn_w3_s, L1_ffn_w2_s):
    import concourse.bacc as bacc
    from concourse.bass_utils import run_bass_kernel_spmd

    def chunks(w):
        w = np.asarray(w)
        w = w.reshape(*w.shape[:-2], -1, 128, w.shape[-1])
        return np.swapaxes(w, -3, -2)

    def flat(w, keep):
        return w.reshape(*w.shape[:keep], -1)

    l = np.arange(L)
    m = np.where(l % 2 == 0, l // 2, L // 2 + (L - 1 - l) // 2)
    dct = np.cos(2 * np.pi * ((np.arange(DK)[:, None] * m[None, :]) % L) / L).astype(np.float32)
    half = HD // 2
    theta = np.float32(10000.0) ** (np.arange(half, dtype=np.float32) / np.float32(half - 1))
    pos = np.arange(N, dtype=np.float32)[:, None] / theta[None, :]
    sincos = np.stack([np.cos(pos), np.sin(pos)]).astype(np.float32).reshape(2, TB, P, half).transpose(2, 0, 1, 3)
    mask = np.zeros((P, 3 * P), np.float32)
    mask[:, 2 * P:] = np.where(np.arange(P)[None, :] > np.arange(P)[:, None], MASKED, 0.0)
    before = (np.arange(E0)[None, :] < np.arange(E0)[:, None]).astype(np.float32)

    heads = np.asarray(L0_attn_W_in).reshape(3, HP, 2 * HD, D).transpose(1, 0, 2, 3).reshape(HP * UW, D)
    head_bias = np.asarray(L0_attn_b_in).reshape(3, HP, 2 * HD).transpose(1, 0, 2).reshape(HP * UW)
    t = lambda w: np.swapaxes(np.asarray(w), -1, -2)
    ffn0 = np.concatenate([
        np.concatenate([flat(chunks(t(L0_ffn_w1)), 2), flat(chunks(t(L0_ffn_w3)), 2), t(L0_ffn_w2)], axis=2),
        np.concatenate([flat(chunks(t(L0_ffn_ws1)), 1), flat(chunks(t(L0_ffn_ws3)), 1), t(L0_ffn_ws2)], axis=1)[None]])
    side = lambda w: np.asarray(w).transpose(1, 0, 2).reshape(D, F1)
    ffn1 = np.concatenate([
        np.concatenate([flat(chunks(L1_ffn_w1_e), 2), flat(chunks(L1_ffn_w3_e), 2), flat(chunks(L1_ffn_w2_e), 2)], axis=2),
        np.concatenate([flat(chunks(side(L1_ffn_w1_s)), 1), flat(chunks(side(L1_ffn_w3_s)), 1),
                        flat(chunks(np.asarray(L1_ffn_w2_s).reshape(F1, D)), 1)], axis=1)[None]])
    arrays = {
        "x": np.asarray(x), "dct": dct, "tok_w": L0_tok_W, "tok_b": L0_tok_b, "tok_alpha": L0_tok_alpha,
        "w_in": chunks(t(heads)), "b_in": head_bias, "w_out": chunks(t(L0_attn_W_out)), "b_out": L0_attn_b_out,
        "sincos": sincos, "mask": mask, "ident_in": np.eye(128, dtype=np.float32),
        "gate0_w": chunks(t(L0_ffn_gate_w)), "gate0_b": L0_ffn_gate_bias, "ffn0_w": ffn0, "tri0": before,
        "l1_w": chunks(np.concatenate([np.asarray(L1_attn_Wq), np.asarray(L1_attn_Wv), np.asarray(L1_attn_Wbeta)], axis=1)),
        "l1_wk": chunks(L1_attn_Wk),
        "l1_b_beta": np.broadcast_to(np.asarray(L1_attn_b_beta)[:, None], (H1, D1)).reshape(DC, 128).T,
        "l1_wo": chunks(L1_attn_Wo),
        "l1_rows": np.stack([np.asarray(L1_attn_b_o), np.asarray(L1_attn_ln_g), np.asarray(L1_attn_ln_b)]),
        "gate1_w": chunks(t(L1_ffn_gate_W)), "ffn1_w": ffn1,
    }
    nc = bacc.Bacc("TRN2", target_bir_lowering=False, num_devices=1)
    arrays = {k + "_dram": np.ascontiguousarray(v) for k, v in arrays.items()}
    args = [nc.dram_tensor(k, v.shape, mybir.dt.from_np(v.dtype), kind="ExternalInput").ap() for k, v in arrays.items()]
    out = nc.dram_tensor("result_dram", [B * N, D], F32, kind="ExternalOutput").ap()
    build(nc, *args, out)
    r = run_bass_kernel_spmd(nc, [arrays], core_ids=[0])
    return r.results[0]["result_dram"].reshape(B, N, D)
```

```python
import numpy as np

import concourse.bass as bass
from concourse import mybir
from contextlib import ExitStack

F32 = mybir.dt.float32
ALU = mybir.AluOpType
ACT = mybir.ActivationFunctionType
AX = mybir.AxisListType

B, L, N = 8, 512, 375
D, DK = 256, 64
P = 125
TB = N // P
TT = B * TB
LC = L // 128
DC = D // 128
NH, HD = 16, 64
HP = NH // 2
UW = 3 * 2 * HD
E0, F0 = 16, 128
E1, F1 = 8, 1024
FC1 = F1 // 128
H1, D1 = 16, 16
GT = 4
GN = GT * P
NG = TT // GT
TOPK1 = 2
SR = 256
SLOTS = (TOPK1 * B * N + E1 * (SR - 1)) // SR
RW = D + 1
NOWHERE = 1 << 24
EPS = 1e-5
SCALE = HD ** -0.5
MASKED = -1e30
BIG = 3e38


PRIMED = dict(x_free=2, tok_free=2, xt_ready=2, pj_read=2, rope_ready=2, masked=2, exped=2, ptT_ready=1,
              o_normed=1, oT_ready=2, hid0_ready=2, hid1_ready=2, shid_ready=2, xsT_ready=2, ysb_ready=4,
              y0_added=2, y1_added=2, stage_copied=2,
              u_made=2, vs_ready=1, beta_ready=1, scanned=2, scan_out=1, l1_added=3)


def wait_apart(eng, sem, value, unused):
    eng.wait_ge(sem, value)
    eng.sem_inc(unused, 1)


class Count:

    def __init__(self, eng, sem):
        self.eng, self.sem, self.base, self.n, self.outer = eng, sem, 0, 0, []

    def enter(self, it, per):
        self.outer.append((self.base, self.n))
        self.base, self.n = self.base + self.n + it * per, 0

    def leave(self, times, per):
        assert self.n == per, (self.n, per)
        base, n = self.outer.pop()
        self.base, self.n = base, n + times * per

    def __call__(self, ins, apart=None):
        ins.then_inc(self.sem, 1)
        self.n += 1
        if apart:
            wait_apart(self.eng, self.sem, self.base + self.n, apart)
        else:
            self.eng.wait_ge(self.sem, self.base + self.n)


def build(nc, x, dct, tok_w, tok_b, tok_alpha, w_in, b_in, w_out, b_out, sincos, mask, ident_in,
          gate0_w, gate0_b, ffn0_w, tri0, l1_w, l1_wk, l1_b_beta, l1_wo, l1_rows, gate1_w, ffn1_w, earlier,
          route_rows, dest_in, empty_row, out):
    ctx = ExitStack()
    with ctx:
        def sb(name, shape):
            return ctx.enter_context(nc.sbuf_tensor(name, shape, F32))

        def sem(name):
            return ctx.enter_context(nc.semaphore(name))

        bank = [ctx.enter_context(nc.psum_tensor(f"bank{i}", [128, 512], F32)) for i in range(8)]

        Hs = sb("hidden", [P, TT, D])
        XN = sb("normed", [P, TT, RW])
        XT = sb("normed_T", [128, DC, B * N])
        ident = sb("ident", [128, 128])
        stage = sb("norm_stage", [P, 2, D])
        stats = sb("stats", [P, 2, 6])
        pair = sb("mean_var_pair", [P, 2, 2])
        mv = sb("mean_var", [P, TT, 2])
        sd = sb("std", [P, TT])
        rstd = sb("rstd", [P, TT])
        eps = sb("eps", [P, 1])
        alpha = sb("alpha", [P, 1])
        alpha_b = sb("alpha_b", [P, D])
        bout_rows = sb("bout_rows", [P, D])
        l1rows = sb("l1_rows", [P, 3, D])
        comb0 = sb("comb0", [P, TT, E0 + 1])
        half_shared = sb("shared_weight", [P, 1])
        gate_k = sb("gate_of_choice", [P, TOPK1, TT])
        pos_k = ctx.enter_context(nc.sbuf_tensor("row_of_choice", [P, TOPK1, TT], mybir.dt.uint32))
        place = ctx.enter_context(nc.sbuf_tensor("place", [128, 2, 2], mybir.dt.uint32))
        slot_expert = ctx.enter_context(nc.sbuf_tensor("slot_expert", [1, SLOTS], mybir.dt.int32))
        dest = ctx.enter_context(nc.sbuf_tensor("dest", [P, TOPK1, TT], mybir.dt.int32))
        xs_dram = nc.dram_tensor("expert_rows", [SLOTS * SR, RW], F32, kind="Internal").ap()
        ys_dram = nc.dram_tensor("expert_results", [TOPK1 * B * N, D], F32, kind="Internal").ap()
        g0w = sb("gate0_w", [128, DC, E0])
        g1w = sb("gate1_w", [128, DC, E1])
        g0b = sb("gate0_b", [P, E0])
        tri = sb("tri", [P, E0, E0])
        small = sb("small", [P, 6, TT * E0])

        AR = 22600
        arena = sb("arena", [128, AR])

        class Arena:
            def __init__(self):
                self.at = 0

            def take(self, parts, *dims):
                n = int(np.prod(dims))
                v = arena[0:parts, self.at:self.at + n]
                self.at += n
                assert self.at <= AR, self.at
                if len(dims) > 1:
                    names = "abcde"[:len(dims)]
                    v = v.rearrange(f"p ({' '.join(names)}) -> p {' '.join(names)}",
                                    **{k: d for k, d in zip(names[1:], dims[1:])})
                return v

        a = Arena()
        xbuf = a.take(128, 2, LC, N)
        cT = a.take(DK, L)
        tokw = a.take(DK, D)
        cw = a.take(128, LC, D)
        a = Arena()
        win = a.take(128, DC, HP * UW)
        wout = a.take(128, HP, D)
        cs = a.take(P, 2, TB, 32)
        mk = a.take(P, 3 * P)
        xtb = a.take(128, DC, N)
        qkb = a.take(P, 2, 4, 2, 32)
        mcos = a.take(P, 2, 4, 2, 32)
        msin = a.take(P, 2, 4, 2, 32)
        rk = a.take(P, 2, TB, 4, 64)
        vv = a.take(P, HP, TB, 2, HD + 1)
        qT = a.take(128, 2, 2, N)
        kT = a.take(128, 2, N)
        sm = a.take(P, 2, N)
        nmax = a.take(P, 2)
        pr = a.take(P, 2, 2, 6 * P)
        ptT = a.take(P, 2, N)
        rsum = a.take(P, 6)
        xn_flat = XN[:, :, :].rearrange("p t d -> p (t d)")
        bin_rows = xn_flat[:, 0:HP * UW]
        on = xn_flat[:, HP * UW:HP * UW + TB * D * 4].rearrange("p (t a h d) -> p t a h d", t=TB, a=HP, h=2)
        a = Arena()
        w13 = a.take(128, 2, 2, DC, F0)
        w2 = a.take(128, 2, D)
        hid = a.take(128, 2, GN)
        sg = a.take(128, 2, GN)
        cmpA = a.take(P, TT, E0, E0)
        cmpB = a.take(P, TT, E0, E0)
        a = Arena()
        l1w = a.take(128, DC, 4, D)
        lraw = a.take(128, DC, 2 * D + H1)
        lwo = a.take(128, DC, D)
        hsum = a.take(128, DC, 2, H1)
        bbeta = a.take(128, DC)
        vsb = a.take(128, 2, N)
        bet = a.take(128, 2, N)
        uu = a.take(128, 2, N)
        ss = a.take(128, 2, N)
        oo = a.take(128, 2, DC, N)
        ztmp = a.take(P, 2, D)
        a = Arena()
        earl = a.take(P, P)
        ones = a.take(P, P)
        rows1 = a.take(P, TT * E1 + 12 + SLOTS + E1)
        c8a = a.take(P, TT, E1, E1)
        c8b = a.take(P, TT, E1, E1)
        rank1 = a.take(P, TT, E1)
        sel = a.take(P, 3, TT, E1)
        tot = a.take(P, TT * E1)
        incl = a.take(P, TT * E1)
        nsl = a.take(P, E1)
        send = a.take(P, E1)
        sbase = a.take(P, E1)
        ncmp = a.take(P, E1, 12)
        scmp = a.take(1, SLOTS, E1)
        sexp = a.take(1, SLOTS)
        posf = a.take(P, TT)
        prod = a.take(P, TT, E1)
        a = Arena()
        fw = a.take(128, 2, 3 * DC * F1)
        fhid = a.take(128, 2, FC1, GN)
        fsg = a.take(128, 2, GN)
        a = Arena()
        a.take(128, 2, 3 * DC * F1)
        shid = a.take(128, 2, FC1, SR)
        ssg = a.take(128, 2, SR)
        xs = a.take(128, 2, 2, RW)
        xsT = a.take(128, 2, DC, SR)
        ysb = a.take(128, 2, 2, D)
        a = Arena()
        back = a.take(P, TOPK1, TT, D)
        oT1 = sb("heads_T", [128, HP, N])

        S = {}

        def s(name):
            if name not in S:
                S[name] = sem(name)
            return S[name]

        phase_done = s("phase_done")

        block = ctx.enter_context(nc.Block())

        def barrier(eng, k):
            eng.drain().then_inc(phase_done, 1)
            eng.wait_ge(phase_done, 5 * k)

        def tile_of(buf, g):
            return buf[:, bass.ds(g, 1), 0:D].rearrange("p o d -> p (o d)")

        @block.sync
        def _(sp):
            for name, n in PRIMED.items():
                sp.sem_inc(s(name), n)
            sp.dma_start(cT, dct).then_inc(s("load_tok"), 16)
            sp.dma_start(tokw, tok_w).then_inc(s("load_tok"), 16)
            sp.dma_start(ident[:, :], ident_in).then_inc(s("load_tok"), 16)
            sp.dma_start(alpha[:, :], tok_alpha.partition_broadcast(P)).then_inc(s("load_tok"), 16)
            sp.dma_start(alpha_b[:, :], tok_b.partition_broadcast(P)).then_inc(s("load_tok"), 16)
            sp.dma_start(bout_rows[:, :], b_out.partition_broadcast(P)).then_inc(s("load_rows"), 16)
            sp.dma_start(l1rows[:, :, :], l1_rows.partition_broadcast(P)).then_inc(s("load_rows"), 16)
            sp.dma_start(g0b[:, :], gate0_b.partition_broadcast(P)).then_inc(s("load_rows"), 16)
            sp.dma_start(tri[:, :, :], tri0.partition_broadcast(P)).then_inc(s("load_rows"), 16)
            sp.dma_start(g0w[:, :, :], gate0_w).then_inc(s("load_rows"), 16)
            sp.dma_start(g1w[:, :, :], gate1_w).then_inc(s("load_rows"), 16)
            sp.dma_start(dest[:, :, :], dest_in).then_inc(s("load_rows"), 16)
            sp.dma_start(xs_dram, empty_row.partition_broadcast(SLOTS * SR)).then_inc(s("slots_empty"), 16)
            with sp.Fori(0, B // 2) as bb:
                for j in range(2):
                    sp.wait_ge(s("x_free"), 2 * bb + j + 1)
                    sp.dma_start(xbuf[:, j], x[bass.ds(2 * bb + j, 1)].rearrange("o (c p) n -> p (o c) n", p=128))\
                        .then_inc(s(f"x_ready{j}"), 16)
            barrier(sp, 1)
            sp.dma_start(win, w_in).then_inc(s("load_attn"), 16)
            sp.dma_start(bin_rows, b_in.partition_broadcast(P)).then_inc(s("load_attn"), 16)
            sp.dma_start(wout, w_out).then_inc(s("load_attn"), 16)
            sp.dma_start(cs, sincos).then_inc(s("load_attn"), 16)
            sp.dma_start(mk, mask).then_inc(s("load_attn"), 16)
            barrier(sp, 2)
            barrier(sp, 3)
            for i in range(2):
                sp.dma_start(w13[:, i], ffn0_w[i, :, 0:4 * F0]).then_inc(s(f"w0_ready{i}"), 16)
                sp.dma_start(w2[:, i], ffn0_w[i, :, 4 * F0:4 * F0 + D]).then_inc(s(f"w0_ready{i}"), 16)
            with sp.Fori(1, E0 // 2) as ee:
                for i in range(2):
                    sp.wait_ge(s("y0_ready"), (2 * ee + i - 1) * 2 * NG)
                    sp.dma_start(w13[:, i], ffn0_w[bass.ds(2 * ee + i, 1), :, 0:4 * F0].rearrange("o p n -> p (o n)"))\
                        .then_inc(s(f"w0_ready{i}"), 16)
                    sp.dma_start(w2[:, i], ffn0_w[bass.ds(2 * ee + i, 1), :, 4 * F0:4 * F0 + D].rearrange("o p n -> p (o n)"))\
                        .then_inc(s(f"w0_ready{i}"), 16)
            sp.wait_ge(s("y0_ready"), (E0 - 1) * 2 * NG)
            sp.dma_start(w13[:, 0], ffn0_w[E0, :, 0:4 * F0]).then_inc(s("w0_ready0"), 16)
            sp.dma_start(w2[:, 0], ffn0_w[E0, :, 4 * F0:4 * F0 + D]).then_inc(s("w0_ready0"), 16)
            barrier(sp, 4)
            sp.dma_start(lraw, l1_w).then_inc(s("load_l1"), 16)
            sp.dma_start(lwo, l1_wo).then_inc(s("load_l1"), 16)
            sp.dma_start(l1w[:, :, 0, :], l1_wk).then_inc(s("load_l1"), 16)
            sp.dma_start(bbeta, l1_b_beta).then_inc(s("load_l1"), 16)
            barrier(sp, 5)
            barrier(sp, 6)
            sp.dma_start(earl, earlier).then_inc(s("load_route"), 16)
            sp.dma_start(rows1, route_rows.partition_broadcast(P)).then_inc(s("load_route"), 16)
            barrier(sp, 7)
            sp.dma_start(fw[:, 1], ffn1_w[E1]).then_inc(s("w1_shared"), 16)
            def slot_weights(slot, i):
                e = sp.value_load(slot_expert[0:1, bass.ds(slot, 1)], min_val=0, max_val=E1 - 1)
                sp.dma_start(fw[:, i], ffn1_w[bass.ds(e, 1)].rearrange("o p n -> p (o n)"))\
                    .then_inc(s(f"w1_ready{i}"), 16)

            def slot_rows(slot, i):
                sp.dma_start(xs[:, i], xs_dram[bass.ds(slot * SR, SR), :].rearrange("(a p) n -> p a n", p=128))\
                    .then_inc(s(f"xs_ready{i}"), 16)

            slot_weights(0, 0)
            sp.wait_ge(s("rows_sent"), 16 * TOPK1 * TT)
            barrier(sp, 8)
            slot_rows(0, 0)
            slot_rows(1, 1)
            slot_weights(1, 1)
            with sp.Fori(0, (SLOTS - 3) // 2) as ss_:
                for i in range(2):
                    slot = 2 * ss_ + (2 + i)
                    sp.wait_ge(s("slot_turned"), slot - 1)
                    sp.wait_ge(s("place_ready"), slot - 1)
                    slot_rows(slot, i)
                    sp.wait_ge(s("slot_out"), slot - 1)
                    slot_weights(slot, i)
            sp.wait_ge(s("slot_turned"), SLOTS - 2)
            sp.wait_ge(s("place_ready"), SLOTS - 2)
            slot_rows(SLOTS - 1, 0)
            sp.wait_ge(s("slot_out"), SLOTS - 2)
            slot_weights(SLOTS - 1, 0)
            for i in range(2):
                n = (SLOTS + 1 - i) // 2
                for a_ in range(2):
                    sp.wait_ge(s(f"y_sent{i}{a_}"), 16 * n)
            barrier(sp, 9)
            yv = ys_dram.rearrange("(k t p) d -> p k t d", k=TOPK1, p=P)
            for q in range(4):
                for k in range(TOPK1):
                    sp.dma_start(back[:, k, q * 6:(q + 1) * 6, :], yv[:, k, q * 6:(q + 1) * 6, :])\
                        .then_inc(s(f"back{q}"), 16)
            ov = out.rearrange("(t p) d -> p t d", p=P)
            for q in range(4):
                sp.wait_ge(s("summed"), q + 1)
                sp.dma_start(ov[:, q * 6:(q + 1) * 6, :], Hs[:, q * 6:(q + 1) * 6, :]).then_inc(s("stored"), 16)
            sp.wait_ge(s("stored"), 64)
        @block.tensor
        def _(pe):
            def transpose_normed(k):
                with pe.Fori(0, TT // 2) as tt:
                    for i in range(2):
                        g = k * TT + 2 * tt + i
                        pe.wait_ge(s("stage_ready"), g + 1)
                        pe.wait_ge(s("xt_ready"), g + 1)
                        for c in range(DC):
                            m = pe.transpose(bank[4 + i][:, c * P:(c + 1) * P], stage[:, i, c * 128:(c + 1) * 128],
                                             ident[0:P, 0:P])
                        m.then_inc(s("turned"), 1)

            def gate_scores(w, e, sem_name):
                for t in range(TT):
                    for c in range(DC):
                        m = pe.matmul(bank[0][0:P, t * e:(t + 1) * e], XT[:, c, t * P:(t + 1) * P], w[:, c, :],
                                      start=(c == 0), stop=(c == DC - 1))
                m.then_inc(s(sem_name), 1)

            pe.wait_ge(s("load_tok"), 80)
            for c in range(LC):
                m = pe.matmul(bank[c // 2][:, (c % 2) * D:(c % 2 + 1) * D], cT[:, c * 128:(c + 1) * 128], tokw,
                              start=True, stop=True)
            m.then_inc(s("cw_made"), 1)
            pe.wait_ge(s("cw_ready"), 1)
            with pe.Fori(0, B // 2) as bb:
                for j in range(2):
                    pe.wait_ge(s(f"x_ready{j}"), 16 * bb + 16)
                    for t in range(TB):
                        i = j * TB + t
                        pe.wait_ge(s("tok_free"), 6 * bb + i + 1)
                        for c in range(LC):
                            m = pe.matmul(bank[i % 2][0:P, 0:D], xbuf[:, j, c, t * P:(t + 1) * P], cw[:, c, :],
                                          start=(c == 0), stop=(c == LC - 1))
                        m.then_inc(s("tok_made"), 1)
                    pe.drain().then_inc(s("x_free"), 1)
            barrier(pe, 1)
            transpose_normed(0)
            barrier(pe, 2)

            pe.wait_ge(s("load_attn"), 80)

            def project(b, hp, par, t):
                n = (b * HP + hp) * TB + t
                pe.wait_ge(s("pj_read"), n + 1)
                for c in range(DC):
                    m = pe.matmul(bank[(par + t) % 2][0:P, 0:UW], xtb[:, c, t * P:(t + 1) * P],
                                  win[:, c, bass.ds(hp * UW, UW)], start=(c == 0), stop=(c == DC - 1))
                m.then_inc(s("pj_made"), 1)

            def turn_qk(b, hp, par):
                u = b * HP + hp
                pe.wait_ge(s("rope_ready"), (u + 1) * TB + 2)
                for k in range(2):
                    for t in range(TB):
                        m = pe.transpose(bank[2 + k][:, t * P:(t + 1) * P],
                                         rk[:, par, t, 2 * k:2 * k + 2, :].rearrange("p a b -> p (a b)"), ident[0:P, 0:P])
                m.then_inc(s("qk_turned"), 1)

            def scores(b, hp, par, g):
                n = (b * HP + hp) * 6 + g
                h, qt = g // TB, g % TB
                pe.wait_ge(s("qkT_ready"), b * HP + hp + 1)
                pe.wait_ge(s("masked"), n + 1)
                pe.matmul(bank[4 + g % 2][0:P, 0:(qt + 1) * P], qT[:, par, h, qt * P:(qt + 1) * P],
                          kT[:, par, 0:(qt + 1) * P], start=True, stop=True).then_inc(s("scored"), 1)

            def turn_probs(b, hp, par, g):
                n = (b * HP + hp) * 6 + g
                h, qt = g // TB, g % TB
                pe.wait_ge(s("exped"), n + 3)
                pe.wait_ge(s("ptT_ready"), n + 1)
                for j in range(qt + 1):
                    o = (0, P, 3 * P)[qt] + j * P
                    m = pe.transpose(bank[6][0:P, j * P:(j + 1) * P], pr[:, par, h, o:o + P], ident[0:P, 0:P])
                m.then_inc(s("p_turned"), 1)

            def weigh(b, hp, par, g):
                u = b * HP + hp
                h, qt = g // TB, g % TB
                if g == 0:
                    pe.wait_ge(s("o_normed"), u + 1)
                pe.wait_ge(s("ptT_ready"), u * 6 + g + 2)
                for j in range(qt + 1):
                    m = pe.matmul(bank[7][0:P, g * (HD + 1):(g + 1) * (HD + 1)], ptT[:, g % 2, j * P:(j + 1) * P],
                                  vv[:, bass.ds(hp, 1), j, h, :].rearrange("p o d -> p (o d)"),
                                  start=(j == 0), stop=(j == qt))
                if g == 5:
                    m.then_inc(s("weighed"), 1)

            with pe.Fori(0, B) as b:
                pe.wait_ge(s("xtb_ready"), b + 1)
                for t in range(TB):
                    project(b, 0, 0, t)
                turn_qk(b, 0, 0)

                def step(hp, par, before, after):
                    for g in range(6):
                        scores(b, hp, par, g)
                        if after and g % 2 == 0:
                            project(b, hp + 1, 1 - par, g // 2)
                        if before:
                            turn_probs(b, hp - 1, 1 - par, g)
                            if g >= 1:
                                weigh(b, hp - 1, 1 - par, g - 1)
                    if before:
                        weigh(b, hp - 1, 1 - par, 5)
                    if after:
                        turn_qk(b, hp + 1, 1 - par)

                step(0, 0, False, True)
                with pe.Fori(0, HP // 2 - 1) as hh:
                    for i in range(2):
                        step(2 * hh + (1 + i), (1 + i) % 2, True, True)
                step(HP - 1, 1, True, False)
                for g in range(6):
                    turn_probs(b, HP - 1, 1, g)
                    if g >= 1:
                        weigh(b, HP - 1, 1, g - 1)
                weigh(b, HP - 1, 1, 5)
                pe.wait_ge(s("o_normed"), b * HP + HP + 1)
                for hp in range(HP):
                    pe.wait_ge(s("oT_ready"), b * HP + hp + 1)
                    for t in range(TB):
                        m = pe.transpose(bank[2 + hp % 2][:, t * P:(t + 1) * P],
                                         on[:, t, hp].rearrange("p a b -> p (a b)"), ident[0:P, 0:P])
                    m.then_inc(s("o_turned"), 1)
                pe.wait_ge(s("oT_ready"), b * HP + HP + 2)
                pe.wait_ge(s("masked"), (b + 1) * HP * 6 + 2)
                for t in range(TB):
                    for hp in range(HP):
                        m = pe.matmul(bank[(4, 5, 7)[t]][0:P, 0:D], oT1[:, hp, t * P:(t + 1) * P], wout[:, hp, :],
                                      start=(hp == 0), stop=(hp == HP - 1))
                    m.then_inc(s("att_made"), 1)
                pe.wait_ge(s("att_added"), TB * b + TB)
            barrier(pe, 3)

            def feed_forward(k, experts, fc, e, i, w1_at, w3_at, w2_at, hidden):
                with pe.Fori(0, NG // 2) as gg:
                    for j in range(2):
                        for f in range(fc):
                            n = ((e * NG) + 2 * gg + j) * fc + f
                            r = f % 2 if fc > 1 else j
                            pe.wait_ge(s(f"hid{k}_ready"), n + 1)
                            for w, bk, name in ((w1_at, 0, "up"), (w3_at, 2, "side")):
                                for c in range(DC):
                                    m = pe.matmul(bank[bk + r][:, 0:GN], w(i, c, f),
                                                  XT[:, c, bass.ds((2 * gg + j) * GN, GN)],
                                                  start=(c == 0), stop=(c == DC - 1))
                                m.then_inc(s(f"{name}{k}_made"), 1)
                    for j in range(2):
                        m_ = e * NG + 2 * gg + j
                        pe.wait_ge(s(f"hid{k}_ready"), (m_ + 1) * fc + 2)
                        for h in range(GT // 2):
                            pe.wait_ge(s(f"y{k}_added"), 2 * m_ + h + 1)
                            for t in range(2):
                                for f in range(fc):
                                    m = pe.matmul(bank[4 + h][0:P, t * D:(t + 1) * D],
                                                  hidden(j, f)[:, (2 * h + t) * P:(2 * h + t + 1) * P], w2_at(i, f),
                                                  start=(f == 0), stop=(f == fc - 1))
                            m.then_inc(s(f"y{k}_ready"), 1)

            transpose_normed(1)
            pe.wait_ge(s("xt_ready"), 2 * TT + 2)
            pe.wait_ge(s("load_rows"), 112)
            gate_scores(g0w, E0, "gate0_made")

            def w0_1(i, c, f):
                return w13[:, i, 0, c, :]

            def w0_3(i, c, f):
                return w13[:, i, 1, c, :]

            def w0_2(i, f):
                return w2[:, i, :]

            def hid0(j, f):
                return hid[:, j, :]

            pe.wait_ge(s("gate0_sig"), 1)
            with pe.Fori(0, E0 // 2) as ee:
                for i in range(2):
                    wait_apart(pe, s(f"w0_ready{i}"), 32 * ee + 32, s("unused"))
                    feed_forward(0, E0, 1, 2 * ee + i, i, w0_1, w0_3, w0_2, hid0)
            pe.wait_ge(s("w0_ready0"), 32 * (E0 // 2) + 32)
            feed_forward(0, E0, 1, E0, 0, w0_1, w0_3, w0_2, hid0)
            barrier(pe, 4)

            transpose_normed(2)
            barrier(pe, 5)
            pe.wait_ge(s("l1w_ready"), 1)
            with pe.Fori(0, B) as b:
                for c in range(DC):
                    for q in range(4):
                        pe.wait_ge(s(("u_made", "vs_ready", "beta_ready", "scan_out")[q]), DC * b + c + (2 if q == 0 else 1))
                        for kc in range(DC):
                            m = pe.matmul(bank[q][:, 0:N], l1w[:, kc, q, c * 128:(c + 1) * 128],
                                          XT[:, kc, bass.ds(b * N, N)], start=(kc == 0), stop=(kc == DC - 1))
                        m.then_inc(s(f"l1_made{q}"), 1)
                pe.wait_ge(s("scan_out"), DC * b + DC + 1)
                for t in range(TB):
                    pe.wait_ge(s("l1_added"), TB * b + t + 1)
                    for c in range(DC):
                        m = pe.matmul(bank[4 + t][0:P, 0:D], oo[:, 0, c, t * P:(t + 1) * P], lwo[:, c, :],
                                      start=(c == 0), stop=(c == DC - 1))
                    m.then_inc(s("l1_out"), 1)
            barrier(pe, 6)
            transpose_normed(3)
            pe.wait_ge(s("xt_ready"), 4 * TT + 2)
            gate_scores(g1w, E1, "gate1_made")
            pe.wait_ge(s("load_route"), 32)
            pe.wait_ge(s("chosen"), 1)
            pe.matmul(bank[1][0:P, 0:TT * E1], earl, sel[:, 2].rearrange("p t e -> p (t e)"), start=True, stop=True)
            pe.matmul(bank[2][0:P, 0:TT * E1], ones, sel[:, 2].rearrange("p t e -> p (t e)"), start=True, stop=True)\
                .then_inc(s("counted"), 1)
            barrier(pe, 7)

            fwv = fw.rearrange("p i (w n) -> p i w n", w=3)
            f13 = fwv[:, :, 0:2, :].rearrange("p i w (c n) -> p i w c n", c=DC)
            f2 = fwv[:, :, 2, :].rearrange("p i (f n) -> p i f n", f=FC1)

            def w1_1(i, c, f):
                return f13[:, i, 0, c, f * 128:(f + 1) * 128]

            def w1_3(i, c, f):
                return f13[:, i, 1, c, f * 128:(f + 1) * 128]

            def w1_2(i, f):
                return f2[:, i, f, :]

            def hid1(j, f):
                return fhid[:, j, f, :]

            pe.wait_ge(s("w1_shared"), 16)
            feed_forward(1, 0, FC1, 0, 1, w1_1, w1_3, w1_2, hid1)
            barrier(pe, 8)

            def turn_rows(slot, i):
                pe.wait_ge(s(f"xs_ready{i}"), slot * 8 + (16 - 8 * i))
                pe.wait_ge(s("xsT_ready"), slot + 1)
                for c in range(DC):
                    for a_ in range(2):
                        m = pe.transpose(bank[2 + i][:, (2 * c + a_) * 128:(2 * c + a_ + 1) * 128],
                                         xs[:, i, a_, c * 128:(c + 1) * 128], ident[:, :])
                m.then_inc(s("slot_turned"), 1)

            def slot_hidden(slot, i):
                pe.wait_ge(s(f"w1_ready{i}"), slot * 8 + (16 - 8 * i))
                pe.wait_ge(s("xsT_ready"), slot + 3)
                for f in range(FC1):
                    pe.wait_ge(s("shid_ready"), slot * FC1 + f + 1)
                    for q, w in enumerate((w1_1, w1_3)):
                        for c in range(DC):
                            m = pe.matmul(bank[f % 2][:, q * SR:(q + 1) * SR], w(i, c, f), xsT[:, i, c, :],
                                          start=(c == 0), stop=(c == DC - 1))
                    m.then_inc(s("slot_up"), 1)

            def slot_result(slot, i):
                pe.wait_ge(s("shid_ready"), (slot + 1) * FC1 + 2)
                pe.wait_ge(s("ysb_ready"), 2 * slot + 1)
                for a_ in range(2):
                    for f in range(FC1):
                        m = pe.matmul(bank[4 + 2 * i + a_][:, 0:D], shid[:, i, f, a_ * 128:(a_ + 1) * 128], w1_2(i, f),
                                      start=(f == 0), stop=(f == FC1 - 1))
                m.then_inc(s("slot_out"), 1)

            turn_rows(0, 0)
            with pe.Fori(0, (SLOTS - 1) // 2) as ss_:
                slot_hidden(2 * ss_, 0)
                turn_rows(2 * ss_ + 1, 1)
                slot_hidden(2 * ss_ + 1, 1)
                slot_result(2 * ss_, 0)
                turn_rows(2 * ss_ + 2, 0)
                slot_result(2 * ss_ + 1, 1)
            slot_hidden(SLOTS - 1, 0)
            slot_result(SLOTS - 1, 0)
            barrier(pe, 9)

        @block.scalar
        def _(act):
            def copy_turned(k):
                act.wait_ge(s("var_ready"), (k + 1) * (TT // 2))
                act.activation(sd[:, :], mv[:, :, 1], ACT.Sqrt, bias=eps[:, 0:1]).then_inc(s("sd_ready"), 1)
                with act.Fori(0, TT // 2) as tt:
                    for i in range(2):
                        act.wait_ge(s("turned"), k * TT + 2 * tt + i + 1)
                        act.activation(XT[:, :, bass.ds((2 * tt + i) * P, P)],
                                       bank[4 + i][:, 0:DC * P].rearrange("p (c n) -> p c n", c=DC),
                                       ACT.Copy).then_inc(s("xt_ready"), 1)

            act.wait_ge(s("eps_ready"), 1)
            barrier(act, 1)
            copy_turned(0)
            barrier(act, 2)

            def exps(b, hp, par, g):
                n = (b * HP + hp) * 6 + g
                h, qt = g // TB, g % TB
                w, o = (qt + 1) * P, (0, P, 3 * P)[qt]
                act.wait_ge(s("masked"), n + 3)
                act.activation(pr[:, par, h, o:o + w], sm[:, g % 2, 0:w], ACT.Exp, bias=nmax[:, g % 2:g % 2 + 1],
                               scale=-1.0).then_inc(s("exped"), 1)

            def copy_probs(b, hp, g):
                n = (b * HP + hp) * 6 + g
                w = (g % TB + 1) * P
                act.wait_ge(s("p_turned"), n + 1)
                act.activation(ptT[:, g % 2, 0:w], bank[6][0:P, 0:w], ACT.Copy).then_inc(s("ptT_ready"), 1)

            with act.Fori(0, B) as b:
                def step(hp, par, before):
                    for g in range(6):
                        exps(b, hp, par, g)
                        if before:
                            copy_probs(b, hp - 1, g)

                step(0, 0, False)
                with act.Fori(0, HP // 2 - 1) as hh:
                    for i in range(2):
                        step(2 * hh + (1 + i), (1 + i) % 2, True)
                step(HP - 1, 1, True)
                for g in range(6):
                    copy_probs(b, HP - 1, g)
                for hp in range(HP):
                    act.wait_ge(s("o_turned"), b * HP + hp + 1)
                    act.activation(oT1[:, hp, :], bank[2 + hp % 2][:, 0:N], ACT.Copy).then_inc(s("oT_ready"), 1)
            barrier(act, 3)

            def silus(k, fc, e, sgv):
                with act.Fori(0, NG // 2) as gg:
                    for j in range(2):
                        for f in range(fc):
                            n = (e * NG + 2 * gg + j) * fc + f
                            r = f % 2 if fc > 1 else j
                            act.wait_ge(s(f"up{k}_made"), n + 1)
                            act.wait_ge(s(f"hid{k}_ready"), n + 1)
                            act.activation(sgv[:, r, :], bank[r][:, 0:GN], ACT.Silu).then_inc(s(f"silu{k}"), 1)

            copy_turned(1)
            act.wait_ge(s("gate0_made"), 1)
            act.activation(small[:, 0, :], bank[0][0:P, 0:TT * E0], ACT.Sigmoid).then_inc(s("gate0_sig"), 1)
            with act.Fori(0, E0 // 2) as ee:
                for i in range(2):
                    silus(0, 1, 2 * ee + i, sg)
            silus(0, 1, E0, sg)
            barrier(act, 4)
            copy_turned(2)
            barrier(act, 5)
            with act.Fori(0, B) as b:
                for c in range(DC):
                    act.wait_ge(s("l1_made1"), DC * b + c + 1)
                    act.wait_ge(s("u_made"), DC * b + c + 1)
                    act.activation(vsb[:, c, :], bank[1][:, 0:N], ACT.Copy).then_inc(s("vs_ready"), 1)
                    act.wait_ge(s("l1_made2"), DC * b + c + 1)
                    act.wait_ge(s("scanned"), DC * b + c + 1)
                    act.activation(bet[:, c, :], bank[2][:, 0:N], ACT.Sigmoid, bias=bbeta[:, c:c + 1])\
                        .then_inc(s("beta_ready"), 1)
            barrier(act, 6)
            act.wait_ge(s("var2_ready"), TT // 2)
            act.activation(sd[:, :], mv[:, :, 1], ACT.Sqrt, bias=eps[:, 0:1]).then_inc(s("sd2_ready"), 1)
            copy_turned(3)
            act.wait_ge(s("gate1_made"), 1)
            act.wait_ge(s("gate1_max"), 1)
            act.activation(small[:, 1, 0:TT * E1], small[:, 0, 0:TT * E1], ACT.Exp).then_inc(s("gate1_exp"), 1)
            barrier(act, 7)
            silus(1, FC1, 0, fsg)
            barrier(act, 8)

            def copy_rows(slot, i):
                act.wait_ge(s("slot_turned"), slot + 1)
                act.activation(xsT[:, i].rearrange("p c n -> p (c n)"), bank[2 + i][:, :], ACT.Copy)\
                    .then_inc(s("xsT_ready"), 1)

            def slot_silu(slot, i):
                for f in range(FC1):
                    act.wait_ge(s("slot_up"), slot * FC1 + f + 1)
                    act.activation(ssg[:, f % 2, :], bank[f % 2][:, 0:SR], ACT.Silu).then_inc(s("slot_silu"), 1)

            def copy_results(slot, i):
                act.wait_ge(s("slot_out"), slot + 1)
                act.wait_ge(s("place_ready"), slot + 1)
                for a_ in range(2):
                    act.activation(ysb[:, i, a_, :], bank[4 + 2 * i + a_][:, 0:D], ACT.Copy).then_inc(s("ysb_ready"), 1)

            copy_rows(0, 0)
            with act.Fori(0, (SLOTS - 1) // 2) as ss_:
                slot_silu(2 * ss_, 0)
                copy_rows(2 * ss_ + 1, 1)
                slot_silu(2 * ss_ + 1, 1)
                copy_results(2 * ss_, 0)
                copy_rows(2 * ss_ + 2, 0)
                copy_results(2 * ss_ + 1, 1)
            slot_silu(SLOTS - 1, 0)
            copy_results(SLOTS - 1, 0)
            barrier(act, 9)

        @block.gpsimd
        def _(pool):
            chain = Count(pool, s("pool_step"))
            pool.memset(eps[:, :], EPS).then_inc(s("eps_ready"), 1)
            barrier(pool, 1)
            barrier(pool, 2)
            pool.wait_ge(s("load_rows"), 112)
            pool.memset(qT[:, :, :, :], 0.0).then_inc(s("q_zero"), 1)
            pool.memset(vv[:, :, :, :, HD:HD + 1], 1.0).then_inc(s("q_zero"), 1)

            def rope(b, hp, par):
                for t in range(TB):
                    n = (b * HP + hp) * TB + t
                    r = (par + t) % 2
                    pool.wait_ge(s("roped"), n + 1)
                    pool.tensor_tensor(rk[:, par, t, :, 0:32], mcos[:, r, :, 1, :], msin[:, r, :, 0, :], ALU.add)
                    pool.tensor_tensor(rk[:, par, t, :, 32:64], mcos[:, r, :, 0, :], msin[:, r, :, 1, :],
                                       ALU.subtract).then_inc(s("rope_ready"), 1)

            with pool.Fori(0, B) as b:
                pool.wait_ge(s("pj_read"), b * HP * TB + 2)
                pool.tensor_copy(xtb, XT[:, :, bass.ds(b * N, N)]).then_inc(s("xtb_ready"), 1)
                for t in range(TB):
                    ins = pool.tensor_tensor(Hs[:, bass.ds(b * TB + t, 1), :].rearrange("p o d -> p (o d)"),
                                             Hs[:, bass.ds(b * TB + t, 1), :].rearrange("p o d -> p (o d)"),
                                             bout_rows[:, :], ALU.add)
                ins.then_inc(s("bout_added"), 1)
                rope(b, 0, 0)
                rope(b, 1, 1)
                with pool.Fori(0, HP // 2 - 1) as hh:
                    for i in range(2):
                        rope(b, 2 * hh + (2 + i), i)
            barrier(pool, 3)
            barrier(pool, 4)
            with pool.Fori(0, TT // 2) as tt:
                for i in range(2):
                    pool.wait_ge(s("stage_ready"), 2 * TT + 2 * tt + i + 1)
                    pool.tensor_copy(tile_of(XN, 2 * tt + i), stage[:, i, :])\
                        .then_inc(s("stage_copied"), 1)
            barrier(pool, 5)
            barrier(pool, 6)
            pool.memset(ones, 1.0).then_inc(s("ones_ready"), 1)
            with pool.Fori(0, TT // 2) as tt:
                for i in range(2):
                    pool.wait_ge(s("stage_ready"), 3 * TT + 2 * tt + i + 1)
                    pool.tensor_copy(tile_of(XN, 2 * tt + i), stage[:, i, :]).then_inc(s("stage_copied"), 1)
            barrier(pool, 7)
            pool.wait_ge(s("slots_empty"), 16)
            for k in range(TOPK1):
                if k:
                    pool.wait_ge(s("rows_sent"), 16 * k * TT)
                pool.tensor_copy(XN[:, :, D].bitcast(mybir.dt.int32), dest[:, k, :]).then_inc(s("dest_ready"), 1)
                pool.wait_ge(s("dest_ready"), k + 1)
                for t in range(TT):
                    pool.indirect_dma_start(out=xs_dram, out_offset=bass.IndirectOffsetOnAxis(ap=pos_k[:, k, t:t + 1], axis=0),
                                            in_=XN[:, t, :], in_offset=None).then_inc(s("rows_sent"), 16)
            barrier(pool, 8)

            def send_results(slot, i, first=False):
                pool.wait_ge(s(f"xs_ready{i}"), slot * 8 + (16 - 8 * i))
                if not first:
                    for a_ in range(2):
                        pool.wait_ge(s(f"y_sent{i}{a_}"), slot * 8 - 8 * i)
                pool.sem_inc(s("unused"), 1)
                pool.tensor_copy(place[:, i, :], xs[:, i, :, D].bitcast(mybir.dt.uint32)).then_inc(s("place_ready"), 1)
                pool.wait_ge(s("place_ready"), slot + 1)
                for a_ in range(2):
                    pool.wait_ge(s("ysb_ready"), 2 * slot + a_ + 5)
                    pool.sem_inc(s("unused"), 1)
                    pool.indirect_dma_start(out=ys_dram,
                                            out_offset=bass.IndirectOffsetOnAxis(
                                                ap=place[:, i, a_:a_ + 1], axis=0),
                                            in_=ysb[:, i, a_, :], in_offset=None, bounds_check=TOPK1 * B * N - 1,
                                            oob_is_err=False).then_inc(s(f"y_sent{i}{a_}"), 16)

            for i in range(2):
                send_results(i, i, True)
            with pool.Fori(1, (SLOTS - 1) // 2) as ss_:
                send_results(2 * ss_, 0)
                send_results(2 * ss_ + 1, 1)
            send_results(SLOTS - 1, 0)
            barrier(pool, 9)

        @block.vector
        def _(v):
            chain = Count(v, s("dve_step"))

            def tile(buf, g):
                return tile_of(buf, g)

            def variances(src, sem_name):
                with v.Fori(0, TT // 2) as tt:
                    chain.enter(tt, 3)
                    for i in range(2):
                        st = v.bn_stats(stats[:, i, :], tile(src, 2 * tt + i))
                        if i == 0:
                            st.then_inc(s("dve_step"), 1)
                            chain.n += 1
                    chain(st, apart=s("unused"))
                    for i in range(2):
                        ag = v.bn_aggr(pair[:, i, :], stats[:, i, :])
                    chain(ag)
                    v.tensor_copy(mv[:, bass.ds(2 * tt, 2), :], pair[:, :, :]).then_inc(s(sem_name), 1)
                chain.leave(TT // 2, 3)

            def normalise(k, src, extra_wait=None, extra_base=0):
                variances(src, "var_ready")
                v.wait_ge(s("sd_ready"), k + 1)
                chain(v.reciprocal(rstd[:, :], sd[:, :]))
                with v.Fori(0, TT // 2) as tt:
                    for i in range(2):
                        g = 2 * tt + i
                        v.wait_ge(s("xt_ready"), k * TT + g + 1)
                        if extra_wait:
                            v.wait_ge(s(extra_wait), extra_base + g + 1)
                        v.tensor_scalar(stage[:, i, :], tile(src, g), mv[:, bass.ds(g, 1), 0], rstd[:, bass.ds(g, 1)],
                                        ALU.subtract, ALU.mult).then_inc(s("stage_ready"), 1)

            v.wait_ge(s("load_tok"), 80)
            v.wait_ge(s("cw_made"), 1)
            for h in range(2):
                cp = v.tensor_copy(cw[:, 2 * h:2 * h + 2, :].rearrange("p a b -> p (a b)"), bank[h][:, :])
            cp.then_inc(s("cw_ready"), 1)
            chain(v.tensor_scalar(alpha_b[:, :], alpha_b[:, :], alpha[:, 0:1], None, ALU.mult))
            with v.Fori(0, B // 2) as bb:
                for i in range(2 * TB):
                    g = 2 * TB * bb + i
                    v.wait_ge(s("tok_made"), g + 1)
                    v.scalar_tensor_tensor(tile(Hs, g), bank[i % 2][0:P, 0:D], alpha[:, 0:1], alpha_b[:, :],
                                           ALU.mult, ALU.add).then_inc(s("tok_free"), 1)
            v.wait_ge(s("tok_free"), TT + 2)
            barrier(v, 1)
            normalise(0, Hs)
            barrier(v, 2)

            v.wait_ge(s("load_attn"), 80)
            v.wait_ge(s("q_zero"), 2)

            def take_projection(b, hp, par, t):
                n = (b * HP + hp) * TB + t
                r = (par + t) % 2
                v.wait_ge(s("pj_made"), n + 1)
                v.tensor_tensor(vv[:, bass.ds(hp, 1), t, :, 0:HD].rearrange("p o h d -> p (o h) d"),
                                bank[r][0:P, 4 * HD:6 * HD].rearrange("p (h d) -> p h d", h=2),
                                bin_rows[:, bass.ds(hp * UW + 4 * HD, 2 * HD)].rearrange("p (h d) -> p h d", h=2),
                                ALU.add)
                v.tensor_tensor(qkb[:, r].rearrange("p a b c -> p (a b c)"), bank[r][0:P, 0:4 * HD],
                                bin_rows[:, bass.ds(hp * UW, 4 * HD)], ALU.add).then_inc(s("pj_read"), 1)
                v.wait_ge(s("pj_read"), n + 3)
                v.wait_ge(s("rope_ready"), n + 1)
                x8 = qkb[:, r].rearrange("p a b c -> p (a b) c")
                for k, m in ((0, mcos), (1, msin)):
                    ins = v.tensor_tensor(m[:, r].rearrange("p a b c -> p (a b) c"), x8,
                                          cs[:, k, t, :].unsqueeze(1).to_broadcast([P, 8, 32]), ALU.mult)
                ins.then_inc(s("roped"), 1)

            def take_qkT(b, hp, par):
                v.wait_ge(s("qk_turned"), b * HP + hp + 1)
                v.tensor_copy(qT[0:64, par, 0, :], bank[2][0:64, 0:N])
                v.tensor_copy(qT[64:128, par, 1, :], bank[2][64:128, 0:N])
                v.tensor_copy(kT[:, par, :], bank[3][:, 0:N]).then_inc(s("qkT_ready"), 1)

            def mask_scores(b, hp, g):
                n = (b * HP + hp) * 6 + g
                w = (g % TB + 1) * P
                v.wait_ge(s("exped"), n + 1)
                wait_apart(v, s("scored"), n + 1, s("unused"))
                v.tensor_tensor_reduce(sm[:, g % 2, 0:w], bank[4 + g % 2][0:P, 0:w], mk[:, 3 * P - w:3 * P], -SCALE, BIG,
                                       ALU.add, ALU.min, nmax[:, g % 2:g % 2 + 1]).then_inc(s("masked"), 1)

            def divide(b, hp):
                v.wait_ge(s("weighed"), b * HP + hp + 1)
                ob = bank[7][0:P, 0:6 * (HD + 1)].rearrange("p (g d) -> p g d", d=HD + 1)
                chain(v.reciprocal(rsum, ob[:, :, HD]))
                for h in range(2):
                    ins = v.tensor_tensor(on[:, :, bass.ds(hp, 1), h, :].rearrange("p t o d -> p t (o d)"),
                                          ob[:, h * TB:(h + 1) * TB, 0:HD],
                                          rsum[:, h * TB:(h + 1) * TB].unsqueeze(2).to_broadcast([P, TB, HD]), ALU.mult)
                ins.then_inc(s("o_normed"), 1)

            with v.Fori(0, B) as b:
                chain.enter(b, HP)
                for t in range(TB):
                    take_projection(b, 0, 0, t)
                take_qkT(b, 0, 0)

                def step(hp, par, before, after):
                    for g in range(6):
                        mask_scores(b, hp, g)
                        if after and g % 2 == 0:
                            take_projection(b, hp + 1, 1 - par, g // 2)
                    if after:
                        take_qkT(b, hp + 1, 1 - par)
                    if before:
                        divide(b, hp - 1)

                step(0, 0, False, True)
                with v.Fori(0, HP // 2 - 1) as hh:
                    chain.enter(hh, 2)
                    for i in range(2):
                        step(2 * hh + (1 + i), (1 + i) % 2, True, True)
                chain.leave(HP // 2 - 1, 2)
                step(HP - 1, 1, True, False)
                divide(b, HP - 1)
                v.wait_ge(s("bout_added"), b + 1)
                for t in range(TB):
                    v.wait_ge(s("att_made"), TB * b + t + 1)
                    v.tensor_tensor(tile(Hs, b * TB + t), bank[(4, 5, 7)[t]][0:P, 0:D], tile(Hs, b * TB + t), ALU.add)\
                        .then_inc(s("att_added"), 1)
            chain.leave(B, HP)
            barrier(v, 3)

            normalise(1, Hs)
            v.wait_ge(s("load_rows"), 112)

            def top(src, e, out_ap, keep_n, big_a, big_b, T):
                si = src.unsqueeze(3).to_broadcast([P, T, e, e])
                sj = src.unsqueeze(2).to_broadcast([P, T, e, e])
                tr = tri[:, 0:e, 0:e].unsqueeze(1).to_broadcast([P, T, e, e])
                chain(v.tensor_tensor(big_a, sj, si, ALU.is_equal))
                chain(v.tensor_tensor(big_a, big_a, tr, ALU.mult))
                chain(v.tensor_tensor(big_b, sj, si, ALU.is_gt))
                chain(v.tensor_tensor(big_a, big_a, big_b, ALU.add))
                chain(v.tensor_reduce(out_ap, big_a, AX.X, ALU.add))
                if keep_n is not None:
                    chain(v.tensor_scalar(out_ap, out_ap, float(keep_n), None, ALU.is_lt))

            def sm3(k, e):
                return small[:, k, 0:TT * e].rearrange("p (t e) -> p t e", e=e)

            v.wait_ge(s("gate0_sig"), 1)
            sig, sbias, gmax, keep, rank = (sm3(k, E0) for k in range(5))
            chain(v.tensor_tensor(sbias, sig, g0b[:, :].unsqueeze(1).to_broadcast([P, TT, E0]), ALU.add))
            s4 = sbias.rearrange("p t (g e) -> p (t g) e", g=4)
            gm = small[:, 2, 0:TT * 4]
            chain(v.tensor_reduce(gm, s4, AX.X, ALU.max))
            kp = small[:, 3, 0:TT * 4]
            ca = cmpA.rearrange("p a b c -> p (a b c)")[:, 0:TT * 16].rearrange("p (t i j) -> p t i j", i=4, j=4)
            cb = cmpB.rearrange("p a b c -> p (a b c)")[:, 0:TT * 16].rearrange("p (t i j) -> p t i j", i=4, j=4)
            top(gm.rearrange("p (t g) -> p t g", g=4), 4, kp.rearrange("p (t g) -> p t g", g=4), 2, ca, cb, TT)
            keep3 = kp.unsqueeze(2).to_broadcast([P, TT * 4, 4])
            off = small[:, 4, 0:TT * 4]
            chain(v.tensor_scalar(off, kp, BIG, BIG, ALU.mult, ALU.subtract))
            chain(v.tensor_tensor(s4, s4, keep3, ALU.mult))
            chain(v.tensor_tensor(s4, s4, off.unsqueeze(2).to_broadcast([P, TT * 4, 4]), ALU.add))
            rk5 = sm3(5, E0)
            top(sbias, E0, rk5, 4, cmpA, cmpB, TT)
            chain(v.tensor_tensor(comb0[:, :, 0:E0], rk5, sig, ALU.mult))
            chain(v.memset(comb0[:, :, E0:E0 + 1], 1.0))

            def experts(k, fc, e, sgv, hidden, gate):
                with v.Fori(0, NG // 2) as gg:
                    for j in range(2):
                        for f in range(fc):
                            n = (e * NG + 2 * gg + j) * fc + f
                            r = f % 2 if fc > 1 else j
                            v.wait_ge(s(f"silu{k}"), n + 1)
                            v.wait_ge(s(f"side{k}_made"), n + 1)
                            v.tensor_tensor(hidden(j, f), bank[2 + r][:, 0:GN], sgv[:, r, :], ALU.mult)\
                                .then_inc(s(f"hid{k}_ready"), 1)
                    for j in range(2):
                        m_ = e * NG + 2 * gg + j
                        for h in range(GT // 2):
                            v.wait_ge(s(f"y{k}_ready"), 2 * m_ + h + 1)
                            v.wait_ge(s(f"y{k}_added"), 2 * m_ + h + 1)
                            for t in range(2):
                                g = (2 * gg + j) * GT + 2 * h + t
                                ins = v.scalar_tensor_tensor(tile(Hs, g), bank[4 + h][0:P, t * D:(t + 1) * D],
                                                             gate(g), tile(Hs, g), ALU.mult, ALU.add)
                            ins.then_inc(s(f"y{k}_added"), 1)

            def hid0(j, f):
                return hid[:, j, :]

            with v.Fori(0, E0 // 2) as ee:
                for i in range(2):
                    experts(0, 1, 2 * ee + i, sg, hid0,
                            lambda g, e=2 * ee + i: comb0[:, bass.ds(g, 1), bass.ds(e, 1)].rearrange("p a b -> p (a b)"))
            experts(0, 1, E0, sg, hid0, lambda g: comb0[:, bass.ds(g, 1), E0])
            barrier(v, 4)

            normalise(2, Hs, "stage_copied")
            v.wait_ge(s("load_l1"), 64)
            lr = lraw
            for q in range(2):
                hs = v.tensor_reduce(hsum[:, :, q, :], lr[:, :, q * D:(q + 1) * D].rearrange("p c (h d) -> p c h d", d=D1),
                                     AX.X, ALU.add)
            chain(hs)
            for q, src in ((3, hsum[:, :, 0, :]), (1, hsum[:, :, 1, :]), (2, lr[:, :, 2 * D:2 * D + H1])):
                for c in range(DC):
                    cp = v.tensor_copy(l1w[:, c, q, :].rearrange("p (h d) -> p h d", d=D1),
                                       src[:, c, :].unsqueeze(2).to_broadcast([128, H1, D1]))
            cp.then_inc(s("l1w_ready"), 1)
            barrier(v, 5)
            with v.Fori(0, B) as b:
                for c in range(DC):
                    v.wait_ge(s("vs_ready"), DC * b + c + 2)
                    v.wait_ge(s("l1_made0"), DC * b + c + 1)
                    v.tensor_tensor(uu[:, c, :], bank[0][:, 0:N], vsb[:, c, :], ALU.mult).then_inc(s("u_made"), 1)
                    v.wait_ge(s("u_made"), DC * b + c + 3)
                    v.wait_ge(s("beta_ready"), DC * b + c + 2)
                    v.tensor_tensor_scan(ss[:, c, :], bet[:, c, :], uu[:, c, :], 0.0, ALU.mult, ALU.add)\
                        .then_inc(s("scanned"), 1)
                    v.wait_ge(s("scanned"), DC * b + c + 3)
                    v.wait_ge(s("l1_made3"), DC * b + c + 1)
                    v.tensor_tensor(oo[:, 0, c, :], bank[3][:, 0:N], ss[:, c, :], ALU.mult).then_inc(s("scan_out"), 1)
                for t in range(TB):
                    v.wait_ge(s("l1_out"), TB * b + t + 1)
                    v.tensor_tensor(ztmp[:, t % 2, :], bank[4 + t][0:P, 0:D], l1rows[:, 0, :], ALU.add)\
                        .then_inc(s("z_part"), 1)
                    v.wait_ge(s("z_part"), TB * b + t + 1)
                    v.tensor_tensor(tile(XN, b * TB + t), tile(XN, b * TB + t), ztmp[:, t % 2, :], ALU.add)\
                        .then_inc(s("l1_added"), 1)
            v.wait_ge(s("l1_added"), TT + 3)
            barrier(v, 6)
            variances(XN, "var2_ready")
            v.wait_ge(s("sd2_ready"), 1)
            chain(v.reciprocal(rstd[:, :], sd[:, :]))
            with v.Fori(0, TT // 2) as tt:
                chain.enter(tt, 8)
                for i in range(2):
                    g = 2 * tt + i
                    chain(v.tensor_scalar(tile(XN, g), tile(XN, g), mv[:, bass.ds(g, 1), 0], rstd[:, bass.ds(g, 1)],
                                          ALU.subtract, ALU.mult))
                    chain(v.tensor_tensor(tile(XN, g), tile(XN, g), l1rows[:, 1, :], ALU.mult))
                    chain(v.tensor_tensor(tile(XN, g), tile(XN, g), l1rows[:, 2, :], ALU.add))
                    chain(v.tensor_tensor(tile(Hs, g), tile(Hs, g), tile(XN, g), ALU.add))
            chain.leave(TT // 2, 8)
            normalise(3, Hs, "stage_copied", TT)
            v.wait_ge(s("gate1_made"), 1)
            lg = bank[0][0:P, 0:TT * E1].rearrange("p (t e) -> p t e", e=E1)
            mx = small[:, 2, 0:TT]
            a0, a1 = sm3(0, E1), sm3(1, E1)
            chain(v.tensor_reduce(mx, lg, AX.X, ALU.max))
            v.tensor_tensor(a0, lg, mx.unsqueeze(2).to_broadcast([P, TT, E1]), ALU.subtract).then_inc(s("gate1_max"), 1)
            v.wait_ge(s("gate1_exp"), 1)
            sume = small[:, 3, 0:TT]
            chain(v.tensor_reduce(sume, a1, AX.X, ALU.add))
            chain(v.reciprocal(sume, sume))
            chain(v.tensor_tensor(a1, a1, sume.unsqueeze(2).to_broadcast([P, TT, E1]), ALU.mult))
            top(a1, E1, rank1, None, c8a, c8b, TT)
            v.wait_ge(s("load_route"), 32)
            v.wait_ge(s("ones_ready"), 1)
            for k in range(TOPK1):
                v.tensor_scalar(sel[:, k], rank1, float(k), None, ALU.is_equal)
            v.tensor_scalar(sel[:, 2], rank1, float(TOPK1), None, ALU.is_lt).then_inc(s("chosen"), 1)
            v.wait_ge(s("chosen"), 1)
            resets = rows1[:, 0:TT * E1]
            full = rows1[:, TT * E1:TT * E1 + 12]
            slotno = rows1[:, TT * E1 + 12:TT * E1 + 12 + SLOTS]
            one8 = rows1[:, TT * E1 + 12 + SLOTS:]
            for k in range(TOPK1):
                chain(v.tensor_tensor(prod, sel[:, k], a1, ALU.mult))
                chain(v.tensor_reduce(gate_k[:, k, :], prod, AX.X, ALU.add))
            chain(v.tensor_scalar(gate_k[:, :, :], gate_k[:, :, :], 0.5, None, ALU.mult))
            v.wait_ge(s("counted"), 1)
            chain(v.tensor_copy(tot.rearrange("p (e t) -> p t e", e=E1),
                                bank[2][0:P, 0:TT * E1].rearrange("p (t e) -> p t e", e=E1)))
            chain(v.tensor_tensor_scan(incl, resets, tot, 0.0, ALU.mult, ALU.add))
            cnt = incl.rearrange("p (e t) -> p e t", e=E1)[:, :, TT - 1]
            chain(v.tensor_tensor(ncmp, cnt.unsqueeze(2).to_broadcast([P, E1, 12]),
                                  full.unsqueeze(1).to_broadcast([P, E1, 12]), ALU.is_gt))
            chain(v.tensor_reduce(nsl, ncmp, AX.X, ALU.add))
            chain(v.tensor_tensor_scan(send, one8, nsl, 0.0, ALU.mult, ALU.add))
            chain(v.tensor_tensor(sbase, send, nsl, ALU.subtract))
            chain(v.tensor_scalar(sbase, sbase, float(SR), None, ALU.mult))
            chain(v.tensor_tensor(scmp, send[0:1].unsqueeze(1).to_broadcast([1, SLOTS, E1]),
                                  slotno[0:1].unsqueeze(2).to_broadcast([1, SLOTS, E1]), ALU.is_le))
            chain(v.tensor_reduce(sexp, scmp, AX.X, ALU.add))
            chain(v.tensor_scalar(sexp, sexp, float(E1 - 1), None, ALU.min))
            chain(v.tensor_copy(slot_expert[:, :], sexp))
            chain(v.tensor_tensor(incl, incl, tot, ALU.subtract))
            i3 = incl.rearrange("p (e t) -> p e t", e=E1)
            chain(v.tensor_tensor(i3, i3, sbase.unsqueeze(2).to_broadcast([P, E1, TT]), ALU.add))
            chain(v.tensor_tensor(rank1, bank[1][0:P, 0:TT * E1].rearrange("p (t e) -> p t e", e=E1),
                                  incl.rearrange("p (e t) -> p t e", e=E1), ALU.add))
            for k in range(TOPK1):
                chain(v.tensor_tensor(prod, sel[:, k], rank1, ALU.mult))
                chain(v.tensor_reduce(posf, prod, AX.X, ALU.add))
                chain(v.tensor_copy(pos_k[:, k, :], posf))
            chain(v.memset(half_shared[:, :], 0.5 / E1))
            barrier(v, 7)

            def hid1(j, f):
                return fhid[:, j, f, :]

            experts(1, FC1, 0, fsg, hid1, lambda g: half_shared[:, 0:1])
            barrier(v, 8)

            def slot_units(slot, i):
                for f in range(FC1):
                    v.wait_ge(s("slot_silu"), slot * FC1 + f + 1)
                    v.tensor_tensor(shid[:, i, f, :], bank[f % 2][:, SR:2 * SR], ssg[:, f % 2, :], ALU.mult)\
                        .then_inc(s("shid_ready"), 1)

            with v.Fori(0, (SLOTS - 1) // 2) as ss_:
                slot_units(2 * ss_, 0)
                slot_units(2 * ss_ + 1, 1)
            slot_units(SLOTS - 1, 0)
            barrier(v, 9)
            for q in range(4):
                v.wait_ge(s(f"back{q}"), 32)
                for k in range(TOPK1):
                    for t in range(6 * q, 6 * q + 6):
                        ins = v.scalar_tensor_tensor(Hs[:, t, :], back[:, k, t, :], gate_k[:, k, t:t + 1], Hs[:, t, :],
                                                     ALU.mult, ALU.add)
                    chain(ins)
                v.sem_inc(s("summed"), 1)


def kernel(x, L0_tok_W, L0_tok_b, L0_tok_alpha, L0_attn_W_in, L0_attn_b_in, L0_attn_W_out, L0_attn_b_out,
           L0_ffn_gate_w, L0_ffn_gate_bias, L0_ffn_w1, L0_ffn_w2, L0_ffn_w3, L0_ffn_ws1, L0_ffn_ws2, L0_ffn_ws3,
           L1_attn_Wq, L1_attn_Wk, L1_attn_Wv, L1_attn_Wbeta, L1_attn_b_beta, L1_attn_Wo, L1_attn_b_o,
           L1_attn_ln_g, L1_attn_ln_b, L1_ffn_gate_W, L1_ffn_w1_e, L1_ffn_w3_e, L1_ffn_w2_e,
           L1_ffn_w1_s, L1_ffn_w3_s, L1_ffn_w2_s):
    import concourse.bacc as bacc
    from concourse.bass_utils import run_bass_kernel_spmd

    def chunks(w):
        w = np.asarray(w)
        w = w.reshape(*w.shape[:-2], -1, 128, w.shape[-1])
        return np.swapaxes(w, -3, -2)

    def flat(w, keep):
        return w.reshape(*w.shape[:keep], -1)

    l = np.arange(L)
    m = np.where(l % 2 == 0, l // 2, L // 2 + (L - 1 - l) // 2)
    dct = np.cos(2 * np.pi * ((np.arange(DK)[:, None] * m[None, :]) % L) / L).astype(np.float32)
    half = HD // 2
    theta = np.float32(10000.0) ** (np.arange(half, dtype=np.float32) / np.float32(half - 1))
    pos = np.arange(N, dtype=np.float32)[:, None] / theta[None, :]
    sincos = np.stack([np.cos(pos), np.sin(pos)]).astype(np.float32).reshape(2, TB, P, half).transpose(2, 0, 1, 3)
    mask = np.zeros((P, 3 * P), np.float32)
    mask[:, 2 * P:] = np.where(np.arange(P)[None, :] > np.arange(P)[:, None], MASKED, 0.0)
    before = (np.arange(E0)[None, :] < np.arange(E0)[:, None]).astype(np.float32)

    earlier = (np.arange(P)[:, None] < np.arange(P)[None, :]).astype(np.float32)
    route_rows = np.concatenate([np.tile(np.arange(TT) > 0, E1), np.arange(12) * SR, np.arange(SLOTS), np.ones(E1)])\
        .astype(np.float32)
    dest = np.arange(TOPK1 * B * N, dtype=np.int32).reshape(TOPK1, TT, P).transpose(2, 0, 1)
    empty = np.concatenate([np.zeros(D, np.int32), np.array([NOWHERE], np.int32)]).view(np.float32)

    heads = np.asarray(L0_attn_W_in).reshape(3, HP, 2 * HD, D).transpose(1, 0, 2, 3).reshape(HP * UW, D)
    head_bias = np.asarray(L0_attn_b_in).reshape(3, HP, 2 * HD).transpose(1, 0, 2).reshape(HP * UW)
    t = lambda w: np.swapaxes(np.asarray(w), -1, -2)
    ffn0 = np.concatenate([
        np.concatenate([flat(chunks(t(L0_ffn_w1)), 2), flat(chunks(t(L0_ffn_w3)), 2), t(L0_ffn_w2)], axis=2),
        np.concatenate([flat(chunks(t(L0_ffn_ws1)), 1), flat(chunks(t(L0_ffn_ws3)), 1), t(L0_ffn_ws2)], axis=1)[None]])
    side = lambda w: np.asarray(w).transpose(1, 0, 2).reshape(D, F1)
    ffn1 = np.concatenate([
        np.concatenate([flat(chunks(L1_ffn_w1_e), 2), flat(chunks(L1_ffn_w3_e), 2), flat(chunks(L1_ffn_w2_e), 2)], axis=2),
        np.concatenate([flat(chunks(side(L1_ffn_w1_s)), 1), flat(chunks(side(L1_ffn_w3_s)), 1),
                        flat(chunks(np.asarray(L1_ffn_w2_s).reshape(F1, D)), 1)], axis=1)[None]])
    arrays = {
        "x": np.asarray(x), "dct": dct, "tok_w": L0_tok_W, "tok_b": L0_tok_b, "tok_alpha": L0_tok_alpha,
        "w_in": chunks(t(heads)), "b_in": head_bias, "w_out": chunks(t(L0_attn_W_out)), "b_out": L0_attn_b_out,
        "sincos": sincos, "mask": mask, "ident_in": np.eye(128, dtype=np.float32),
        "gate0_w": chunks(t(L0_ffn_gate_w)), "gate0_b": L0_ffn_gate_bias, "ffn0_w": ffn0, "tri0": before,
        "l1_w": chunks(np.concatenate([np.asarray(L1_attn_Wq), np.asarray(L1_attn_Wv), np.asarray(L1_attn_Wbeta)], axis=1)),
        "l1_wk": chunks(L1_attn_Wk),
        "l1_b_beta": np.broadcast_to(np.asarray(L1_attn_b_beta)[:, None], (H1, D1)).reshape(DC, 128).T,
        "l1_wo": chunks(L1_attn_Wo),
        "l1_rows": np.stack([np.asarray(L1_attn_b_o), np.asarray(L1_attn_ln_g), np.asarray(L1_attn_ln_b)]),
        "gate1_w": chunks(t(L1_ffn_gate_W)), "ffn1_w": ffn1, "earlier": earlier, "route_rows": route_rows,
        "dest_in": dest, "empty_row": empty,
    }
    nc = bacc.Bacc("TRN2", target_bir_lowering=False, num_devices=1)
    arrays = {k + "_dram": np.ascontiguousarray(v) for k, v in arrays.items()}
    args = [nc.dram_tensor(k, v.shape, mybir.dt.from_np(v.dtype), kind="ExternalInput").ap() for k, v in arrays.items()]
    out = nc.dram_tensor("result_dram", [B * N, D], F32, kind="ExternalOutput").ap()
    build(nc, *args, out)
    r = run_bass_kernel_spmd(nc, [arrays], core_ids=[0])
    return r.results[0]["result_dram"].reshape(B, N, D)
```

```python
import numpy as np

import concourse.bass as bass
from concourse import mybir
from contextlib import ExitStack

F32 = mybir.dt.float32
ALU = mybir.AluOpType
ACT = mybir.ActivationFunctionType
AX = mybir.AxisListType

B, L, N = 8, 512, 375
D, DK = 256, 64
P = 125
TB = N // P
TT = B * TB
LC = L // 128
DC = D // 128
NH, HD = 16, 64
HP = NH // 2
UW = 3 * 2 * HD
E0, F0 = 16, 128
E1, F1 = 8, 1024
FC1 = F1 // 128
H1, D1 = 16, 16
GT = 4
GN = GT * P
NG = TT // GT
TOPK0, TOPK1 = 4, 2
SR0, SR = 128, 256
SLOTS0 = (TOPK0 * B * N + E0 * (SR0 - 1)) // SR0
SLOTS = (TOPK1 * B * N + E1 * (SR - 1)) // SR
MOST0, MOST1 = -(-B * N // SR0), -(-B * N // SR)
LAG = 5
RING = 6
TURNS0 = -(-SLOTS0 // RING)
EXPERT_BITS = 4
assert E0 <= 2 ** EXPERT_BITS and EXPERT_BITS * RING <= 24
W0 = 4 * F0 + D
RW = D + 1
FIRST, REST = (0, 1), tuple(range(2, FC1))
NOWHERE = 1 << 24
EPS = 1e-5
SCALE = HD ** -0.5
MASKED = -1e30
BIG = 3e38


PRIMED = dict(tok_free=3, xt_ready=1, turned=1, stage_copied=2, xt_ready5=1, turned5=1, stage_copied5=1,
              pj_read=2, rope_ready=2, masked=2, exped=2, ptT_ready=1, o_normed=1, po_added=2,
              hid0_ready=2, y0_added=2, rowsT0_ready=2, unit0_made=2, unitT0_ready=2, result0_copied=2,
              u_made=2, vs_ready=1, beta_ready=1, scanned=2, scan_out=1, l1_added=1,
              hid1_ready=2, y1_added=2, shid_ready=2, xsT_ready=2, ysb_ready=4)


def wait_apart(eng, sem, value, unused):
    eng.wait_ge(sem, value)
    eng.sem_inc(unused, 1)


class Count:

    def __init__(self, eng, sem):
        self.eng, self.sem, self.n = eng, sem, 0

    def __call__(self, ins):
        ins.then_inc(self.sem, 1)
        self.n += 1
        self.eng.wait_ge(self.sem, self.n)


class Unit:

    def __init__(self, b, hp, par):
        self.b, self.hp, self.par = b, hp, par
        self.u = b * HP + hp


def build(nc, x, dct, tok_w, tok_b, tok_alpha, w_in, b_in, w_out, b_out, sincos, mask, ident_in,
          gate0_w, gate0_b, ffn0_w, l1_w, l1_wk, l1_b_beta, l1_wo, l1_rows, gate1_w, ffn1_w, earlier,
          route_rows0, digits, route_rows, dest_in, empty_row, out):
    ctx = ExitStack()
    with ctx:
        def sb(name, shape):
            return ctx.enter_context(nc.sbuf_tensor(name, shape, F32))

        def sem(name):
            return ctx.enter_context(nc.semaphore(name))

        bank = [ctx.enter_context(nc.psum_tensor(f"bank{i}", [128, 512], F32)) for i in range(8)]

        scores0 = bank[0][0:P, 0:TT * E0]
        scores1 = bank[7][0:P, D:D + TT * E1]

        Hs = sb("hidden", [P, TT, D])
        XN = sb("normed", [P, TT, RW])
        XT = sb("normed_T", [128, DC, B * N])
        ident = sb("ident", [128, 128])
        stage = sb("norm_stage", [P, 2, TB, D])
        stats, mean_var, deviation, inverse = (
            [sb(f"{name}{i}", [P, TB, *dims]) for i in range(2)]
            for name, dims in (("stats", [6]), ("mean_var", [2]), ("std", []), ("inverse_std", [])))
        stats4 = sb("own_stats", [P, TB, 6])
        mean_var4 = sb("own_mean_var", [P, TB, 2])
        deviation4 = sb("own_std", [P, TB])
        inverse4 = sb("own_inverse_std", [P, TB])
        eps = sb("eps", [P, 1])
        alpha = sb("alpha", [P, 1])
        alpha_b = sb("alpha_b", [P, D])
        bout_rows = sb("bout_rows", [P, D])
        l1rows = sb("l1_rows", [P, 3, D])
        one = sb("weight_one", [P, 1])
        gate_k0 = sb("gate_of_choice0", [P, TOPK0, TT])
        pos_k0 = ctx.enter_context(nc.sbuf_tensor("row_of_choice0", [P, TOPK0, TT], mybir.dt.uint32))
        place0 = ctx.enter_context(nc.sbuf_tensor("place0", [SR0, RING], mybir.dt.uint32))
        slot_experts0 = ctx.enter_context(nc.sbuf_tensor("slot_experts0", [1, TURNS0], mybir.dt.int32))
        half_shared = sb("shared_weight", [P, 1])
        gate_k = sb("gate_of_choice", [P, TOPK1, TT])
        pos_k = ctx.enter_context(nc.sbuf_tensor("row_of_choice", [P, TOPK1, TT], mybir.dt.uint32))
        place = ctx.enter_context(nc.sbuf_tensor("place", [128, 2, 2], mybir.dt.uint32))
        slot_expert = ctx.enter_context(nc.sbuf_tensor("slot_expert", [1, SLOTS], mybir.dt.int32))
        dest = ctx.enter_context(nc.sbuf_tensor("dest", [P, TOPK0, TT], mybir.dt.int32))
        xs0_dram = nc.dram_tensor("expert_rows0", [SLOTS0 * SR0, RW], F32, kind="Internal").ap()
        ys0_dram = nc.dram_tensor("expert_results0", [TOPK0 * B * N, D], F32, kind="Internal").ap()
        xs_dram = nc.dram_tensor("expert_rows", [SLOTS * SR, RW], F32, kind="Internal").ap()
        ys_dram = nc.dram_tensor("expert_results", [TOPK1 * B * N, D], F32, kind="Internal").ap()
        g0w = sb("gate0_w", [128, DC, E0])
        g1w = sb("gate1_w", [128, DC, E1])
        g0b = sb("gate0_b", [P, E0])
        small = sb("small", [P, 6, TT * E0])

        AR = 22900
        arena = sb("arena", [128, AR])

        class Arena:
            def __init__(self):
                self.at = 0

            def take(self, parts, *dims):
                n = int(np.prod(dims))
                v = arena[0:parts, self.at:self.at + n]
                self.at += n
                assert self.at <= AR, self.at
                if len(dims) > 1:
                    names = "abcde"[:len(dims)]
                    v = v.rearrange(f"p ({' '.join(names)}) -> p {' '.join(names)}",
                                    **{k: d for k, d in zip(names[1:], dims[1:])})
                return v

        class Router:

            def __init__(self, a, e, choices, slots, most, rows, gates, places, experts, counts):
                self.counts = counts
                self.e, self.choices, self.slots, self.most, self.rows = e, choices, slots, most, rows
                self.gates, self.places, self.experts = gates, places, experts
                self.earlier = a.take(P, P)
                self.ones = a.take(P, P)
                self.consts = a.take(P, TT * e + most + slots + e + choices)
                self.rank = a.take(P, TT, e)
                self.any = a.take(P, TT, e)
                self.sel = a.take(P, choices, TT, e)
                self.prod = a.take(P, choices, TT, e)
                self.total = a.take(P, e, TT)
                self.before = a.take(P, e, TT)
                self.nslots = a.take(P, e)
                self.end = a.take(P, e)
                self.base = a.take(P, e)
                self.over = a.take(P, e, most)
                self.ended = a.take(1, slots, e)
                self.expert = a.take(1, slots)
                self.place = a.take(P, choices, TT)

        a = Arena()
        a.at = DC * HP * UW + HP * D + 2 * TB * 32 + 3 * P
        xbuf = a.take(128, 2, LC, N)
        cT = a.take(DK, L)
        tokw = a.take(DK, D)
        cw = a.take(128, LC, D)
        a = Arena()
        win = a.take(128, DC, HP * UW)
        wout = a.take(128, HP, D)
        cs = a.take(P, 2, TB, 32)
        mk = a.take(P, 3 * P)
        xtb = a.take(128, DC, N)
        qkb = a.take(P, 2, 4, 2, 32)
        mcos = a.take(P, 2, 4, 2, 32)
        msin = a.take(P, 2, 4, 2, 32)
        rk = a.take(P, 2, TB, 4, 64)
        vv = a.take(P, HP, TB, 2, HD + 1)
        qT = a.take(128, 2, 2, N)
        kT = a.take(128, 2, N)
        sm = a.take(P, 2, N)
        nmax = a.take(P, 2)
        pr = a.take(P, 2, 2, 6 * P)
        ptT = a.take(P, 2, N)
        rsum = a.take(P, 6)
        xn_flat = XN[:, :, :].rearrange("p t d -> p (t d)")
        bin_rows = xn_flat[:, 0:HP * UW]
        on = xn_flat[:, HP * UW:HP * UW + 2 * TB * 128].rearrange("p (i t h d) -> p i t h d", i=2, t=TB, h=2)
        a = Arena()
        w0_shared = a.take(128, W0)
        hid = a.take(128, 2, GN)
        sg = a.take(128, 2, GN)
        routed0_at = a.at
        compare0 = a.take(P, TT, E0, E0)
        turn_number = a.take(1, TURNS0)
        digits0 = a.take(P, RING)
        R0 = Router(a, E0, TOPK0, TURNS0 * RING, MOST0, SR0, gate_k0, pos_k0, slot_experts0,
                    (bank[1][0:P, 0:TT * E0], bank[2][0:P, 0:TT * E0]))
        a = Arena()
        a.at = routed0_at
        w0 = a.take(128, E0, W0)
        rows0 = a.take(SR0, RING, RW)
        rowsT0 = a.take(128, 2, DC, SR0)
        silu0 = a.take(SR0, 2, F0)
        unit0 = a.take(SR0, 2, F0)
        unitT0 = a.take(128, 2, SR0)
        result0 = a.take(SR0, RING, D)
        a = Arena()
        l1w = a.take(128, DC, 4, D)
        lraw = a.take(128, DC, 2 * D + H1)
        lwo = a.take(128, DC, D)
        hsum = a.take(128, DC, 2, H1)
        bbeta = a.take(128, DC)
        behind = 2 * 3 * DC * F1
        assert a.at <= behind // 2
        a.at = behind
        back0 = a.take(P, TOPK0, TB, D)
        vsb = a.take(128, 2, N)
        bet = a.take(128, 2, N)
        uu = a.take(128, 2, N)
        ss = a.take(128, 2, N)
        oo = a.take(128, DC, N)
        ztmp = a.take(P, TB, D)
        sum0 = a.take(P, TB, D)
        a = Arena()
        R1 = Router(a, E1, TOPK1, SLOTS, MOST1, SR, gate_k, pos_k, slot_expert,
                    (bank[6][0:P, 0:TT * E1], bank[6][0:P, TT * E1:2 * TT * E1]))
        compare1 = a.take(P, TT, E1, E1)
        assert a.at <= 3 * DC * F1
        a = Arena()
        fw = a.take(128, 2, 3 * DC * F1)
        fhid = a.take(128, 2, FC1, GN)
        fsg = a.take(128, 2, GN)
        a = Arena()
        a.take(128, 2, 3 * DC * F1)
        shid = a.take(128, 2, FC1, SR)
        ssg = a.take(128, 2, SR)
        xs = a.take(128, 2, 2, RW)
        xsT = a.take(128, 2, DC, SR)
        ysb = a.take(128, 2, 2, D)
        a = Arena()
        back = a.take(P, TOPK1, TT, D)
        oT = sb("heads_T", [128, 2, N])

        S = {}

        def s(name):
            if name not in S:
                S[name] = sem(name)
            return S[name]

        phase_done = s("phase_done")

        block = ctx.enter_context(nc.Block())

        def norm_sem(name, k):
            return s(name) if k < 3 else s(name + "5")

        def in_norm(name, k, n):
            return norm_sem(name, k), (k * B if k < 3 else 0) + n

        def barrier(eng, k):
            eng.drain().then_inc(phase_done, 1)
            eng.wait_ge(phase_done, 5 * k)

        def tile_of(buf, g):
            return buf[:, bass.ds(g, 1), 0:D].rearrange("p o d -> p (o d)")

        def walk_batches(eng, step):
            step(0, None, 0)
            with eng.Fori(0, B // 2 - 1) as bb:
                step(2 * bb + 1, 2 * bb, 1)
                step(2 * bb + 2, 2 * bb + 1, 0)
            step(B - 1, B - 2, 1)
            step(None, B - 1, 0)

        def walk_lagged(eng, step):
            def run(b):
                step(*[b - d if not isinstance(b, int) or 0 <= b - d < B else None for d in range(LAG + 1)])

            for b in range(LAG):
                run(b)
            with eng.Fori(LAG, B) as b:
                run(b)
            for b in range(B, B + LAG):
                run(b)

        def walk_slots0(eng, step):
            def run(m, i):
                near = []
                for d in (2, 1, 0, -1):
                    turn = m + (i + d) // RING
                    n = RING * turn + (i + d) % RING
                    near.append((n, (i + d) % RING, turn) if not isinstance(n, int) or 0 <= n < SLOTS0 else None)
                step(*near)

            turns = (SLOTS0 - 2) // RING
            for n in range(-2, RING):
                run(n // RING, n % RING)
            with eng.Fori(1, turns) as m:
                for i in range(RING):
                    run(m, i)
            for n in range(RING * turns, SLOTS0 + 1):
                run(n // RING, n % RING)

        def walk_units(eng, step):
            def run(b, hp, par):
                near = []
                for d in (2, 1, 0, -1, -2):
                    ub, uh = b, hp + d
                    if isinstance(hp, int):
                        ub, uh = (b - 1, uh + HP) if uh < 0 else (b + 1, uh - HP) if uh >= HP else (b, uh)
                    there = not isinstance(ub, int) or 0 <= ub < B
                    near.append(Unit(ub, uh, (par + d) % 2) if there else None)
                step(*near)

            def batch(b):
                run(b, 0, 0)
                run(b, 1, 1)
                with eng.Fori(1, HP // 2 - 1) as hh:
                    for i in range(2):
                        run(b, 2 * hh + i, i)
                run(b, HP - 2, 0)
                run(b, HP - 1, 1)

            run(0, -2, 0)
            run(0, -1, 1)
            batch(0)
            with eng.Fori(1, B - 1) as b:
                batch(b)
            batch(B - 1)
            run(B - 1, HP, 0)
            run(B - 1, HP + 1, 1)

        @block.sync
        def _(sp):
            for name, n in PRIMED.items():
                sp.sem_inc(s(name), n)
            sp.dma_start(cT, dct).then_inc(s("load_tok"), 16)
            sp.dma_start(tokw, tok_w).then_inc(s("load_tok"), 16)
            sp.dma_start(ident[:, :], ident_in).then_inc(s("load_tok"), 16)
            sp.dma_start(alpha[:, :], tok_alpha.partition_broadcast(P)).then_inc(s("load_tok"), 16)
            sp.dma_start(alpha_b[:, :], tok_b.partition_broadcast(P)).then_inc(s("load_tok"), 16)

            def load_x(b, j):
                sp.dma_start(xbuf[:, j], x[bass.ds(b, 1)].rearrange("o (c p) n -> p (o c) n", p=128))\
                    .then_inc(s(f"x_ready{j}"), 16)

            load_x(0, 0)
            load_x(1, 1)
            with sp.Fori(1, B // 2) as bb:
                for j in range(2):
                    sp.wait_ge(s("tok_made"), (2 * bb + j - 1) * TB)
                    load_x(2 * bb + j, j)
            sp.dma_start(win, w_in).then_inc(s("load_attn"), 16)
            sp.dma_start(bin_rows, b_in.partition_broadcast(P)).then_inc(s("load_attn"), 16)
            sp.dma_start(wout, w_out).then_inc(s("load_attn"), 16)
            sp.dma_start(cs, sincos).then_inc(s("load_attn"), 16)
            sp.dma_start(mk, mask).then_inc(s("load_attn"), 16)
            sp.dma_start(bout_rows[:, :], b_out.partition_broadcast(P)).then_inc(s("load_rows"), 16)
            sp.dma_start(l1rows[:, :, :], l1_rows.partition_broadcast(P)).then_inc(s("load_rows"), 16)
            sp.dma_start(g0b[:, :], gate0_b.partition_broadcast(P)).then_inc(s("load_rows"), 16)
            sp.dma_start(g0w[:, :, :], gate0_w).then_inc(s("load_rows"), 16)
            sp.dma_start(g1w[:, :, :], gate1_w).then_inc(s("load_rows"), 16)
            sp.dma_start(dest[:, :, :], dest_in).then_inc(s("load_rows"), 16)
            sp.dma_start(xs0_dram, empty_row.partition_broadcast(SLOTS0 * SR0)).then_inc(s("slots0_empty"), 16)
            sp.dma_start(xs_dram, empty_row.partition_broadcast(SLOTS * SR)).then_inc(s("slots_empty"), 16)
            barrier(sp, 1)
            barrier(sp, 2)
            sp.dma_start(R0.earlier, earlier).then_inc(s("load_route0"), 16)
            sp.dma_start(digits0, digits.partition_broadcast(P)).then_inc(s("load_route0"), 16)
            sp.dma_start(R0.consts, route_rows0.partition_broadcast(P)).then_inc(s("load_route0"), 16)
            sp.dma_start(w0_shared, ffn0_w[E0]).then_inc(s("w0_shared"), 16)
            barrier(sp, 3)
            sp.dma_start(w0, ffn0_w[0:E0].rearrange("e p n -> p e n")).then_inc(s("w0_ready"), 16)
            sp.wait_ge(s("rows0_sent"), 16 * TOPK0 * TT)
            barrier(sp, 4)

            def slot0_rows(n, i):
                sp.dma_start(rows0[:, i], xs0_dram[bass.ds(n * SR0, SR0), :]).then_inc(s(f"rows0_ready{i}"), 16)

            def next_slot0_rows(n, i):
                wait_apart(sp, s("rows0_turned"), n - RING + 1, s("unused"))
                wait_apart(sp, s("result0_copied"), n - RING + 3, s("unused"))
                slot0_rows(n, i)

            for i in range(RING):
                slot0_rows(i, i)
            with sp.Fori(1, SLOTS0 // RING) as m:
                for i in range(RING):
                    next_slot0_rows(RING * m + i, i)
            for n in range(SLOTS0 // RING * RING, SLOTS0):
                next_slot0_rows(n, n % RING)
            for i in range(RING):
                sp.wait_ge(s(f"result0_sent{i}"), 16 * (-(-(SLOTS0 - i) // RING)))
            barrier(sp, 5)
            y0 = ys0_dram.rearrange("(k t p) d -> p k t d", k=TOPK0, p=P)

            def load_back0(b):
                for k in range(TOPK0):
                    sp.dma_start(back0[:, k], y0[:, k, bass.ds(b * TB, TB), :]).then_inc(s("back0_ready"), 16)

            load_back0(0)
            sp.dma_start(lraw, l1_w).then_inc(s("load_l1"), 16)
            sp.dma_start(lwo, l1_wo).then_inc(s("load_l1"), 16)
            sp.dma_start(l1w[:, :, 0, :], l1_wk).then_inc(s("load_l1"), 16)
            sp.dma_start(bbeta, l1_b_beta).then_inc(s("load_l1"), 16)
            with sp.Fori(1, B) as b:
                wait_apart(sp, s("summed0"), b, s("unused"))
                load_back0(b)
            sp.dma_start(fw[:, 1], ffn1_w[E1]).then_inc(s("w1_shared"), 16)
            barrier(sp, 6)
            sp.dma_start(R1.earlier, earlier).then_inc(s("load_route1"), 16)
            sp.dma_start(R1.consts, route_rows.partition_broadcast(P)).then_inc(s("load_route1"), 16)
            W13 = 2 * DC * F1

            def slot_weights(slot, i, first=False):
                e = sp.value_load(slot_expert[0:1, bass.ds(slot, 1)], min_val=0, max_val=E1 - 1)
                if not first:
                    sp.wait_ge(s("slot_up"), FC1 * slot - FC1)
                sp.dma_start(fw[:, i, 0:W13], ffn1_w[bass.ds(e, 1), :, 0:W13].rearrange("o p n -> p (o n)"))\
                    .then_inc(s(f"w13_ready{i}"), 16)
                if not first:
                    sp.wait_ge(s("slot_out"), slot - 1)
                sp.dma_start(fw[:, i, W13:], ffn1_w[bass.ds(e, 1), :, W13:].rearrange("o p n -> p (o n)"))\
                    .then_inc(s(f"w2_ready{i}"), 16)

            def slot_rows(slot, i):
                sp.dma_start(xs[:, i], xs_dram[bass.ds(slot * SR, SR), :].rearrange("(a p) n -> p a n", p=128))\
                    .then_inc(s(f"xs_ready{i}"), 16)

            sp.wait_ge(s("routed"), 1)
            slot_weights(0, 0, True)
            sp.wait_ge(s("rows_sent"), 16 * TOPK1 * TT)
            barrier(sp, 7)
            slot_rows(0, 0)
            slot_rows(1, 1)
            slot_weights(1, 1, True)
            with sp.Fori(0, (SLOTS - 3) // 2) as ss_:
                for i in range(2):
                    slot = 2 * ss_ + (2 + i)
                    sp.wait_ge(s("slot_turned"), slot - 1)
                    sp.wait_ge(s("place_ready"), slot - 1)
                    slot_rows(slot, i)
                    slot_weights(slot, i)
            sp.wait_ge(s("slot_turned"), SLOTS - 2)
            sp.wait_ge(s("place_ready"), SLOTS - 2)
            slot_rows(SLOTS - 1, 0)
            slot_weights(SLOTS - 1, 0)
            for i in range(2):
                n = (SLOTS + 1 - i) // 2
                for a_ in range(2):
                    sp.wait_ge(s(f"y_sent{i}{a_}"), 16 * n)
            barrier(sp, 8)
            yv = ys_dram.rearrange("(k t p) d -> p k t d", k=TOPK1, p=P)
            for q in range(4):
                for k in range(TOPK1):
                    sp.dma_start(back[:, k, q * 6:(q + 1) * 6, :], yv[:, k, q * 6:(q + 1) * 6, :])\
                        .then_inc(s(f"back{q}"), 16)
            ov = out.rearrange("(t p) d -> p t d", p=P)
            for q in range(4):
                sp.wait_ge(s("summed"), q + 1)
                sp.dma_start(ov[:, q * 6:(q + 1) * 6, :], Hs[:, q * 6:(q + 1) * 6, :]).then_inc(s("stored"), 16)
            sp.wait_ge(s("stored"), 64)
        @block.tensor
        def _(pe):
            def turn_batch(k, b, i):
                pe.wait_ge(*in_norm("stage_ready", k, b + 1))
                pe.wait_ge(*in_norm("xt_ready", k, b + 1))
                for c in range(DC):
                    for t in range(TB):
                        m = pe.transpose(bank[4 + c][:, t * P:(t + 1) * P], stage[:, i, t, c * 128:(c + 1) * 128],
                                         ident[0:P, 0:P])
                m.then_inc(norm_sem("turned", k), 1)

            def turn_normed(k, source=None):
                def step(b, before, i):
                    if b is not None and source:
                        source(b, i)
                    if before is not None:
                        turn_batch(k, before, 1 - i)

                walk_batches(pe, step)

            def gate_scores(k, b, w, scores, e):
                pe.wait_ge(*in_norm("xt_ready", k, b + 2))
                for t in range(b * TB, (b + 1) * TB):
                    for c in range(DC):
                        m = pe.matmul(scores[:, t * e:(t + 1) * e], XT[:, c, t * P:(t + 1) * P], w[:, c, :],
                                      start=(c == 0), stop=(c == DC - 1))
                return m

            pe.wait_ge(s("load_tok"), 80)
            for c in range(LC):
                m = pe.matmul(bank[c // 2][:, (c % 2) * D:(c % 2 + 1) * D], cT[:, c * 128:(c + 1) * 128], tokw,
                              start=True, stop=True)
            m.then_inc(s("cw_made"), 1)
            pe.wait_ge(s("cw_ready"), 1)

            def transform(b, i):
                pe.wait_ge(s(f"x_ready{i}"), b * 8 + (16 - 8 * i))
                for t in range(TB):
                    pe.wait_ge(s("tok_free"), b * TB + t + 1)
                    for c in range(LC):
                        m = pe.matmul(bank[t][0:P, 0:D], xbuf[:, i, c, t * P:(t + 1) * P], cw[:, c, :],
                                      start=(c == 0), stop=(c == LC - 1))
                    m.then_inc(s("tok_made"), 1)

            turn_normed(0, transform)
            barrier(pe, 1)

            pe.wait_ge(s("load_attn"), 80)

            def project(w, t):
                pe.wait_ge(s("xtb_ready"), w.b * TB + t + 1)
                pe.wait_ge(s("pj_read"), w.u * TB + t + 1)
                for c in range(DC):
                    m = pe.matmul(bank[(w.par + t) % 2][0:P, 0:UW], xtb[:, c, t * P:(t + 1) * P],
                                  win[:, c, bass.ds(w.hp * UW, UW)], start=(c == 0), stop=(c == DC - 1))
                m.then_inc(s("pj_made"), 1)

            def turn_qk(w, before):
                pe.wait_ge(s("rope_ready"), (w.u + 1) * TB + 2)
                if before:
                    pe.wait_ge(s("oT_ready"), before.u + 1)
                for k in range(2):
                    for t in range(TB):
                        m = pe.transpose(bank[2 + k][:, t * P:(t + 1) * P],
                                         rk[:, w.par, t, 2 * k:2 * k + 2, :].rearrange("p a b -> p (a b)"),
                                         ident[0:P, 0:P])
                m.then_inc(s("qk_turned"), 1)

            def scores(w, g):
                h, qt = g // TB, g % TB
                pe.wait_ge(s("qkT_ready"), w.u + 1)
                pe.wait_ge(s("masked"), w.u * 6 + g + 1)
                pe.matmul(bank[4 + g % 2][0:P, 0:(qt + 1) * P], qT[:, w.par, h, qt * P:(qt + 1) * P],
                          kT[:, w.par, 0:(qt + 1) * P], start=True, stop=True).then_inc(s("scored"), 1)

            def turn_probs(w, g):
                h, qt = g // TB, g % TB
                pe.wait_ge(s("exped"), w.u * 6 + g + 3)
                pe.wait_ge(s("ptT_ready"), w.u * 6 + g + 1)
                for j in range(qt + 1):
                    o = (0, P, 3 * P)[qt] + j * P
                    m = pe.transpose(bank[6][0:P, j * P:(j + 1) * P], pr[:, w.par, h, o:o + P], ident[0:P, 0:P])
                m.then_inc(s("p_turned"), 1)

            def weigh(w, g):
                h, qt = g // TB, g % TB
                if g == 0:
                    pe.wait_ge(s("o_normed"), w.u + 1)
                pe.wait_ge(s("ptT_ready"), w.u * 6 + g + 2)
                for j in range(qt + 1):
                    m = pe.matmul(bank[7][0:P, g * (HD + 1):(g + 1) * (HD + 1)], ptT[:, g % 2, j * P:(j + 1) * P],
                                  vv[:, bass.ds(w.hp, 1), j, h, :].rearrange("p o d -> p (o d)"),
                                  start=(j == 0), stop=(j == qt))
                if g == 5:
                    m.then_inc(s("weighed"), 1)

            def turn_heads(w):
                pe.wait_ge(s("o_normed"), w.u + 2)
                pe.wait_ge(s("po_added"), w.u * 2 + 2)
                for t in range(TB):
                    m = pe.transpose(bank[2][:, t * P:(t + 1) * P],
                                     on[:, w.par, t].rearrange("p a b -> p (a b)"), ident[0:P, 0:P])
                m.then_inc(s("o_turned"), 1)

            def project_out(w, ahead, bk, tiles):
                pe.wait_ge(s("oT_ready"), w.u + 1)
                if ahead:
                    pe.wait_ge(s("qkT_ready"), ahead.u + 1)
                for j, t in enumerate(tiles):
                    m = pe.matmul(bank[bk][0:P, j * D:(j + 1) * D], oT[:, w.par, t * P:(t + 1) * P],
                                  wout[:, bass.ds(w.hp, 1), :].rearrange("p o d -> p (o d)"), start=True, stop=True)
                m.then_inc(s("po_made"), 1)

            def attend(w2, w1, w, l1, l2):
                for g in range(6):
                    if l1:
                        turn_probs(l1, g)
                    if w:
                        scores(w, g)
                    if l1 and g:
                        weigh(l1, g - 1)
                    if w2 and g % 2 == 0:
                        project(w2, g // 2)
                    if l2 and g == 1:
                        turn_heads(l2)
                    if w1 and g == 3:
                        turn_qk(w1, l2)
                    if l2 and g == 4:
                        project_out(l2, w1, 3, (0, 1))
                    if l2 and g == 5:
                        project_out(l2, w1, 2, (2,))
                if l1:
                    weigh(l1, 5)

            walk_units(pe, attend)
            barrier(pe, 2)

            def feed_forward(k, fc, i, w1_at, w3_at, w2_at, hidden, between=None):
                def group_pair(gg, between=None):
                    for j in range(2):
                        for f in range(fc):
                            n = (2 * gg + j) * fc + f
                            r = f % 2 if fc > 1 else j
                            pe.wait_ge(s(f"hid{k}_ready"), n + 1)
                            for w, bk, name in ((w1_at, 0, "up"), (w3_at, 2, "side")):
                                for c in range(DC):
                                    m = pe.matmul(bank[bk + r][:, 0:GN], w(i, c, f),
                                                  XT[:, c, bass.ds((2 * gg + j) * GN, GN)],
                                                  start=(c == 0), stop=(c == DC - 1))
                                m.then_inc(s(f"{name}{k}_made"), 1)
                        if between and j == 0:
                            between()
                    for j in range(2):
                        group = 2 * gg + j
                        pe.wait_ge(s(f"hid{k}_ready"), (group + 1) * fc + 2)
                        for h in range(GT // 2):
                            pe.wait_ge(s(f"y{k}_added"), 2 * group + h + 1)
                            for t in range(2):
                                for f in range(fc):
                                    m = pe.matmul(bank[4 + h][0:P, t * D:(t + 1) * D],
                                                  hidden(j, f)[:, (2 * h + t) * P:(2 * h + t + 1) * P], w2_at(i, f),
                                                  start=(f == 0), stop=(f == fc - 1))
                            m.then_inc(s(f"y{k}_ready"), 1)

                group_pair(0, between)
                with pe.Fori(1, NG // 2) as gg:
                    group_pair(gg)

            pe.wait_ge(s("load_rows"), 96)
            for b in range(B):
                turn_batch(1, b, b % 2)
                if b:
                    gate_scores(1, b - 1, g0w, scores0, E0)
            gate_scores(1, B - 1, g0w, scores0, E0).then_inc(s("gate0_made"), 1)

            def count_chosen(k, R):
                pe.wait_ge(s(f"load_route{k}"), 48 if k == 0 else 32)
                pe.wait_ge(s("chosen"), k + 1)
                for counts, w in zip(R.counts, (R.earlier, R.ones)):
                    m = pe.matmul(counts, w, R.any.rearrange("p t e -> p (t e)"), start=True, stop=True)
                m.then_inc(s("counted"), 1)

            count_chosen(0, R0)
            barrier(pe, 3)

            w0s = w0_shared[:, 0:4 * F0].rearrange("p (w c n) -> p w c n", w=2, c=DC)

            def w0_1(i, c, f):
                return w0s[:, 0, c, :]

            def w0_3(i, c, f):
                return w0s[:, 1, c, :]

            def w0_2(i, f):
                return w0_shared[:, 4 * F0:W0]

            def hid0(j, f):
                return hid[:, j, :]

            pe.wait_ge(s("w0_shared"), 16)
            feed_forward(0, 1, 0, w0_1, w0_3, w0_2, hid0)
            barrier(pe, 4)

            turns_at_hand = {}

            def expert_of(slot, fresh):
                n, i, turn = slot
                if fresh:
                    turns_at_hand[0] = pe.value_load(slot_experts0[0:1, bass.ds(turn, 1)], min_val=0,
                                                     max_val=2 ** (EXPERT_BITS * RING) - 1)
                return (turns_at_hand[0] >> (EXPERT_BITS * i)) & (2 ** EXPERT_BITS - 1)

            def slot0(n2, n1, n0, l1):
                down_expert = up_expert = None
                if l1:
                    down_expert = expert_of(l1, l1[1] == RING - 1 or isinstance(l1[0], int) and l1[0] == SLOTS0 - 1)
                if n1:
                    up_expert = expert_of(n1, n1[1] in (0, 1))
                if n2:
                    n, i, turn = n2
                    pe.wait_ge(s(f"rows0_ready{i}"), 16 * turn + 16)
                    pe.wait_ge(s("rowsT0_ready"), n + 1)
                    for c in range(DC):
                        m = pe.transpose(bank[i % 2][:, c * SR0:(c + 1) * SR0], rows0[:, i, c * 128:(c + 1) * 128],
                                         ident[:, :])
                    m.then_inc(s("rows0_turned"), 1)
                if n1:
                    n, i, turn = n1
                    pe.wait_ge(s("rowsT0_ready"), n + 3)
                    pe.wait_ge(s("unit0_made"), n + 1)
                    for c in range(DC):
                        m = pe.matmul(bank[2 + i % 2][0:SR0, 0:2 * F0].rearrange("p (w n) -> p w n", w=2),
                                      rowsT0[:, i % 2, c, :],
                                      w0[:, bass.ds(up_expert, 1), 0:4 * F0]
                                      .rearrange("p o (w c n) -> p (o w) c n", w=2, c=DC)[:, :, c, :], start=(c == 0), stop=(c == DC - 1))
                    m.then_inc(s("up0_slot"), 1)
                if n0:
                    n, i, turn = n0
                    pe.wait_ge(s("unit0_made"), n + 3)
                    pe.wait_ge(s("unitT0_ready"), n + 1)
                    pe.transpose(bank[4 + i % 2][:, 0:SR0], unit0[:, i % 2, :], ident[:, :])\
                        .then_inc(s("unit0_turned"), 1)
                if l1:
                    n, i, turn = l1
                    pe.wait_ge(s("unitT0_ready"), n + 3)
                    pe.wait_ge(s("result0_copied"), n + 1)
                    pe.matmul(bank[6 + i % 2][0:SR0, 0:D], unitT0[:, i % 2, :],
                              w0[:, bass.ds(down_expert, 1), 4 * F0:W0].rearrange("p o n -> p (o n)"),
                              start=True, stop=True)\
                        .then_inc(s("result0_made"), 1)

            pe.wait_ge(s("w0_ready"), 16)
            walk_slots0(pe, slot0)
            barrier(pe, 5)


            def products(b, c, qs):
                for q in qs:
                    pe.wait_ge(s(("u_made", "vs_ready", "beta_ready", "scan_out")[q]), DC * b + c + (2 if q == 0 else 1))
                    for kc in range(DC):
                        m = pe.matmul(bank[q][:, 0:N], l1w[:, kc, q, c * 128:(c + 1) * 128],
                                      XT[:, kc, bass.ds(b * N, N)], start=(kc == 0), stop=(kc == DC - 1))
                    m.then_inc(s(f"l1_made{q}"), 1)

            scored = []

            def attend1(b0, b1, b2, b3, b4, b5):
                if b2 is not None:
                    if isinstance(b2, int) and b2 == 0:
                        pe.wait_ge(s("l1w_ready"), 1)
                    pe.wait_ge(s("xt_ready"), 2 * B + b2 + 2)
                    products(b2, 0, (0, 1))
                if b3 is not None:
                    pe.wait_ge(s("scan_out"), DC * b3 + DC + 1)
                    pe.wait_ge(s("l1_added"), b3 + 1)
                    for t in range(TB):
                        for c in range(DC):
                            m = pe.matmul(bank[6 + t // 2][0:P, t % 2 * D:(t % 2 + 1) * D], oo[:, c, t * P:(t + 1) * P],
                                          lwo[:, c, :], start=(c == 0), stop=(c == DC - 1))
                    m.then_inc(s("l1_out"), 1)
                if b2 is not None:
                    products(b2, 0, (2, 3))
                if b5 is not None:
                    pe.wait_ge(s("xt_ready"), 2 * B + (B if b1 is None else b1) + 1)
                    turn_batch(3, b5, 1)
                if b2 is not None:
                    products(b2, 1, (0, 1))
                if b1 is not None:
                    if b5 is not None:
                        pe.wait_ge(s("xt_ready5"), b5 + 2)
                    turn_batch(2, b1, 0)
                if b2 is not None:
                    products(b2, 1, (2, 3))
                if isinstance(b5, int):
                    if b3 is not None:
                        pe.wait_ge(s("l1_added"), b3 + 2)
                    for b in range(len(scored), min(len(scored) + 2, b5)):
                        gate_scores(3, b, g1w, scores1, E1)
                        scored.append(b)

            walk_lagged(pe, attend1)
            for b in range(len(scored), B):
                m = gate_scores(3, b, g1w, scores1, E1)
            m.then_inc(s("gate1_made"), 1)
            barrier(pe, 6)

            fwv = fw.rearrange("p i (w n) -> p i w n", w=3)
            f13 = fwv[:, :, 0:2, :].rearrange("p i w (c n) -> p i w c n", c=DC)
            f2 = fwv[:, :, 2, :].rearrange("p i (f n) -> p i f n", f=FC1)

            def w1_1(i, c, f):
                return f13[:, i, 0, c, f * 128:(f + 1) * 128]

            def w1_3(i, c, f):
                return f13[:, i, 1, c, f * 128:(f + 1) * 128]

            def w1_2(i, f):
                return f2[:, i, f, :]

            def hid1(j, f):
                return fhid[:, j, f, :]

            pe.wait_ge(s("w1_shared"), 16)
            feed_forward(1, FC1, 1, w1_1, w1_3, w1_2, hid1, lambda: count_chosen(1, R1))
            barrier(pe, 7)

            def turn_rows(slot, i):
                pe.wait_ge(s(f"xs_ready{i}"), slot * 8 + (16 - 8 * i))
                pe.wait_ge(s("xsT_ready"), slot + 1)
                for c in range(DC):
                    for a_ in range(2):
                        m = pe.transpose(bank[2 + i][:, (2 * c + a_) * 128:(2 * c + a_ + 1) * 128],
                                         xs[:, i, a_, c * 128:(c + 1) * 128], ident[:, :])
                m.then_inc(s("slot_turned"), 1)

            def slot_hidden(slot, i, units):
                if units[0] == 0:
                    pe.wait_ge(s(f"w13_ready{i}"), slot * 8 + (16 - 8 * i))
                    pe.wait_ge(s("xsT_ready"), slot + 3)
                for f in units:
                    pe.wait_ge(s("shid_ready"), slot * FC1 + f + 1)
                    for q, w in enumerate((w1_1, w1_3)):
                        for c in range(DC):
                            m = pe.matmul(bank[f % 2][:, q * SR:(q + 1) * SR], w(i, c, f), xsT[:, i, c, :],
                                          start=(c == 0), stop=(c == DC - 1))
                    m.then_inc(s("slot_up"), 1)

            def slot_result(slot, i):
                pe.wait_ge(s(f"w2_ready{i}"), slot * 8 + (16 - 8 * i))
                pe.wait_ge(s("shid_ready"), (slot + 1) * FC1 + 2)
                pe.wait_ge(s("ysb_ready"), 2 * slot + 2)
                for a_ in range(2):
                    for f in range(FC1):
                        m = pe.matmul(bank[4 + 2 * i + a_][:, 0:D], shid[:, i, f, a_ * 128:(a_ + 1) * 128], w1_2(i, f),
                                      start=(f == 0), stop=(f == FC1 - 1))
                m.then_inc(s("slot_out"), 1)

            turn_rows(0, 0)
            slot_hidden(0, 0, FIRST)
            with pe.Fori(0, (SLOTS - 1) // 2) as ss_:
                turn_rows(2 * ss_ + 1, 1)
                slot_hidden(2 * ss_, 0, REST)
                slot_hidden(2 * ss_ + 1, 1, FIRST)
                slot_result(2 * ss_, 0)
                turn_rows(2 * ss_ + 2, 0)
                slot_hidden(2 * ss_ + 1, 1, REST)
                slot_hidden(2 * ss_ + 2, 0, FIRST)
                slot_result(2 * ss_ + 1, 1)
            slot_hidden(SLOTS - 1, 0, REST)
            slot_result(SLOTS - 1, 0)
            barrier(pe, 8)

        @block.scalar
        def _(act):
            def deviations(k, b):
                act.wait_ge(*in_norm("var_ready", k, b + 1))
                act.activation(deviation[k // 3][:, :], mean_var[k // 3][:, :, 1], ACT.Sqrt, bias=eps[:, 0:1])\
                    .then_inc(norm_sem("sd_ready", k), 1)

            def copy_batch(k, b):
                act.wait_ge(*in_norm("turned", k, b + 2))
                for c in range(DC):
                    ins = act.activation(XT[:, c, bass.ds(b * N, N)], bank[4 + c][:, 0:N], ACT.Copy)
                ins.then_inc(norm_sem("xt_ready", k), 1)

            def copy_turned(k):
                def step(b, before, i):
                    if b is not None:
                        deviations(k, b)
                    if before is not None:
                        copy_batch(k, before)

                walk_batches(act, step)

            act.wait_ge(s("eps_ready"), 1)
            copy_turned(0)
            barrier(act, 1)

            def exps(w, g):
                h, qt = g // TB, g % TB
                wd, o = (qt + 1) * P, (0, P, 3 * P)[qt]
                act.wait_ge(s("masked"), w.u * 6 + g + 3)
                act.activation(pr[:, w.par, h, o:o + wd], sm[:, g % 2, 0:wd], ACT.Exp, bias=nmax[:, g % 2:g % 2 + 1],
                               scale=-1.0).then_inc(s("exped"), 1)

            def copy_probs(w, g):
                wd = (g % TB + 1) * P
                act.wait_ge(s("p_turned"), w.u * 6 + g + 1)
                act.activation(ptT[:, g % 2, 0:wd], bank[6][0:P, 0:wd], ACT.Copy).then_inc(s("ptT_ready"), 1)

            def attend(w2, w1, w, l1, l2):
                for g in range(6):
                    if l1:
                        copy_probs(l1, g)
                    if g == 0 and l1:
                        exps(l1, 5)
                    if g and w:
                        exps(w, g - 1)
                    if g == 1 and l2:
                        act.wait_ge(s("o_turned"), l2.u + 1)
                        act.activation(oT[:, l2.par, :], bank[2][:, 0:N], ACT.Copy).then_inc(s("oT_ready"), 1)

            walk_units(act, attend)
            barrier(act, 2)

            def silus(k, fc, e, sgv):
                with act.Fori(0, NG // 2) as gg:
                    for j in range(2):
                        for f in range(fc):
                            n = (e * NG + 2 * gg + j) * fc + f
                            r = f % 2 if fc > 1 else j
                            act.wait_ge(s(f"up{k}_made"), n + 1)
                            act.wait_ge(s(f"hid{k}_ready"), n + 1)
                            act.activation(sgv[:, r, :], bank[r][:, 0:GN], ACT.Silu).then_inc(s(f"silu{k}"), 1)

            copy_turned(1)
            act.wait_ge(s("gate0_made"), 1)
            act.activation(small[:, 0, :], scores0, ACT.Sigmoid).then_inc(s("gate0_sig"), 1)
            barrier(act, 3)
            silus(0, 1, 0, sg)
            barrier(act, 4)

            def slot0(n2, n1, n0, l1):
                if n2:
                    n, i, turn = n2
                    act.wait_ge(s("rows0_turned"), n + 1)
                    act.activation(rowsT0[:, i % 2].rearrange("p c n -> p (c n)"), bank[i % 2][:, 0:D], ACT.Copy)\
                        .then_inc(s("rowsT0_ready"), 1)
                if n1:
                    n, i, turn = n1
                    act.wait_ge(s("up0_slot"), n + 1)
                    act.wait_ge(s("unit0_made"), n + 1)
                    act.activation(silu0[:, i % 2, :], bank[2 + i % 2][0:SR0, 0:F0], ACT.Silu)\
                        .then_inc(s("slot0_silu"), 1)

            walk_slots0(act, slot0)
            barrier(act, 5)
            def decay(b, c):
                act.wait_ge(s("l1_made1"), DC * b + c + 1)
                act.wait_ge(s("u_made"), DC * b + c + 1)
                act.activation(vsb[:, c, :], bank[1][:, 0:N], ACT.Copy).then_inc(s("vs_ready"), 1)
                act.wait_ge(s("l1_made2"), DC * b + c + 1)
                act.wait_ge(s("scanned"), DC * b + c + 1)
                act.activation(bet[:, c, :], bank[2][:, 0:N], ACT.Sigmoid, bias=bbeta[:, c:c + 1])\
                    .then_inc(s("beta_ready"), 1)

            def attend1(b0, b1, b2, b3, b4, b5):
                if b2 is not None:
                    decay(b2, 0)
                if b5 is not None:
                    copy_batch(3, b5)
                if b0 is not None:
                    act.wait_ge(s("back0_ready"), (b0 + 1) * (16 * TOPK0))
                    for k in range(TOPK0):
                        for t in range(TB):
                            ins = act.activation(back0[:, k, t, :], back0[:, k, t, :], ACT.Copy,
                                                 scale=gate_k0[:, k, bass.ds(b0 * TB + t, 1)])
                    ins.then_inc(s("scaled0"), 1)
                if b2 is not None:
                    decay(b2, 1)
                if b1 is not None:
                    copy_batch(2, b1)
                if b3 is not None:
                    act.wait_ge(s("var4_ready"), b3 + 1)
                    act.activation(deviation4[:, :], mean_var4[:, :, 1], ACT.Sqrt, bias=eps[:, 0:1])\
                        .then_inc(s("sd4_ready"), 1)
                if b4 is not None:
                    deviations(3, b4)
                if b0 is not None:
                    deviations(2, b0)

            walk_lagged(act, attend1)
            barrier(act, 6)
            act.wait_ge(s("gate1_made"), 1)
            act.wait_ge(s("gate1_max"), 1)
            act.activation(small[:, 1, 0:TT * E1], small[:, 0, 0:TT * E1], ACT.Exp).then_inc(s("gate1_exp"), 1)
            silus(1, FC1, 0, fsg)
            barrier(act, 7)

            def copy_rows(slot, i):
                act.wait_ge(s("slot_turned"), slot + 1)
                act.activation(xsT[:, i].rearrange("p c n -> p (c n)"), bank[2 + i][:, :], ACT.Copy)\
                    .then_inc(s("xsT_ready"), 1)

            def slot_silu(slot, units):
                for f in units:
                    act.wait_ge(s("slot_up"), slot * FC1 + f + 1)
                    act.activation(ssg[:, f % 2, :], bank[f % 2][:, 0:SR], ACT.Silu).then_inc(s("slot_silu"), 1)

            def copy_results(slot, i):
                act.wait_ge(s("slot_out"), slot + 1)
                act.wait_ge(s("place_ready"), slot + 1)
                for a_ in range(2):
                    act.activation(ysb[:, i, a_, :], bank[4 + 2 * i + a_][:, 0:D], ACT.Copy).then_inc(s("ysb_ready"), 1)

            copy_rows(0, 0)
            slot_silu(0, FIRST)
            with act.Fori(0, (SLOTS - 1) // 2) as ss_:
                copy_rows(2 * ss_ + 1, 1)
                slot_silu(2 * ss_, REST)
                slot_silu(2 * ss_ + 1, FIRST)
                copy_results(2 * ss_, 0)
                copy_rows(2 * ss_ + 2, 0)
                slot_silu(2 * ss_ + 1, REST)
                slot_silu(2 * ss_ + 2, FIRST)
                copy_results(2 * ss_ + 1, 1)
            slot_silu(SLOTS - 1, REST)
            copy_results(SLOTS - 1, 0)
            barrier(act, 8)

        @block.gpsimd
        def _(pool):
            pool.memset(eps[:, :], EPS).then_inc(s("eps_ready"), 1)

            def keep_batch(k, b, i):
                pool.wait_ge(*in_norm("stage_ready", k, b + 1))
                pool.tensor_copy(XN[:, bass.ds(b * TB, TB), 0:D], stage[:, i]).then_inc(norm_sem("stage_copied", k), 1)

            def keep_normed(k):
                with pool.Fori(0, B // 2) as bb:
                    for i in range(2):
                        keep_batch(k, 2 * bb + i, i)

            barrier(pool, 1)
            pool.wait_ge(s("load_rows"), 96)
            pool.memset(qT[:, :, :, :], 0.0).then_inc(s("q_zero"), 1)
            pool.memset(vv[:, :, :, :, HD:HD + 1], 1.0).then_inc(s("q_zero"), 1)

            def place_tile(b, t):
                if not isinstance(b, int) or b > 0:
                    pool.wait_ge(s("pj_made"), b * HP * TB - TB + t + 1)
                pool.tensor_copy(xtb[:, :, t * P:(t + 1) * P], XT[:, :, bass.ds(b * N + t * P, P)])\
                    .then_inc(s("xtb_ready"), 1)

            def rope(w, t):
                r = (w.par + t) % 2
                pool.wait_ge(s("roped"), w.u * TB + t + 1)
                pool.tensor_tensor(rk[:, w.par, t, :, 0:32], mcos[:, r, :, 1, :], msin[:, r, :, 0, :], ALU.add)
                pool.tensor_tensor(rk[:, w.par, t, :, 32:64], mcos[:, r, :, 0, :], msin[:, r, :, 1, :],
                                   ALU.subtract).then_inc(s("rope_ready"), 1)

            def add_bias(b):
                for t in range(TB):
                    ins = pool.tensor_tensor(tile_of(Hs, b * TB + t), tile_of(Hs, b * TB + t), bout_rows[:, :], ALU.add)
                ins.then_inc(s("bout_added"), 1)

            def attend(w2, w1, w, l1, l2):
                if w2 and isinstance(w2.hp, int) and w2.hp == 0:
                    for t in range(TB):
                        place_tile(w2.b, t)
                if w2:
                    for t in range(TB):
                        rope(w2, t)
                if w and isinstance(w.hp, int) and w.hp == 0:
                    add_bias(w.b)

            walk_units(pool, attend)
            barrier(pool, 2)
            pool.memset(R0.ones, 1.0).then_inc(s("ones_ready"), 1)
            keep_normed(1)
            barrier(pool, 3)

            def send_rows(choices, places, rows_dram, sent, stated):
                for k in range(choices):
                    if k:
                        pool.wait_ge(s(sent), 16 * k * TT)
                    pool.tensor_copy(XN[:, :, D].bitcast(mybir.dt.int32), dest[:, k, :]).then_inc(s("dest_ready"), 1)
                    pool.wait_ge(s("dest_ready"), stated + k + 1)
                    for t in range(TT):
                        pool.indirect_dma_start(out=rows_dram,
                                                out_offset=bass.IndirectOffsetOnAxis(ap=places[:, k, t:t + 1], axis=0),
                                                in_=XN[:, t, :], in_offset=None).then_inc(s(sent), 16)

            pool.wait_ge(s("slots0_empty"), 16)
            send_rows(TOPK0, pos_k0, xs0_dram, "rows0_sent", 0)
            barrier(pool, 4)

            def slot0(n2, n1, n0, l1):
                if l1:
                    n, i, turn = l1
                    if not isinstance(turn, int) or turn > 0:
                        pool.wait_ge(s(f"result0_sent{i}"), 16 * turn)
                    pool.sem_inc(s("buffer0_free"), 1)
                    pool.wait_ge(s("result0_copied"), n + 3)
                    pool.sem_inc(s("unused"), 1)
                    pool.indirect_dma_start(out=ys0_dram,
                                            out_offset=bass.IndirectOffsetOnAxis(ap=place0[:, i:i + 1], axis=0),
                                            in_=result0[:, i, :], in_offset=None, bounds_check=TOPK0 * B * N - 1,
                                            oob_is_err=False).then_inc(s(f"result0_sent{i}"), 16)

            walk_slots0(pool, slot0)
            barrier(pool, 5)

            def attend1(b0, b1, b2, b3, b4, b5):
                if b5 is not None:
                    keep_batch(3, b5, 1)
                if b0 is not None:
                    pool.wait_ge(s("scaled0"), b0 + 1)
                    if not isinstance(b0, int) or b0 > 0:
                        pool.wait_ge(s("combined"), b0)
                    pool.sem_inc(s("unused"), 1)
                    pool.tensor_tensor(back0[:, 0:2], back0[:, 0:2], back0[:, 2:4], ALU.add).then_inc(s("paired0"), 1)
                    wait_apart(pool, s("paired0"), b0 + 1, s("unused"))
                    pool.tensor_tensor(sum0[:, :, :], back0[:, 0], back0[:, 1], ALU.add).then_inc(s("summed0"), 1)
                if b1 is not None:
                    keep_batch(2, b1, 0)
                if b3 is not None:
                    z = XN[:, bass.ds(b3 * TB, TB), 0:D]
                    wait_apart(pool, s("normed4"), b3 + 1, s("unused"))
                    pool.tensor_tensor(z, z, l1rows[:, 1, :].unsqueeze(1).to_broadcast([P, TB, D]), ALU.mult)\
                        .then_inc(s("scaled4"), 1)
                    wait_apart(pool, s("scaled4"), b3 + 1, s("unused"))
                    pool.tensor_tensor(z, z, l1rows[:, 2, :].unsqueeze(1).to_broadcast([P, TB, D]), ALU.add)\
                        .then_inc(s("offset4"), 1)

            walk_lagged(pool, attend1)
            barrier(pool, 6)
            pool.memset(R1.ones, 1.0).then_inc(s("ones_ready"), 1)
            pool.wait_ge(s("slots_empty"), 16)
            pool.wait_ge(s("routed"), 1)
            send_rows(TOPK1, pos_k, xs_dram, "rows_sent", TOPK0)
            barrier(pool, 7)

            def send_results(slot, i, first=False):
                pool.wait_ge(s(f"xs_ready{i}"), slot * 8 + (16 - 8 * i))
                if not first:
                    for a_ in range(2):
                        pool.wait_ge(s(f"y_sent{i}{a_}"), slot * 8 - 8 * i)
                pool.sem_inc(s("unused"), 1)
                pool.tensor_copy(place[:, i, :], xs[:, i, :, D].bitcast(mybir.dt.uint32)).then_inc(s("place_ready"), 1)
                pool.wait_ge(s("place_ready"), slot + 1)
                for a_ in range(2):
                    pool.wait_ge(s("ysb_ready"), 2 * slot + a_ + 5)
                    pool.sem_inc(s("unused"), 1)
                    pool.indirect_dma_start(out=ys_dram,
                                            out_offset=bass.IndirectOffsetOnAxis(
                                                ap=place[:, i, a_:a_ + 1], axis=0),
                                            in_=ysb[:, i, a_, :], in_offset=None, bounds_check=TOPK1 * B * N - 1,
                                            oob_is_err=False).then_inc(s(f"y_sent{i}{a_}"), 16)

            for i in range(2):
                send_results(i, i, True)
            with pool.Fori(1, (SLOTS - 1) // 2) as ss_:
                send_results(2 * ss_, 0)
                send_results(2 * ss_ + 1, 1)
            send_results(SLOTS - 1, 0)
            barrier(pool, 8)

        @block.vector
        def _(v):
            chain = Count(v, s("dve_step"))

            def tile(buf, g):
                return tile_of(buf, g)

            def variances(k, b, src):
                for t in range(TB):
                    ins = v.bn_stats(stats[k // 3][:, t, :], tile(src, b * TB + t))
                ins.then_inc(norm_sem("stats_ready", k), 1)
                wait_apart(v, *in_norm("stats_ready", k, b + 1), s("unused"))
                for t in range(TB):
                    ins = v.bn_aggr(mean_var[k // 3][:, t, :], stats[k // 3][:, t, :])
                ins.then_inc(norm_sem("var_ready", k), 1)

            def normalise_batch(k, b, i, src, kept=None):
                v.wait_ge(*in_norm("sd_ready", k, b + 1))
                v.reciprocal(inverse[k // 3][:, :], deviation[k // 3][:, :]).then_inc(norm_sem("inverse_ready", k), 1)
                v.wait_ge(*in_norm("inverse_ready", k, b + 1))
                v.wait_ge(*in_norm("turned", k, b + 1))
                if kept is not None:
                    v.wait_ge(norm_sem("stage_copied", k), kept + b)
                for t in range(TB):
                    ins = v.tensor_scalar(stage[:, i, t, :], tile(src, b * TB + t), mean_var[k // 3][:, t, 0:1],
                                          inverse[k // 3][:, t:t + 1], ALU.subtract, ALU.mult)
                ins.then_inc(norm_sem("stage_ready", k), 1)

            def normalise(k, src, kept=None, source=None):
                def step(b, before, i):
                    if before is not None:
                        normalise_batch(k, before, 1 - i, src, kept)
                    if b is not None:
                        if source:
                            source(b, i)
                        variances(k, b, src)

                walk_batches(v, step)

            v.wait_ge(s("load_tok"), 80)
            v.wait_ge(s("cw_made"), 1)
            for h in range(2):
                cp = v.tensor_copy(cw[:, 2 * h:2 * h + 2, :].rearrange("p a b -> p (a b)"), bank[h][:, :])
            cp.then_inc(s("cw_ready"), 1)
            chain(v.tensor_scalar(alpha_b[:, :], alpha_b[:, :], alpha[:, 0:1], None, ALU.mult))

            def take_transform(b, i):
                for t in range(TB):
                    g = b * TB + t
                    v.wait_ge(s("tok_made"), g + 1)
                    v.scalar_tensor_tensor(tile(Hs, g), bank[t][0:P, 0:D], alpha[:, 0:1], alpha_b[:, :],
                                           ALU.mult, ALU.add).then_inc(s("tok_free"), 1)
                wait_apart(v, s("tok_free"), b * TB + TB + 3, s("unused"))

            normalise(0, Hs, source=take_transform)
            barrier(v, 1)

            v.wait_ge(s("load_attn"), 80)
            v.wait_ge(s("q_zero"), 2)

            def take_projection(w, t):
                n = w.u * TB + t
                r = (w.par + t) % 2
                v.wait_ge(s("pj_made"), n + 1)
                v.tensor_tensor(vv[:, bass.ds(w.hp, 1), t, :, 0:HD].rearrange("p o h d -> p (o h) d"),
                                bank[r][0:P, 4 * HD:6 * HD].rearrange("p (h d) -> p h d", h=2),
                                bin_rows[:, bass.ds(w.hp * UW + 4 * HD, 2 * HD)].rearrange("p (h d) -> p h d", h=2),
                                ALU.add)
                v.tensor_tensor(qkb[:, r].rearrange("p a b c -> p (a b c)"), bank[r][0:P, 0:4 * HD],
                                bin_rows[:, bass.ds(w.hp * UW, 4 * HD)], ALU.add).then_inc(s("pj_read"), 1)
                v.wait_ge(s("pj_read"), n + 3)
                v.wait_ge(s("rope_ready"), n + 1)
                x8 = qkb[:, r].rearrange("p a b c -> p (a b) c")
                for k, m in ((0, mcos), (1, msin)):
                    ins = v.tensor_tensor(m[:, r].rearrange("p a b c -> p (a b) c"), x8,
                                          cs[:, k, t, :].unsqueeze(1).to_broadcast([P, 8, 32]), ALU.mult)
                ins.then_inc(s("roped"), 1)

            def take_qkT(w):
                v.wait_ge(s("qk_turned"), w.u + 1)
                v.tensor_copy(qT[0:64, w.par, 0, :], bank[2][0:64, 0:N])
                v.tensor_copy(qT[64:128, w.par, 1, :], bank[2][64:128, 0:N])
                v.tensor_copy(kT[:, w.par, :], bank[3][:, 0:N]).then_inc(s("qkT_ready"), 1)

            def mask_scores(w, g):
                wd = (g % TB + 1) * P
                v.wait_ge(s("exped"), w.u * 6 + g + 1)
                wait_apart(v, s("scored"), w.u * 6 + g + 1, s("unused"))
                v.tensor_tensor_reduce(sm[:, g % 2, 0:wd], bank[4 + g % 2][0:P, 0:wd], mk[:, 3 * P - wd:3 * P], -SCALE,
                                       BIG, ALU.add, ALU.min, nmax[:, g % 2:g % 2 + 1]).then_inc(s("masked"), 1)

            def divide(w):
                v.wait_ge(s("weighed"), w.u + 1)
                ob = bank[7][0:P, 0:6 * (HD + 1)].rearrange("p (g d) -> p g d", d=HD + 1)
                v.reciprocal(rsum, ob[:, :, HD]).then_inc(s("sum_turned"), 1)
                v.wait_ge(s("sum_turned"), w.u + 1)
                for h in range(2):
                    ins = v.tensor_tensor(on[:, w.par, :, h, :], ob[:, h * TB:(h + 1) * TB, 0:HD],
                                          rsum[:, h * TB:(h + 1) * TB].unsqueeze(2).to_broadcast([P, TB, HD]), ALU.mult)
                ins.then_inc(s("o_normed"), 1)

            def add_out(w, n, bk, t, tiles):
                v.wait_ge(s("bout_added"), w.b + 1)
                v.wait_ge(s("po_made"), w.u * 2 + n + 1)
                v.wait_ge(s("po_added"), w.u * 2 + n + 1)
                h = Hs[:, bass.ds(w.b * TB + t, tiles), :].rearrange("p t d -> p (t d)")
                v.tensor_tensor(h, bank[bk][0:P, 0:tiles * D], h, ALU.add).then_inc(s("po_added"), 1)

            def attend(w2, w1, w, l1, l2):
                if l2:
                    divide(l2)
                for g in range(6):
                    if w:
                        mask_scores(w, g)
                    if w2 and g % 2 == 0:
                        take_projection(w2, g // 2)
                    if w1 and g == 3:
                        take_qkT(w1)
                    if l2 and g == 4:
                        add_out(l2, 0, 3, 0, 2)
                    if l2 and g == 5:
                        add_out(l2, 1, 2, 2, 1)

            walk_units(v, attend)
            barrier(v, 2)

            normalise(1, Hs, kept=1)
            v.wait_ge(s("load_rows"), 96)

            def top(src, e, out_ap, keep_n, before, T):
                for i in range(e):
                    v.memset(before[:, :, i, i:i + 1], 0.0)
                    this = src[:, :, i:i + 1]
                    if i < e - 1:
                        ins = v.tensor_tensor(before[:, :, i, i + 1:e], src[:, :, i + 1:e],
                                              this.to_broadcast([P, T, e - 1 - i]), ALU.is_gt)
                    if i:
                        ins = v.tensor_tensor(before[:, :, i, 0:i], src[:, :, 0:i], this.to_broadcast([P, T, i]),
                                              ALU.is_ge)
                chain(ins)
                chain(v.tensor_reduce(out_ap, before, AX.X, ALU.add))
                if keep_n is not None:
                    chain(v.tensor_scalar(out_ap, out_ap, float(keep_n), None, ALU.is_lt))

            def sm3(k, e):
                return small[:, k, 0:TT * e].rearrange("p (t e) -> p t e", e=e)

            v.wait_ge(s("gate0_sig"), 1)
            sig, sbias = sm3(0, E0), sm3(1, E0)
            chain(v.tensor_tensor(sbias, sig, g0b[:, :].unsqueeze(1).to_broadcast([P, TT, E0]), ALU.add))
            s4 = sbias.rearrange("p t (g e) -> p (t g) e", g=4)
            gm = small[:, 2, 0:TT * 4]
            chain(v.tensor_reduce(gm, s4, AX.X, ALU.max))
            kp = small[:, 3, 0:TT * 4]
            ca = compare0.rearrange("p a b c -> p (a b c)")[:, 0:TT * 16].rearrange("p (t i j) -> p t i j", i=4, j=4)
            top(gm.rearrange("p (t g) -> p t g", g=4), 4, kp.rearrange("p (t g) -> p t g", g=4), 2, ca, TT)
            keep3 = kp.unsqueeze(2).to_broadcast([P, TT * 4, 4])
            off = small[:, 4, 0:TT * 4]
            chain(v.tensor_scalar(off, kp, BIG, BIG, ALU.mult, ALU.subtract))
            chain(v.tensor_tensor(s4, s4, keep3, ALU.mult))
            chain(v.tensor_tensor(s4, s4, off.unsqueeze(2).to_broadcast([P, TT * 4, 4]), ALU.add))
            top(sbias, E0, R0.rank, None, compare0, TT)

            def route(k, R, probs):
                at = [0]

                def const(n):
                    at[0] += n
                    return R.consts[:, at[0] - n:at[0]]

                resets = const(TT * R.e)
                full = const(R.most)
                slotno = const(R.slots)
                ones_e = const(R.e)
                choice = const(R.choices)
                each = [P, R.choices, TT, R.e]

                def choose():
                    v.wait_ge(s(f"load_route{k}"), 48 if k == 0 else 32)
                    v.wait_ge(s("ones_ready"), k + 1)
                    v.tensor_scalar(R.any, R.rank, float(R.choices), None, ALU.is_lt).then_inc(s("chosen"), 1)
                    v.wait_ge(s("chosen"), k + 1)
                    chain(v.tensor_tensor(R.sel, R.rank.unsqueeze(1).to_broadcast(each),
                                          choice.unsqueeze(2).unsqueeze(3).to_broadcast(each), ALU.is_equal))
                    chain(v.tensor_tensor(R.prod, R.sel, probs.unsqueeze(1).to_broadcast(each), ALU.mult))
                    chain(v.tensor_reduce(R.gates[:, :, :], R.prod, AX.X, ALU.add))

                def find_rows():
                    v.wait_ge(s("counted"), k + 1)
                    chain(v.tensor_copy(R.total, R.counts[1].rearrange("p (t e) -> p e t", e=R.e)))
                    chain(v.tensor_tensor_scan(R.before.rearrange("p e t -> p (e t)"), resets,
                                               R.total.rearrange("p e t -> p (e t)"), 0.0, ALU.mult, ALU.add))
                    chain(v.tensor_tensor(R.over, R.before[:, :, TT - 1].unsqueeze(2).to_broadcast([P, R.e, R.most]),
                                          full.unsqueeze(1).to_broadcast([P, R.e, R.most]), ALU.is_gt))
                    chain(v.tensor_reduce(R.nslots, R.over, AX.X, ALU.add))
                    chain(v.tensor_tensor_scan(R.end, ones_e, R.nslots, 0.0, ALU.mult, ALU.add))
                    chain(v.tensor_tensor(R.base, R.end, R.nslots, ALU.subtract))
                    chain(v.tensor_scalar(R.base, R.base, float(R.rows), None, ALU.mult))
                    chain(v.tensor_tensor(R.before, R.before, R.total, ALU.subtract))
                    chain(v.tensor_tensor(R.before, R.before, R.base.unsqueeze(2).to_broadcast([P, R.e, TT]), ALU.add))
                    chain(v.tensor_tensor(R.rank, R.counts[0].rearrange("p (t e) -> p t e", e=R.e),
                                          R.before.rearrange("p e t -> p t e"), ALU.add))
                    chain(v.tensor_tensor(R.prod, R.sel, R.rank.unsqueeze(1).to_broadcast(each), ALU.mult))
                    chain(v.tensor_reduce(R.place, R.prod, AX.X, ALU.add))
                    chain(v.tensor_copy(R.places[:, :, :], R.place))

                def find_experts():
                    chain(v.tensor_tensor(R.ended, R.end[0:1].unsqueeze(1).to_broadcast([1, R.slots, R.e]),
                                          slotno[0:1].unsqueeze(2).to_broadcast([1, R.slots, R.e]), ALU.is_le))
                    chain(v.tensor_reduce(R.expert, R.ended, AX.X, ALU.add))
                    chain(v.tensor_scalar(R.expert, R.expert, float(R.e - 1), None, ALU.min))
                    if k == 0:
                        turns = R.expert.rearrange("p (m i) -> p m i", i=RING)
                        chain(v.tensor_tensor(turns, turns, digits0[0:1].unsqueeze(1).to_broadcast([1, TURNS0, RING]),
                                              ALU.mult))
                        chain(v.tensor_reduce(turn_number, turns, AX.X, ALU.add))
                        chain(v.tensor_copy(R.experts[:, :], turn_number))
                    else:
                        chain(v.tensor_copy(R.experts[:, :], R.expert))

                return choose, find_rows, find_experts

            for part in route(0, R0, sig):
                part()
            chain(v.memset(one[:, :], 1.0))
            barrier(v, 3)

            def experts(k, fc, sgv, hidden, gate, between={}):
                def group_pair(gg, between={}):
                    for j in range(2):
                        for f in range(fc):
                            if (j, f) in between:
                                between[j, f]()
                            n = (2 * gg + j) * fc + f
                            r = f % 2 if fc > 1 else j
                            v.wait_ge(s(f"silu{k}"), n + 1)
                            v.wait_ge(s(f"side{k}_made"), n + 1)
                            v.tensor_tensor(hidden(j, f), bank[2 + r][:, 0:GN], sgv[:, r, :], ALU.mult)\
                                .then_inc(s(f"hid{k}_ready"), 1)
                    for j in range(2):
                        group = 2 * gg + j
                        for h in range(GT // 2):
                            v.wait_ge(s(f"y{k}_ready"), 2 * group + h + 1)
                            v.wait_ge(s(f"y{k}_added"), 2 * group + h + 1)
                            for t in range(2):
                                g = group * GT + 2 * h + t
                                ins = v.scalar_tensor_tensor(tile(Hs, g), bank[4 + h][0:P, t * D:(t + 1) * D],
                                                             gate(g), tile(Hs, g), ALU.mult, ALU.add)
                            ins.then_inc(s(f"y{k}_added"), 1)

                group_pair(0, between)
                with v.Fori(1, NG // 2) as gg:
                    group_pair(gg)

            def hid0(j, f):
                return hid[:, j, :]

            experts(0, 1, sg, hid0, lambda g: one[:, 0:1])
            barrier(v, 4)

            def slot0(n2, n1, n0, l1):
                if n1:
                    n, i, turn = n1
                    v.wait_ge(s("slot0_silu"), n + 1)
                    v.tensor_tensor(unit0[:, i % 2, :], bank[2 + i % 2][0:SR0, F0:2 * F0], silu0[:, i % 2, :], ALU.mult)\
                        .then_inc(s("unit0_made"), 1)
                if n0:
                    n, i, turn = n0
                    v.wait_ge(s("unit0_turned"), n + 1)
                    v.tensor_copy(unitT0[:, i % 2, :], bank[4 + i % 2][:, 0:SR0]).then_inc(s("unitT0_ready"), 1)
                if l1:
                    n, i, turn = l1
                    v.wait_ge(s("buffer0_free"), n + 1)
                    v.wait_ge(s("result0_made"), n + 1)
                    v.tensor_copy(place0[:, i:i + 1], rows0[:, i, D:RW].bitcast(mybir.dt.uint32))
                    v.tensor_copy(result0[:, i, :], bank[6 + i % 2][0:SR0, 0:D]).then_inc(s("result0_copied"), 1)

            walk_slots0(v, slot0)
            barrier(v, 5)

            def combine(b):
                h = Hs[:, bass.ds(b * TB, TB), :]
                v.wait_ge(s("summed0"), b + 1)
                v.tensor_tensor(h, h, sum0[:, :, :], ALU.add).then_inc(s("combined"), 1)
                wait_apart(v, s("combined"), b + 1, s("unused"))

            def prepare_weights():
                v.wait_ge(s("load_l1"), 64)
                for q in range(2):
                    hs = v.tensor_reduce(hsum[:, :, q, :],
                                         lraw[:, :, q * D:(q + 1) * D].rearrange("p c (h d) -> p c h d", d=D1),
                                         AX.X, ALU.add)
                chain(hs)
                for q, src in ((3, hsum[:, :, 0, :]), (1, hsum[:, :, 1, :]), (2, lraw[:, :, 2 * D:2 * D + H1])):
                    for c in range(DC):
                        cp = v.tensor_copy(l1w[:, c, q, :].rearrange("p (h d) -> p h d", d=D1),
                                           src[:, c, :].unsqueeze(2).to_broadcast([128, H1, D1]))
                cp.then_inc(s("l1w_ready"), 1)

            def decay_values(b, c, before=None):
                v.wait_ge(s("vs_ready"), DC * b + c + 2)
                v.wait_ge(s("l1_made0"), DC * b + c + 1)
                v.tensor_tensor(uu[:, c, :], bank[0][:, 0:N], vsb[:, c, :], ALU.mult).then_inc(s("u_made"), 1)
                v.wait_ge(s("u_made"), DC * b + c + 3)
                v.wait_ge(s("beta_ready"), DC * b + c + 2)
                v.tensor_tensor_scan(ss[:, c, :], bet[:, c, :], uu[:, c, :], 0.0, ALU.mult, ALU.add)\
                    .then_inc(s("scanned"), 1)
                v.wait_ge(s("scanned"), DC * b + c + 3)
                v.wait_ge(s("l1_made3"), DC * b + c + 1)
                if before is not None:
                    v.wait_ge(s("l1_out"), before + 1)
                v.tensor_tensor(oo[:, c, :], bank[3][:, 0:N], ss[:, c, :], ALU.mult).then_inc(s("scan_out"), 1)

            def attend1(b0, b1, b2, b3, b4, b5):
                if b5 is not None:
                    normalise_batch(3, b5, 1, Hs, kept=1)
                if b1 is not None:
                    normalise_batch(2, b1, 0, Hs, kept=B + 2)
                if b2 is not None:
                    decay_values(b2, 0, b3)
                if b3 is not None:
                    z = XN[:, bass.ds(b3 * TB, TB), 0:D]
                    v.wait_ge(s("l1_out"), b3 + 1)
                    v.wait_ge(s("stage_copied"), B + b3 + 3)
                    v.tensor_tensor(ztmp[:, 0:2, :], bank[6][0:P, :].rearrange("p (t d) -> p t d", t=2),
                                    l1rows[:, 0, :].unsqueeze(1).to_broadcast([P, 2, D]), ALU.add)
                    v.tensor_tensor(ztmp[:, 2, :], bank[7][0:P, 0:D], l1rows[:, 0, :], ALU.add)\
                        .then_inc(s("l1_added"), 1)
                    v.wait_ge(s("l1_added"), b3 + 2)
                    v.tensor_tensor(z, z, ztmp[:, :, :], ALU.add).then_inc(s("z_made"), 1)
                    wait_apart(v, s("z_made"), b3 + 1, s("unused"))
                    for t in range(TB):
                        ins = v.bn_stats(stats4[:, t, :], tile(XN, b3 * TB + t))
                    ins.then_inc(s("stats4_ready"), 1)
                    wait_apart(v, s("stats4_ready"), b3 + 1, s("unused"))
                    for t in range(TB):
                        ins = v.bn_aggr(mean_var4[:, t, :], stats4[:, t, :])
                    ins.then_inc(s("var4_ready"), 1)
                if b2 is not None:
                    decay_values(b2, 1)
                if b4 is not None:
                    h = Hs[:, bass.ds(b4 * TB, TB), :]
                    v.wait_ge(s("offset4"), b4 + 1)
                    v.tensor_tensor(h, h, XN[:, bass.ds(b4 * TB, TB), 0:D], ALU.add).then_inc(s("h_added"), 1)
                    wait_apart(v, s("h_added"), b4 + 1, s("unused"))
                    variances(3, b4, Hs)
                if b0 is not None:
                    combine(b0)
                    variances(2, b0, Hs)
                    if isinstance(b0, int) and b0 == 0:
                        prepare_weights()
                if b3 is not None:
                    v.wait_ge(s("sd4_ready"), b3 + 1)
                    v.reciprocal(inverse4[:, :], deviation4[:, :]).then_inc(s("inverse4_ready"), 1)
                    v.wait_ge(s("inverse4_ready"), b3 + 1)
                    for t in range(TB):
                        g = b3 * TB + t
                        ins = v.tensor_scalar(tile(XN, g), tile(XN, g), mean_var4[:, t, 0:1], inverse4[:, t:t + 1],
                                              ALU.subtract, ALU.mult)
                    ins.then_inc(s("normed4"), 1)

            walk_lagged(v, attend1)
            barrier(v, 6)
            v.memset(half_shared[:, :], 0.5 / E1)
            scores = scores1.rearrange("p (t e) -> p t e", e=E1)
            reduced = small[:, 2, 0:TT]
            below, probs = sm3(0, E1), sm3(1, E1)

            def below_maximum():
                v.wait_ge(s("gate1_made"), 1)
                chain(v.tensor_reduce(reduced, scores, AX.X, ALU.max))
                v.tensor_tensor(below, scores, reduced.unsqueeze(2).to_broadcast([P, TT, E1]), ALU.subtract)\
                    .then_inc(s("gate1_max"), 1)

            def softmax():
                v.wait_ge(s("gate1_exp"), 1)
                chain(v.tensor_reduce(reduced, probs, AX.X, ALU.add))
                chain(v.reciprocal(reduced, reduced))
                chain(v.tensor_tensor(probs, probs, reduced.unsqueeze(2).to_broadcast([P, TT, E1]), ALU.mult))

            def rank_experts():
                top(probs, E1, R1.rank, None, compare1, TT)

            choose, find_rows, find_experts = route(1, R1, probs)

            def find_all():
                find_rows()
                find_experts()
                chain(v.tensor_scalar(gate_k[:, :, :], gate_k[:, :, :], 0.5, None, ALU.mult))
                v.sem_inc(s("routed"), 1)

            def hid1(j, f):
                return fhid[:, j, f, :]

            experts(1, FC1, fsg, hid1, lambda g: half_shared[:, 0:1],
                    {(0, 0): below_maximum, (0, 1): softmax, (0, 3): rank_experts, (0, 5): choose, (1, 1): find_all})
            barrier(v, 7)

            def slot_units(slot, i):
                for f in range(FC1):
                    v.wait_ge(s("slot_silu"), slot * FC1 + f + 1)
                    v.tensor_tensor(shid[:, i, f, :], bank[f % 2][:, SR:2 * SR], ssg[:, f % 2, :], ALU.mult)\
                        .then_inc(s("shid_ready"), 1)

            with v.Fori(0, (SLOTS - 1) // 2) as ss_:
                slot_units(2 * ss_, 0)
                slot_units(2 * ss_ + 1, 1)
            slot_units(SLOTS - 1, 0)
            barrier(v, 8)
            for q in range(4):
                v.wait_ge(s(f"back{q}"), 32)
                for k in range(TOPK1):
                    for t in range(6 * q, 6 * q + 6):
                        ins = v.scalar_tensor_tensor(Hs[:, t, :], back[:, k, t, :], gate_k[:, k, t:t + 1], Hs[:, t, :],
                                                     ALU.mult, ALU.add)
                    chain(ins)
                v.sem_inc(s("summed"), 1)


def kernel(x, L0_tok_W, L0_tok_b, L0_tok_alpha, L0_attn_W_in, L0_attn_b_in, L0_attn_W_out, L0_attn_b_out,
           L0_ffn_gate_w, L0_ffn_gate_bias, L0_ffn_w1, L0_ffn_w2, L0_ffn_w3, L0_ffn_ws1, L0_ffn_ws2, L0_ffn_ws3,
           L1_attn_Wq, L1_attn_Wk, L1_attn_Wv, L1_attn_Wbeta, L1_attn_b_beta, L1_attn_Wo, L1_attn_b_o,
           L1_attn_ln_g, L1_attn_ln_b, L1_ffn_gate_W, L1_ffn_w1_e, L1_ffn_w3_e, L1_ffn_w2_e,
           L1_ffn_w1_s, L1_ffn_w3_s, L1_ffn_w2_s):
    import concourse.bacc as bacc
    from concourse.bass_utils import run_bass_kernel_spmd

    def chunks(w):
        w = np.asarray(w)
        w = w.reshape(*w.shape[:-2], -1, 128, w.shape[-1])
        return np.swapaxes(w, -3, -2)

    def flat(w, keep):
        return w.reshape(*w.shape[:keep], -1)

    l = np.arange(L)
    m = np.where(l % 2 == 0, l // 2, L // 2 + (L - 1 - l) // 2)
    dct = np.cos(2 * np.pi * ((np.arange(DK)[:, None] * m[None, :]) % L) / L).astype(np.float32)
    half = HD // 2
    theta = np.float32(10000.0) ** (np.arange(half, dtype=np.float32) / np.float32(half - 1))
    pos = np.arange(N, dtype=np.float32)[:, None] / theta[None, :]
    sincos = np.stack([np.cos(pos), np.sin(pos)]).astype(np.float32).reshape(2, TB, P, half).transpose(2, 0, 1, 3)
    mask = np.zeros((P, 3 * P), np.float32)
    mask[:, 2 * P:] = np.where(np.arange(P)[None, :] > np.arange(P)[:, None], MASKED, 0.0)

    earlier = (np.arange(P)[:, None] < np.arange(P)[None, :]).astype(np.float32)
    route_rows0, route_rows1 = (
        np.concatenate([np.tile(np.arange(TT) > 0, e), np.arange(most) * rows, np.arange(slots), np.ones(e),
                        np.arange(choices)]).astype(np.float32)
        for e, most, rows, slots, choices in ((E0, MOST0, SR0, TURNS0 * RING, TOPK0), (E1, MOST1, SR, SLOTS, TOPK1)))
    digits = (2.0 ** (EXPERT_BITS * np.arange(RING))).astype(np.float32)
    dest = np.arange(TOPK0 * B * N, dtype=np.int32).reshape(TOPK0, TT, P).transpose(2, 0, 1)
    empty = np.concatenate([np.zeros(D, np.int32), np.array([NOWHERE], np.int32)]).view(np.float32)

    heads = np.asarray(L0_attn_W_in).reshape(3, HP, 2 * HD, D).transpose(1, 0, 2, 3).reshape(HP * UW, D)
    head_bias = np.asarray(L0_attn_b_in).reshape(3, HP, 2 * HD).transpose(1, 0, 2).reshape(HP * UW)
    t = lambda w: np.swapaxes(np.asarray(w), -1, -2)
    ffn0 = np.concatenate([
        np.concatenate([flat(chunks(t(L0_ffn_w1)), 2), flat(chunks(t(L0_ffn_w3)), 2), t(L0_ffn_w2)], axis=2),
        np.concatenate([flat(chunks(t(L0_ffn_ws1)), 1), flat(chunks(t(L0_ffn_ws3)), 1), t(L0_ffn_ws2)], axis=1)[None]])
    side = lambda w: np.asarray(w).transpose(1, 0, 2).reshape(D, F1)
    ffn1 = np.concatenate([
        np.concatenate([flat(chunks(L1_ffn_w1_e), 2), flat(chunks(L1_ffn_w3_e), 2), flat(chunks(L1_ffn_w2_e), 2)], axis=2),
        np.concatenate([flat(chunks(side(L1_ffn_w1_s)), 1), flat(chunks(side(L1_ffn_w3_s)), 1),
                        flat(chunks(np.asarray(L1_ffn_w2_s).reshape(F1, D)), 1)], axis=1)[None]])
    arrays = {
        "x": np.asarray(x), "dct": dct, "tok_w": L0_tok_W, "tok_b": L0_tok_b, "tok_alpha": L0_tok_alpha,
        "w_in": chunks(t(heads)), "b_in": head_bias, "w_out": chunks(t(L0_attn_W_out)), "b_out": L0_attn_b_out,
        "sincos": sincos, "mask": mask, "ident_in": np.eye(128, dtype=np.float32),
        "gate0_w": chunks(t(L0_ffn_gate_w)), "gate0_b": L0_ffn_gate_bias, "ffn0_w": ffn0,
        "l1_w": chunks(np.concatenate([np.asarray(L1_attn_Wq), np.asarray(L1_attn_Wv), np.asarray(L1_attn_Wbeta)], axis=1)),
        "l1_wk": chunks(L1_attn_Wk),
        "l1_b_beta": np.broadcast_to(np.asarray(L1_attn_b_beta)[:, None], (H1, D1)).reshape(DC, 128).T,
        "l1_wo": chunks(L1_attn_Wo),
        "l1_rows": np.stack([np.asarray(L1_attn_b_o), np.asarray(L1_attn_ln_g), np.asarray(L1_attn_ln_b)]),
        "gate1_w": chunks(t(L1_ffn_gate_W)), "ffn1_w": ffn1, "earlier": earlier,
        "route_rows0": route_rows0, "digits": digits, "route_rows": route_rows1,
        "dest_in": dest, "empty_row": empty,
    }
    nc = bacc.Bacc("TRN2", target_bir_lowering=False, num_devices=1)
    arrays = {k + "_dram": np.ascontiguousarray(v) for k, v in arrays.items()}
    args = [nc.dram_tensor(k, v.shape, mybir.dt.from_np(v.dtype), kind="ExternalInput").ap() for k, v in arrays.items()]
    out = nc.dram_tensor("result_dram", [B * N, D], F32, kind="ExternalOutput").ap()
    build(nc, *args, out)
    r = run_bass_kernel_spmd(nc, [arrays], core_ids=[0])
    return r.results[0]["result_dram"].reshape(B, N, D)
```
